# Optimizing a Trainium2 kernel written in Bass

```python
import numpy as np
import jax
import jax.numpy as jnp

def _softmax(x, axis=-1):
    return jax.nn.softmax(x, axis=axis)

def _gelu(x):
    return jax.nn.gelu(x, approximate=True)

def _silu(x):
    return jax.nn.silu(x)

def _sigmoid(x):
    return jax.nn.sigmoid(x)

def _layernorm(x, axis=-1, eps=1e-05):
    m = jnp.mean(x, axis=axis, keepdims=True)
    v = jnp.var(x, axis=axis, keepdims=True)
    return (x - m) / jnp.sqrt(v + eps)

def _scatter_add(tgt, idx, src, axis=0):
    return tgt.at[idx].add(src)

def _segment_sum(src, seg, n):
    return jax.ops.segment_sum(src, seg, n)
kernel_name = 'mk_decoder_preln_d1_seqx_r4_4f6002'

def setup_inputs(seed: int=0):
    np.random.seed(seed)
    _w = jnp.asarray

    def _rec_inputs():
        import jax
        import jax.numpy as jnp
        _rk = jax.random.key(seed)
        x = 7.22e-05 + 1 * jax.random.normal(jax.random.fold_in(_rk, 1), (4, 512, 256), jnp.float32)
        _lenS = 512 - jax.random.randint(jax.random.fold_in(_rk, 7), (4,), 0, max(1, 512 // 4) + 1, jnp.int32)
        _lenS2 = 64 - jax.random.randint(jax.random.fold_in(_rk, 8), (4,), 0, max(1, 64 // 4) + 1, jnp.int32)
        _ctx_1024P = jax.random.normal(jax.random.fold_in(_rk, 11), (4, 16, 256), jnp.float32)
        _ctx_1024c = jax.random.dirichlet(jax.random.fold_in(_rk, 511), 0.3 * jnp.ones((16,), jnp.float32), (4, 64))
        _ctx_1024t = jnp.einsum('bsk,bkd->bsd', _ctx_1024c, _ctx_1024P)
        _ctx_1024t = _ctx_1024t * jax.lax.rsqrt(jnp.mean(jnp.square(_ctx_1024t)) + 1e-12) * 0.953939
        ctx_1024 = 4.13588e-05 + 0.999923 * (_ctx_1024t + 0.3 * jax.random.normal(jax.random.fold_in(_rk, 611), (4, 64, 256), jnp.float32))
        return (x, ctx_1024)
    x, ctx_1024 = _rec_inputs()

    def _L0_attn_setup():
        import jax, jax.numpy as jnp
        import numpy as np
        NUM_HEADS = 16
        WINDOW = 32
        HIDDEN = 256
        HEAD_DIM = HIDDEN // NUM_HEADS
        key = jax.random.key(seed)
        ks = jax.random.split(key, 9)
        B, S, H = (2, 512, HIDDEN)
        s = 0.02
        return {'hidden_states': jax.random.normal(ks[0], (B, S, H), jnp.float32), 'Wq': jax.random.normal(ks[1], (H, H), jnp.float32) * s, 'bq': jnp.zeros((H,), jnp.float32), 'Wk': jax.random.normal(ks[2], (H, H), jnp.float32) * s, 'bk': jnp.zeros((H,), jnp.float32), 'Wv': jax.random.normal(ks[3], (H, H), jnp.float32) * s, 'bv': jnp.zeros((H,), jnp.float32), 'Wo': jax.random.normal(ks[4], (H, H), jnp.float32) * s, 'bo': jnp.zeros((H,), jnp.float32)}
    _L0_attn_all = _L0_attn_setup()
    _L0_attn_in = {k: v for k, v in _L0_attn_all.items() if k in ('Wq', 'bq', 'Wk', 'bk', 'Wv', 'bv', 'Wo', 'bo')}
    del _L0_attn_all

    def _L0_xattn_setup():
        import jax, jax.numpy as jnp
        import numpy as np
        HEADS = 16
        EMBED = 256
        HEAD_DIM = EMBED // HEADS
        key = jax.random.key(seed)
        ks = jax.random.split(key, 11)
        B, S, E = (4, 512, EMBED)
        s = 1.0 / np.sqrt(E)
        return {'query': jax.random.normal(ks[0], (B, S, E), jnp.float32), 'key': jax.random.normal(ks[1], (B, S, E), jnp.float32), 'value': jax.random.normal(ks[2], (B, S, E), jnp.float32), 'Wq': jax.random.normal(ks[3], (E, E), jnp.float32) * s, 'bq': jax.random.normal(ks[4], (E,), jnp.float32) * s, 'Wk': jax.random.normal(ks[5], (E, E), jnp.float32) * s, 'bk': jax.random.normal(ks[6], (E,), jnp.float32) * s, 'Wv': jax.random.normal(ks[7], (E, E), jnp.float32) * s, 'bv': jax.random.normal(ks[8], (E,), jnp.float32) * s, 'Wo': jax.random.normal(ks[9], (E, E), jnp.float32) * s, 'bo': jax.random.normal(ks[10], (E,), jnp.float32) * s}
    _L0_xattn_all = _L0_xattn_setup()
    _L0_xattn_in = {k: v for k, v in _L0_xattn_all.items() if k in ('Wq', 'bq', 'Wk', 'bk', 'Wv', 'bv', 'Wo', 'bo')}
    del _L0_xattn_all

    def _L0_ffn_setup():
        import jax, jax.numpy as jnp
        import numpy as np
        H = 256
        I = 512
        E = 32
        B, S = (4, 512)

        def _grouped_mm(a, w, group_sizes):
            return jax.lax.ragged_dot(a, w, group_sizes)

        def _swiglu(x, gw, uw, dw):
            return jax.nn.silu(x @ gw) * (x @ uw) @ dw
        key = jax.random.key(seed)
        ks = jax.random.split(key, 8)
        scale = 0.02
        inp = {'hidden_states': jax.random.normal(ks[0], (B, S, H), dtype=jnp.float32), 'gate_w': jax.random.normal(ks[1], (H, E), dtype=jnp.float32) * scale, 'shared_gate_w': jax.random.normal(ks[2], (H, I), dtype=jnp.float32) * scale, 'shared_up_w': jax.random.normal(ks[3], (H, I), dtype=jnp.float32) * scale, 'shared_down_w': jax.random.normal(ks[4], (I, H), dtype=jnp.float32) * scale, 'routed_gate_w': jax.random.normal(ks[5], (E, H, I), dtype=jnp.float32) * scale, 'routed_up_w': jax.random.normal(ks[6], (E, H, I), dtype=jnp.float32) * scale, 'routed_down_w': jax.random.normal(ks[7], (E, I, H), dtype=jnp.float32) * scale}
        return inp
    _L0_ffn_all = _L0_ffn_setup()
    _L0_ffn_in = {k: v for k, v in _L0_ffn_all.items() if k in ('gate_w', 'shared_gate_w', 'shared_up_w', 'shared_down_w', 'routed_gate_w', 'routed_up_w', 'routed_down_w')}
    del _L0_ffn_all
    return {'x': x, 'ctx_1024': ctx_1024, 'L0_attn_Wq': _L0_attn_in['Wq'], 'L0_attn_bq': _L0_attn_in['bq'], 'L0_attn_Wk': _L0_attn_in['Wk'], 'L0_attn_bk': _L0_attn_in['bk'], 'L0_attn_Wv': _L0_attn_in['Wv'], 'L0_attn_bv': _L0_attn_in['bv'], 'L0_attn_Wo': _L0_attn_in['Wo'], 'L0_attn_bo': _L0_attn_in['bo'], 'L0_xattn_Wq': _L0_xattn_in['Wq'], 'L0_xattn_bq': _L0_xattn_in['bq'], 'L0_xattn_Wk': _L0_xattn_in['Wk'], 'L0_xattn_bk': _L0_xattn_in['bk'], 'L0_xattn_Wv': _L0_xattn_in['Wv'], 'L0_xattn_bv': _L0_xattn_in['bv'], 'L0_xattn_Wo': _L0_xattn_in['Wo'], 'L0_xattn_bo': _L0_xattn_in['bo'], 'L0_ffn_gate_w': _L0_ffn_in['gate_w'], 'L0_ffn_shared_gate_w': _L0_ffn_in['shared_gate_w'], 'L0_ffn_shared_up_w': _L0_ffn_in['shared_up_w'], 'L0_ffn_shared_down_w': _L0_ffn_in['shared_down_w'], 'L0_ffn_routed_gate_w': _L0_ffn_in['routed_gate_w'], 'L0_ffn_routed_up_w': _L0_ffn_in['routed_up_w'], 'L0_ffn_routed_down_w': _L0_ffn_in['routed_down_w']}

def reference(x, ctx_1024, L0_attn_Wq, L0_attn_bq, L0_attn_Wk, L0_attn_bk, L0_attn_Wv, L0_attn_bv, L0_attn_Wo, L0_attn_bo, L0_xattn_Wq, L0_xattn_bq, L0_xattn_Wk, L0_xattn_bk, L0_xattn_Wv, L0_xattn_bv, L0_xattn_Wo, L0_xattn_bo, L0_ffn_gate_w, L0_ffn_shared_gate_w, L0_ffn_shared_up_w, L0_ffn_shared_down_w, L0_ffn_routed_gate_w, L0_ffn_routed_up_w, L0_ffn_routed_down_w):
    import jax
    import jax.numpy as jnp

    def _L0_attn_ref(hidden_states, Wq, bq, Wk, bk, Wv, bv, Wo, bo):
        import jax, jax.numpy as jnp
        import numpy as np
        NUM_HEADS = 16
        WINDOW = 32
        HIDDEN = 256
        HEAD_DIM = HIDDEN // NUM_HEADS
        B, S, H = hidden_states.shape
        scale = jnp.sqrt(jnp.asarray(HEAD_DIM, hidden_states.dtype))
        q = (hidden_states @ Wq.T + bq).reshape(B, S, NUM_HEADS, HEAD_DIM)
        k = (hidden_states @ Wk.T + bk).reshape(B, S, NUM_HEADS, HEAD_DIM)
        v = (hidden_states @ Wv.T + bv).reshape(B, S, NUM_HEADS, HEAD_DIM)
        scores = jnp.einsum('bihd,bjhd->bhij', q, k) / scale
        blk = jnp.arange(S) // WINDOW
        allowed = blk[:, None] >= blk[None, :]
        scores = jnp.where(allowed, scores, jnp.zeros((), scores.dtype))
        probs = jax.nn.softmax(scores, axis=-1)
        ctx = jnp.einsum('bhij,bjhd->bihd', probs, v).reshape(B, S, H)
        return ctx @ Wo.T + bo

    def _L0_xattn_ref(query, key, value, Wq, bq, Wk, bk, Wv, bv, Wo, bo):
        import jax, jax.numpy as jnp
        import numpy as np
        HEADS = 16
        EMBED = 256
        HEAD_DIM = EMBED // HEADS
        B, Sq, E = query.shape
        Sk = key.shape[1]
        H, D = (HEADS, HEAD_DIM)
        q = (query @ Wq.T + bq).reshape(B, Sq, H, D)
        k = (key @ Wk.T + bk).reshape(B, Sk, H, D)
        v = (value @ Wv.T + bv).reshape(B, Sk, H, D)
        scores = jnp.einsum('bqhd,bkhd->bhqk', q, k) / np.sqrt(D).astype(jnp.float32)
        attn = jax.nn.softmax(scores, axis=-1)
        out = jnp.einsum('bhqk,bkhd->bqhd', attn, v).reshape(B, Sq, E)
        return out @ Wo.T + bo

    def _L0_ffn_ref(hidden_states, gate_w, shared_gate_w, shared_up_w, shared_down_w, routed_gate_w, routed_up_w, routed_down_w):
        import jax, jax.numpy as jnp
        import numpy as np
        H = 256
        I = 512
        E = 32
        B, S = (4, 512)

        def _grouped_mm(a, w, group_sizes):
            return jax.lax.ragged_dot(a, w, group_sizes)

        def _swiglu(x, gw, uw, dw):
            return jax.nn.silu(x @ gw) * (x @ uw) @ dw
        b, s, h = hidden_states.shape
        x = hidden_states.reshape(-1, h)
        shared_out = _swiglu(x, shared_gate_w, shared_up_w, shared_down_w)
        logits = x @ gate_w
        topk_ids = jnp.argmax(logits, axis=-1)
        topk_val = jnp.max(logits, axis=-1)
        scores = jax.nn.sigmoid(topk_val)[:, None]
        xs = x * scores
        tokens_per_expert = jnp.zeros((E,), jnp.int32).at[topk_ids].add(1)
        order = jnp.argsort(topk_ids)
        sorted_x = xs[order]
        g = _grouped_mm(sorted_x, routed_gate_w, tokens_per_expert)
        u = _grouped_mm(sorted_x, routed_up_w, tokens_per_expert)
        d = _grouped_mm(jax.nn.silu(g) * u, routed_down_w, tokens_per_expert)
        inv = jnp.argsort(order)
        routed_out = d[inv]
        return (shared_out + routed_out).reshape(b, s, h)
    x = x + _L0_attn_ref(_layernorm(x, axis=-1), L0_attn_Wq, L0_attn_bq, L0_attn_Wk, L0_attn_bk, L0_attn_Wv, L0_attn_bv, L0_attn_Wo, L0_attn_bo)
    x = x + _L0_xattn_ref(_layernorm(x, axis=-1), ctx_1024, ctx_1024, L0_xattn_Wq, L0_xattn_bq, L0_xattn_Wk, L0_xattn_bk, L0_xattn_Wv, L0_xattn_bv, L0_xattn_Wo, L0_xattn_bo)
    x = x + _L0_ffn_ref(_layernorm(x, axis=-1), L0_ffn_gate_w, L0_ffn_shared_gate_w, L0_ffn_shared_up_w, L0_ffn_shared_down_w, L0_ffn_routed_gate_w, L0_ffn_routed_up_w, L0_ffn_routed_down_w)
    return x

_drawn_inputs = setup_inputs


def setup_inputs(seed=0):
    import zlib

    import numpy as np

    out = dict(_drawn_inputs(seed))
    spreads = {'L0_attn_bq': (0.0, 0.8),
     'L0_attn_bk': (0.0, 0.8),
     'L0_attn_bv': (0.0, 0.291),
     'L0_attn_bo': (0.0, 0.1)}
    factors = {'L0_attn_Wq': 8.0,
     'L0_attn_Wk': 8.0,
     'L0_attn_Wv': 8.0,
     'L0_xattn_bq': 4.054,
     'L0_xattn_bk': 8.0,
     'L0_ffn_gate_w': 6.394,
     'L0_ffn_shared_gate_w': 2.78,
     'L0_ffn_shared_up_w': 2.75,
     'L0_ffn_shared_down_w': 2.728,
     'L0_ffn_routed_gate_w': 6.528,
     'L0_ffn_routed_up_w': 6.495,
     'L0_ffn_routed_down_w': 6.504}
    for name, (base, spread) in spreads.items():
        noise = np.random.default_rng([zlib.crc32(name.encode()), seed]).standard_normal(out[name].shape)
        drawn = base * np.exp(spread * noise) if base else spread * noise
        out[name] = jnp.asarray(drawn.astype(out[name].dtype))
    for name, factor in factors.items():
        out[name] = (out[name] * factor).astype(out[name].dtype)
    return out
```

```python
from contextlib import ExitStack

import numpy as np
import concourse.bass as bass
from concourse import mybir

ALU = mybir.AluOpType
ACT = mybir.ActivationFunctionType
AX = mybir.AxisListType
F32 = mybir.dt.float32
F32R = mybir.dt.float32r
BF16 = mybir.dt.bfloat16
I32 = mybir.dt.int32
U32 = mybir.dt.uint32

P = 128
B, S, H = 4, 512, 256
HEADS, D = 16, 16
SC = 64
EXPERTS, INNER = 32, 512
QT = S // P
TILES = B * QT
HC = H // P
IC = INNER // P
GROUPS = HEADS // 4
PAIRS = HEADS // 2
OVER = TILES - 1
SLOTS = EXPERTS + OVER
RING = 4
EPS = 1e-5
SCALE = D ** -0.5
BIG = 1e30
STEPS_PER_BATCH = 61
VCONSTS = 13
CONSTS = 17
NOBODY = 4096
RSQRT_MAGIC = 0x5F3759DF
WIDTH = D + 1
VROW = HEADS * WIDTH

WCOLS = {"qkv": (HC, 3 * H), "o": (HC, H), "xq": (HC, H), "xkv": (HC, 2 * H), "xo": (HC, H),
         "gu": (HC, 2 * INNER), "dn": (IC, H), "gate": (HC, P)}
BCOLS = {"qkv": 3 * H, "o": H, "xq": H, "xkv": 2 * H, "xo": H}


class Bank:

    def __init__(self, tile, ready, done):
        self.tile, self.ready, self.done, self.order = tile, ready, done, {}

    def free(self, key, b):
        return b * len(self.order) + (self.order[key] + 1)

    def filled(self, key, b):
        return b * len(self.order) + (self.order[key] + 1)

    def emptied(self, key, b):
        return b * len(self.order) + (self.order[key] + 2)

    def cleared(self, b):
        return b * len(self.order) + 1


def misc_jobs():
    order = [("ctxT",), ("ctxkv",), ("ctxkA",), ("ctxkc",)]
    order += [("xT", 1, 0), ("xT", 1, 1)]
    for t in range(QT):
        order += [("qk", t), ("v", t)]
        if t + 2 < QT:
            order += [("xT", 1, t + 2)]
        order += [("kA", t, 0), ("kA", t, 1), ("c", t)]
    for g in range(GROUPS):
        order += [("qA", g, 0), ("qA", g, 1)]
    for t in range(QT):
        order += [("suf", t), ("oT", 1, t)]
    for t in range(QT):
        order += [("o2", 1, t), ("pr", 1, t)]
    order += [("xT", 2, 0), ("xT", 2, 1)]
    for t in range(QT):
        order += [("q2", t)]
        if t + 2 < QT:
            order += [("xT", 2, t + 2)]
        order += [("c2", t), ("qA2", t, 0), ("qA2", t, 1)]
    for t in range(QT):
        order += [("oT", 2, t)]
    for t in range(QT):
        order += [("o2", 2, t), ("pr", 2, t)]
    for t in range(QT):
        order += [("xT", 3, t)]
    order += [("lg",), ("lgT",)]
    for t in range(QT):
        order += [("dn", t)]
    return order


def max_jobs(g):
    n = []
    for t in range(QT):
        per = max(1, 4 // (t + 1)) if t < 2 else 1
        n += [(t, h, per) for h in range(0, 4, per)]
    return [("mx", g, t, h, per) for t, h, per in n]


EXPJOBS = [[(0, 0)], [(1, 0), (3, 3 * P)], [(2, 0)]]
EXPCOLS = [4 * P, 4 * P, 2 * P]
PBASE = [0, 4 * P, 8 * P]
KTCOL = {0: 0, 1: 4 * P, 3: 7 * P, 2: 8 * P}
PCOLS = 10 * P
KTORDER = [0, 1, 3, 2]


def build_decoder(nc, x, ctx_in, weights, biases, experts_w, rows, table, out):
    with ExitStack() as stack:
        memory = {"next": -(-nc.sbuf_base // 32) * 32}
        offset = {}

        def sb(name, shape, dt=F32, over=None, skip=0):
            size = int(np.prod(shape[1:])) * (2 if dt == BF16 else 4)
            if over is None:
                offset[name] = memory["next"]
                memory["next"] += -(-size // 32) * 32
            else:
                offset[name] = offset[over] + skip
            return nc.alloc_sbuf_tensor_at(name, shape, dt, offset=offset[name])

        def sem(name):
            return stack.enter_context(nc.semaphore(name))

        wcols = sum(c * n for c, n in WCOLS.values())
        w_hl = sb("w_hl", [P, 2, wcols], F32R)
        bias = sb("bias", [P, sum(BCOLS.values())])
        x1 = sb("x1", [P, QT, H])
        x2 = sb("x2", [P, QT, H])
        xn = sb("xn", [P, 2, H])
        xt = sb("xt", [P, 2, HC, S], F32R)
        qk = sb("qk", [P, 2 * H])
        qa = sb("qa", [P, QT, HEADS, 64], F32R)
        ka = sb("ka", [P, HEADS, 64], F32R)
        qat = sb("qat", [P, PAIRS, S], F32R)
        kat = sb("kat", [P, PAIRS, S], F32R)
        maxr = sb("maxr", [P, 8, S], F32R)
        probs = sb("probs", [P, 4 * PCOLS])
        vb = sb("vb", [P, QT, VROW + 16])
        ctxr = sb("ctxr", [SC, H])
        ctxt = sb("ctxt", [P, 2, HC, 2, SC], F32R)
        kxt = sb("kxt", [P, PAIRS, P], F32R)
        kxc = sb("kxc", [P, 2, 8, SC], F32R)
        vx = sb("vx", [P, PAIRS, 2, 32])
        stats = sb("stats", [P, QT, 6])
        mv = sb("mv", [P, QT, 2])
        nrm = sb("nrm", [P, 6, QT])
        nmax = sb("nmax", [P, QT, HEADS])
        emi = sb("emi", [P, QT, HEADS])
        em = sb("em", [P, QT, HEADS])
        t17 = sb("t17", [P, VROW])
        num = sb("num", [P, VROW])
        rec = sb("rec", [P, HEADS])
        ohl = sb("ohl", [P, 2, HC, P], F32R)
        score = sb("score", [P, 4, QT])
        lga = sb("lga", [P, TILES, EXPERTS])
        ident = sb("ident", [P, P])
        ident_b = sb("ident_b", [P, P], BF16)
        later_b = sb("later_b", [P, P], BF16)
        later = sb("later", [P, P])
        ones = sb("ones", [P, P])
        ones_b = sb("ones_b", [P, P], BF16)
        below_b = sb("below_b", [P, P], BF16)
        head_mask = sb("head_mask", [P, 8])
        zero_floor = sb("zero_floor", [P, QT, 4])
        upto = sb("upto", [P, EXPERTS, EXPERTS], BF16)
        onehot = sb("onehot", [P, TILES, EXPERTS], BF16)
        desc = sb("desc", [P, EXPERTS])
        steps128 = sb("steps128", [P, OVER])
        ovn = sb("ovn", [P, OVER])
        tokens = sb("tokens", [P, TILES], I32)
        nobody = sb("nobody", [P, SLOTS], I32)

        ckv, cka = qk, ka[0:SC, :, :]
        qct = maxr[:, 0:2, :]
        kct = maxr[:, 2:4, :]
        km = maxr[:, 4:8, :]
        th = sb("th", [P, 2, S], over="maxr")
        gated = sb("gated", [P, S], over="maxr", skip=4 * 2 * S)
        hid = sb("hid", [P, 2, S], over="maxr", skip=4 * 4 * S)
        lgs = sb("lgs", [P, S], over="maxr", skip=4 * 6 * S)
        ots = sb("ots", [P, GROUPS, S], over="xt")
        hhl = sb("hhl", [P, 2, IC, S], F32R, over="probs")
        row = sb("row", [P, QT, 2 * H], over="kat")
        raw = sb("raw", [P, PAIRS * S], over="qat")
        raw2 = sb("raw2", [P, PAIRS * S], over="kat")
        w, at = {}, 0
        wraw = {}
        for name, (c, n) in WCOLS.items():
            w[name] = w_hl[:, :, at:at + c * n].rearrange("p a (c n) -> p a c n", c=c)
            w[name + "_flat"] = (at, c * n)
            at += c * n
        bs, bat = {}, 0
        for name, n in BCOLS.items():
            bs[name] = bias[:, bat:bat + n]
            bat += n
        room = {0: 0, 1: 0}
        for name in ("qkv", "gu", "o", "xq", "xkv", "xo", "dn", "gate"):
            c, n = WCOLS[name]
            k = 0 if room[0] + c * n <= PAIRS * S else 1
            wraw[name] = (raw, raw2)[k][:, room[k]:room[k] + c * n]
            room[k] += c * n
        assert max(room.values()) <= PAIRS * S

        o_all = sb("o_all", [P, QT, H], over="probs")
        ring = sb("ring", [P, RING, 3 * HC * INNER], over="w_hl")
        tabs = sb("tabs", [P, SLOTS], I32)
        slot_i = sb("slot_i", [P, TILES], I32)
        ctl_i = sb("ctl_i", [1, 16], I32)
        big = sb("big", [P, QT * HEADS * 64], over="qa")
        idx = sb("idx", [P, 1], I32)
        gath = sb("gath", [P, RING, 2 * H], over="qat")
        outr = sb("outr", [P, RING, H], over="qat", skip=4 * RING * 2 * H)
        xe = sb("xe", [P, 2, H], over="kat")
        the = sb("the", [P, INNER], over="kat", skip=4 * 512)
        ge = sb("ge", [P, INNER], over="kat", skip=4 * 1024)
        he = sb("he", [P, 2, INNER], over="kat", skip=4 * 1536)

        place = {}
        at = 0
        for name, shape in {"a": (TILES, EXPERTS), "b": (TILES, EXPERTS), "c15": (TILES, OVER), "e15": (EXPERTS, OVER),
                            "cum": (EXPERTS, EXPERTS), "mx": (TILES,), "cm": (TILES,), "rank": (TILES,),
                            "chunk": (TILES,), "nov": (EXPERTS,), "end": (EXPERTS,), "beg": (EXPERTS,),
                            "ob": (TILES,), "e": (TILES,), "t1": (TILES,), "t2": (TILES,), "t3": (TILES,),
                            "o15": (OVER, EXPERTS), "oe": (OVER,)}.items():
            n = shape[0] * (shape[1] if len(shape) > 1 else 1)
            v = big[:, at:at + n]
            place[name] = v if len(shape) == 1 else v.rearrange("p (a b) -> p a b", a=shape[0])
            at += n
        assert at <= QT * HEADS * 64

        def bank(name):
            tile = stack.enter_context(nc.psum_tensor(name, [P, 512], F32))
            return Bank(tile, sem(name + "_ready"), sem(name + "_done"))

        misc = [bank(f"misc{i}") for i in range(2)]
        smax = [bank(f"smax{i}") for i in range(2)]
        sexp = [bank(f"sexp{i}") for i in range(3)]
        pv = bank("pv")

        BANK = {}

        def put(banks, keys):
            for i, key in enumerate(keys):
                k = banks[i % len(banks)]
                BANK[key] = k
                k.order[key] = len(k.order)

        put(misc, misc_jobs())
        put(smax, [j for g in range(GROUPS) for j in max_jobs(g)]
            + [("mx2", t, k) for t in range(QT) for k in range(2)] + [("gate", c) for c in range(IC)])
        put(sexp, [("sc", g, j, h) for g in range(GROUPS) for j in range(3) for h in range(4)]
            + [("sc2", p) for p in range(PAIRS)] + [("up", c) for c in range(IC)])
        put([pv], [("pv", g) for g in range(GROUPS)] + [("pv2", g) for g in range(GROUPS)])

        in_bias = sem("in_bias")
        in_w = sem("in_w")
        in_x = sem("in_x")
        in_ctx = sem("in_ctx")
        consts_made = sem("consts_made")
        vconsts_made = sem("vconsts_made")
        w_high = sem("w_high")
        w_low = sem("w_low")
        normed = sem("normed")
        xt_high = sem("xt_high")
        dve_step = sem("dve_step")
        ctx_high = sem("ctx_high")
        ctxv_put = sem("ctxv_put")
        cka_high = sem("cka_high")
        cka_low = sem("cka_low")
        k_high = sem("k_high")
        k_low = sem("k_low")
        q_high = sem("q_high")
        q_low = sem("q_low")
        km_made = sem("km_made")
        shift_put = sem("shift_put")
        emi_made = sem("emi_made")
        em_made = sem("em_made")
        masked = sem("masked")
        pv_read = sem("pv_read")
        xb_made = sem("xb_made")
        o_made = sem("o_made")
        o_high = sem("o_high")
        tanh_made = sem("tanh_made")
        hid_high = sem("hid_high")
        hid_low = sem("hid_low")
        btanh_made = sem("btanh_made")
        row_made = sem("row_made")
        row_out = sem("row_out")
        table_set = sem("table_set")
        oh_made = sem("oh_made")
        ranked = sem("ranked")
        slots_made = sem("slots_made")
        table_put = sem("table_put")
        table_in = sem("table_in")
        idx_made = sem("idx_made")
        in_e = [sem(f"in_e{u}") for u in range(RING)]
        gathered = [sem(f"gathered{u}") for u in range(RING)]
        e_t = sem("e_t")
        e_x = sem("e_x")
        e_g = sem("e_g")
        e_u = sem("e_u")
        e_th = sem("e_th")
        e_gd = sem("e_gd")
        e_h = sem("e_h")
        e_y = sem("e_y")
        e_o = sem("e_o")
        scattered = [sem(f"scattered{u}") for u in range(RING)]

        passed = sem("passed")
        block = stack.enter_context(nc.Block())

        @block.sync
        def _(sp):
            for k in (*misc, *smax, *sexp, pv):
                sp.sem_inc(k.done, 1)
            sp.sem_inc(row_out, 16)
            for k in (e_gd, e_h):
                sp.sem_inc(k, 1)
            for name, n in BCOLS.items():
                sp.dma_start(bs[name], biases[name].partition_broadcast(P)).then_inc(in_bias, 16)
            for name, (c, n) in WCOLS.items():
                sp.dma_start(wraw[name].rearrange("p (c n) -> p c n", c=c),
                             weights[name].rearrange("(c p) n -> p c n", p=P)).then_inc(in_w, 16)
            sp.wait_ge(vconsts_made, VCONSTS)
            sp.dma_start(table, nobody[:, :]).then_inc(table_set, 16)
            with sp.Fori(0, B) as b:
                for key in (("lg",), ("lgT",)):
                    sp.wait_ge(BANK[key].done, BANK[key].cleared(b))
                    sp.sem_inc(passed, 1)
                sp.sem_inc(passed, 1)
                sp.dma_start(x1[:, :, :], x.rearrange("(b t p) h -> b p t h", b=B, p=P)[b])\
                    .then_inc(in_x, 16)
                k = BANK["ctxT",]
                sp.wait_ge(k.done, k.cleared(b))
                sp.sem_inc(passed, 1)
                sp.dma_start(ctxr[:, :], ctx_in.rearrange("(b s) h -> b s h", b=B)[b]).then_inc(in_ctx, 16)
                for t in range(QT):
                    key = ("dn", t)
                    sp.wait_ge(row_made, b * QT + t + 1)
                    sp.sem_inc(passed, 1)
                    sp.wait_ge(BANK[key].done, BANK[key].emptied(key, b))
                    sp.sem_inc(passed, 1)
                    sp.dma_start(rows.rearrange("(b t p) h -> b t p h", b=B, p=P)[b, t], row[:, t, :])\
                        .then_inc(row_out, 16)
            sp.wait_ge(table_put, 16 * TILES)
            sp.dma_start(tabs[:, :], table).then_inc(table_in, 16)
            k = BANK["dn", QT - 1]
            sp.wait_ge(k.ready, k.filled(("dn", QT - 1), B - 1))
            k = BANK["dn", QT - 2]
            sp.wait_ge(k.ready, k.filled(("dn", QT - 2), B - 1))
            for u in range(RING):
                sp.dma_start(ring[:, u, :], experts_w[u]).then_inc(in_e[u], 16)
            with sp.Fori(1, EXPERTS // RING) as i:
                for u in range(RING):
                    sp.wait_ge(e_y, i * RING + (u + 1 - RING))
                    sp.sem_inc(passed, 1)
                    sp.dma_start(ring[:, u, :], experts_w[i * RING + u]).then_inc(in_e[u], 16)
            sp.wait_ge(e_y, EXPERTS)
            n_over = sp.value_load(ctl_i[0:1, 0:1], min_val=0, max_val=OVER)
            with sp.Fori(0, OVER) as o:
                with sp.If(o < n_over):
                    e = sp.value_load(ctl_i[0:1, bass.ds(o + 1, 1)], min_val=0, max_val=EXPERTS - 1)
                    sp.wait_ge(e_y, o + EXPERTS)
                    sp.dma_start(ring[:, 0, :], experts_w[e]).then_inc(in_e[0], 16)

        @block.gpsimd
        def _(pool):
            pool.memset(ones[:, :], 1.0).then_inc(consts_made, 1)
            pool.memset(ident[:, :], 0.0).then_inc(consts_made, 1)
            pool.memset(zero_floor[:, :, :], 0.0).then_inc(consts_made, 1)
            pool.memset(later_b[:, :], 0.0).then_inc(consts_made, 1)
            pool.memset(upto[:, :, :], 1.0).then_inc(consts_made, 1)
            pool.wait_ge(consts_made, 5)
            pool.affine_select(out=ident[:, :], in_=ident[:, :], compare_op=ALU.not_equal, fill=1.0, base=0,
                               pattern=[[-1, P]], channel_multiplier=1).then_inc(consts_made, 1)
            pool.affine_select(out=later[:, :], in_=ones[:, :], compare_op=ALU.is_ge, fill=0.0, base=-32,
                               pattern=[[-32, 4], [0, 32]], channel_multiplier=1).then_inc(consts_made, 1)
            pool.affine_select(out=later_b[:, :], in_=later_b[:, :], compare_op=ALU.is_ge, fill=-BIG, base=0,
                               pattern=[[-32, 4], [0, 32]], channel_multiplier=1).then_inc(consts_made, 1)
            pool.affine_select(out=zero_floor[:, QT - 1, :], in_=zero_floor[:, QT - 1, :], compare_op=ALU.is_ge,
                               fill=BIG, base=95, pattern=[[0, 4]], channel_multiplier=-1).then_inc(consts_made, 1)
            pool.affine_select(out=head_mask[:, :], in_=ones[:, 0:8], compare_op=ALU.is_ge, fill=0.0, base=0,
                               pattern=[[-D, 8]], channel_multiplier=1).then_inc(consts_made, 1)
            pool.affine_select(out=below_b[:, :], in_=ones[:, :], compare_op=ALU.is_ge, fill=0.0, base=-1,
                               pattern=[[1, P]], channel_multiplier=-1).then_inc(consts_made, 1)
            pool.iota(tokens[:, :], pattern=[[P, TILES]], base=0, channel_multiplier=1).then_inc(consts_made, 1)
            pool.affine_select(out=upto[:, :, :], in_=upto[:, :, :], compare_op=ALU.is_ge, fill=0.0, base=0,
                               pattern=[[1, EXPERTS], [-1, EXPERTS]], channel_multiplier=0).then_inc(consts_made, 1)
            for v, first, step_ in ((desc, EXPERTS, -1), (steps128, P, P), (ovn, 0, 1)):
                pool.iota(v[:, :], pattern=[[step_, v.shape[1]]], base=first, channel_multiplier=0,
                          allow_small_or_imprecise_dtypes=True).then_inc(consts_made, 1)
            pool.wait_ge(consts_made, CONSTS - 1)
            pool.affine_select(out=head_mask[:, :], in_=head_mask[:, :], compare_op=ALU.is_ge, fill=0.0, base=D - 1,
                               pattern=[[D, 8]], channel_multiplier=-1).then_inc(consts_made, 1)
            for n, name in enumerate(WCOLS):
                at, cols = w[name + "_flat"]
                pool.wait_ge(w_high, n + 1)
                pool.tensor_tensor(w_hl[:, 1, at:at + cols], wraw[name],
                                   w_hl[:, 0, at:at + cols].bitcast(F32), ALU.subtract).then_inc(w_low, 1)
            pool.wait_ge(in_bias, 16 * len(BCOLS))
            zero = pool.to_reg(0.0)
            with pool.Fori(0, B) as b:
                for t in range(QT):
                    pool.wait_ge(k_high, b * QT + t + 1)
                    k = BANK["qk", t]
                    pool.wait_ge(k.done, k.emptied(("qk", t), b))
                    pool.tensor_tensor(ka[:, :, D:2 * D], qk[:, H:2 * H].rearrange("p (h d) -> p h d", d=D),
                                       ka[:, :, 0:D].bitcast(F32), ALU.subtract).then_inc(k_low, 1)

                def mask_keys(g):
                    if g == 0:
                        for t in range(QT):
                            k = BANK["c", t]
                            pool.wait_ge(k.done, k.emptied(("c", t), b))
                    else:
                        for j in max_jobs(g - 1)[-2:]:
                            pool.wait_ge(BANK[j].ready, BANK[j].filled(j, b))
                    pool.sem_inc(passed, 1)
                    for i in range(4):
                        h = 4 * g + i
                        ins = pool.tensor_scalar(km[:, i, :], kct[:, h // 8, :].bitcast(F32),
                                                 head_mask[:, h % 8:h % 8 + 1], None, ALU.mult)
                    ins.then_inc(km_made, 1)

                mask_keys(0)
                for g in range(GROUPS):
                    if g + 1 < GROUPS:
                        mask_keys(g + 1)
                    for n, kt in enumerate(KTORDER):
                        job = [0, 1, 1, 2][n]
                        for h in range(1, 4):
                            key = ("sc", g, job, h)
                            pool.wait_ge(BANK[key].done, BANK[key].emptied(key, b))
                            pool.sem_inc(passed, 1)
                        v = probs.rearrange("p (h n) -> p h n", h=4)[:, :, KTCOL[kt]:KTCOL[kt] + P]
                        pool.affine_select(out=v, in_=v, compare_op=ALU.is_ge, fill=zero, base=31,
                                           pattern=[[0, 4], [32, 4], [0, 32]], channel_multiplier=-1)\
                            .then_inc(masked, 1)
                pool.wait_ge(normed, b * 3 * QT + QT)
                for t in range(QT):
                    pool.tensor_tensor(x1[:, t, :], x1[:, t, :], bs["o"], ALU.add).then_inc(xb_made, 1)
                for t in range(QT):
                    key = ("pr", 1, t)
                    pool.wait_ge(BANK[key].done, BANK[key].emptied(key, b))
                    pool.tensor_tensor(x2[:, t, :], x1[:, t, :], bs["xo"], ALU.add).then_inc(xb_made, 1)
                for c in range(IC):
                    pool.wait_ge(hid_high, b * IC + c + 1)
                    pool.tensor_tensor(hhl[:, 1, c, :], hid[:, c % 2, :], hhl[:, 0, c, :].bitcast(F32),
                                       ALU.subtract).then_inc(hid_low, 1)
            pool.wait_ge(table_set, 16)
            pool.wait_ge(slots_made, 1)
            for i in range(TILES):
                pool.indirect_dma_start(out=table.rearrange("p (s o) -> (p s) o", o=1), out_offset=bass.IndirectOffsetOnAxis(ap=slot_i[:, i:i + 1].bitcast(U32), axis=0),
                                        in_=tokens[:, i:i + 1], in_offset=None).then_inc(table_put, 16)
            pool.wait_ge(row_out, 16 * TILES + 16)

            def gather(index, u):
                pool.indirect_dma_start(out=gath[:, u, :], out_offset=None, in_=rows,
                                        in_offset=bass.IndirectOffsetOnAxis(ap=index.bitcast(U32), axis=0),
                                        bounds_check=TILES * P - 1, oob_is_err=False).then_inc(gathered[u], 16)

            def scatter(index, u):
                pool.indirect_dma_start(out=out, in_=outr[:, u, :], in_offset=None,
                                        out_offset=bass.IndirectOffsetOnAxis(ap=index.bitcast(U32), axis=0),
                                        bounds_check=TILES * P - 1, oob_is_err=False).then_inc(scattered[u], 16)

            pool.wait_ge(table_in, 16)
            for t in range(RING):
                gather(tabs[:, t:t + 1], t)
            for t in range(EXPERTS):
                pool.wait_ge(e_o, t + 1)
                scatter(tabs[:, t:t + 1], t % RING)
                if t + RING < EXPERTS:
                    gather(tabs[:, t + RING:t + RING + 1], t % RING)
            for u in range(RING):
                pool.wait_ge(scattered[u], 16 * EXPERTS // RING)
            n_over = pool.value_load(ctl_i[0:1, 0:1], min_val=0, max_val=OVER)
            with pool.Fori(0, OVER) as o:
                with pool.If(o < n_over):
                    pool.wait_ge(idx_made, o + 1)
                    pool.sem_inc(passed, 1)
                    gather(idx[:, 0:1], 0)
                    pool.wait_ge(e_o, o + (EXPERTS + 1))
                    pool.sem_inc(passed, 1)
                    scatter(idx[:, 0:1], 0)
                    pool.wait_ge(scattered[0], o * 16 + (16 * EXPERTS // RING + 16))

        @block.scalar
        def _(act):
            for n, name in enumerate(WCOLS):
                at, cols = w[name + "_flat"]
                act.wait_ge(in_w, 16 * len(WCOLS))
                act.activation(w_hl[:, 0, at:at + cols], wraw[name], ACT.Copy).then_inc(w_high, 1)
            with act.Fori(0, B) as b:
                def filled(key):
                    act.wait_ge(BANK[key].ready, BANK[key].filled(key, b))
                    return BANK[key].tile

                def xt_part(s, t):
                    ps = filled(("xT", s, t))
                    act.activation(xt[:, 0, :, t * P:(t + 1) * P], ps[:, 0:H].rearrange("p (c n) -> p c n", c=HC),
                                   ACT.Copy).then_inc(xt_high, 1)

                def qa_high(t, key):
                    act.wait_ge(BANK[key].done, BANK[key].emptied(key, b))
                    act.activation(qa[:, t, :, 0:2 * D].rearrange("p h (a d) -> p h a d", a=2),
                                   qk[:, 0:H].rearrange("p (h d) -> p h d", d=D).unsqueeze(2)
                                   .broadcast_to([P, HEADS, 2, D]), ACT.Copy, scale=SCALE).then_inc(q_high, 1)

                ps = filled(("ctxT",))
                for c in range(HC):
                    ins = act.activation(ctxt[:, 0, c, :, :], ps[:, c * SC:(c + 1) * SC].unsqueeze(1)
                                         .broadcast_to([P, 2, SC]), ACT.Copy)
                ins.then_inc(ctx_high, 1)
                k = BANK["ctxkv",]
                act.wait_ge(k.done, k.emptied(("ctxkv",), b))
                act.activation(cka[:, :, :].rearrange("p h (a d) -> p h a d", a=4)[:, :, 0:4:2, :],
                               ckv[0:SC, 0:H].rearrange("p (h d) -> p h d", d=D).unsqueeze(2)
                               .broadcast_to([SC, HEADS, 2, D]), ACT.Copy).then_inc(cka_high, 1)
                for a in range(2):
                    ins = act.activation(vx[64 * a:64 * a + 64, :, a, 0:D],
                                         ckv[64 * a:64 * a + 64, H:2 * H].rearrange("p (q a d) -> p q a d", a=2, d=D)[:, :, a, :],
                                         ACT.Copy)
                    ins.then_inc(ctxv_put, 1)
                for key in [("xT", 1, 0), ("xT", 1, 1)]:
                    xt_part(1, key[2])
                for t in range(QT):
                    k = BANK["qk", t]
                    act.wait_ge(k.done, k.emptied(("qk", t), b))
                    if t > 0:
                        key = ("kA", t - 1, 1)
                        act.wait_ge(BANK[key].ready, BANK[key].filled(key, b))
                    else:
                        act.wait_ge(row_out, b * 16 * QT + 16)
                    act.activation(ka[:, :, :].rearrange("p h (a d) -> p h a d", a=4)[:, :, 0:4:2, :],
                                   qk[:, H:2 * H].rearrange("p (h d) -> p h d", d=D).unsqueeze(2)
                                   .broadcast_to([P, HEADS, 2, D]), ACT.Copy).then_inc(k_high, 1)
                    qa_high(t, ("qk", t))
                    if t + 2 < QT:
                        xt_part(1, t + 2)
                    key = ("kA", t, 0)
                    ps = filled(key)
                    act.activation(kat[:, 0:4, t * P:(t + 1) * P], ps[:, :].rearrange("p (q n) -> p q n", q=4),
                                   ACT.Copy).then_inc(BANK[key].done, 1)
                    key = ("c", t)
                    ps = filled(key)
                    act.activation(qct[:, :, t * P:(t + 1) * P], ps[:, 0:2 * P].rearrange("p (q n) -> p q n", q=2),
                                   ACT.Copy, scale=SCALE)
                    act.activation(kct[:, :, t * P:(t + 1) * P], ps[:, 2 * P:4 * P].rearrange("p (q n) -> p q n", q=2),
                                   ACT.Copy).then_inc(BANK[key].done, 1)
                for g in range(GROUPS):
                    key = ("qA", g, 0)
                    ps = filled(key)
                    act.activation(qat[:, 2 * g, :], ps[:, :], ACT.Copy).then_inc(BANK[key].done, 1)
                    for j in range(3):
                        if g > 0:
                            act.wait_ge(pv_read, b * 5 * GROUPS + 4 * (g - 1) + [1, 3, 4][j])
                        for h in range(4):
                            key = ("sc", g, j, h)
                            ps = filled(key)
                            act.activation(probs[:, h * PCOLS + PBASE[j]:h * PCOLS + PBASE[j] + EXPCOLS[j]],
                                           ps[:, 0:EXPCOLS[j]], ACT.Exp).then_inc(BANK[key].done, 1)
                act.wait_ge(emi_made, b + 1)
                act.activation(em[:, :, :], emi[:, :, :], ACT.Exp).then_inc(em_made, 1)

                def o_part(s, t):
                    key = ("o2", s, t)
                    ps = filled(key)
                    act.activation(ohl[:, 0, :, :], ps[:, 0:H].rearrange("p (c n) -> p c n", c=HC), ACT.Copy)\
                        .then_inc(o_high, 1)

                for t in range(QT):
                    o_part(1, t)
                xt_part(2, 0)
                xt_part(2, 1)
                for t in range(QT):
                    qa_high(t, ("q2", t))
                    if t + 2 < QT:
                        xt_part(2, t + 2)
                    key = ("c2", t)
                    ps = filled(key)
                    act.activation(qct[:, :, t * P:(t + 1) * P], ps[:, 0:2 * P].rearrange("p (q n) -> p q n", q=2),
                                   ACT.Copy, scale=SCALE).then_inc(BANK[key].done, 1)
                    key = ("qA2", t, 0)
                    ps = filled(key)
                    act.activation(qat[:, 0:4, t * P:(t + 1) * P], ps[:, :].rearrange("p (q n) -> p q n", q=4),
                                   ACT.Copy).then_inc(BANK[key].done, 1)
                for p in range(PAIRS):
                    key = ("sc2", p)
                    ps = filled(key)
                    act.activation(probs[:, p * S:(p + 1) * S], ps[:, :], ACT.Exp).then_inc(BANK[key].done, 1)
                for t in range(QT):
                    o_part(2, t)
                for t in range(QT):
                    xt_part(3, t)
                key = ("lg",)
                ps = filled(key)
                act.activation(lgs[:, :], ps[:, :], ACT.Copy).then_inc(BANK[key].done, 1)
                key = ("lgT",)
                act.wait_ge(BANK[key].done, BANK[key].emptied(key, b))
                act.activation(score[:, 1, :], score[:, 0, :], ACT.Tanh, scale=0.5).then_inc(btanh_made, 1)
                for c in range(IC):
                    ps = filled(("gate", c))
                    if c >= 2:
                        act.wait_ge(BANK["gate", c - 2].done, BANK["gate", c - 2].emptied(("gate", c - 2), b))
                    act.activation(th[:, c % 2, :], ps[:, :], ACT.Tanh, scale=0.5).then_inc(tanh_made, 1)
                    if c > 0:
                        act.wait_ge(BANK["up", c - 1].done, BANK["up", c - 1].emptied(("up", c - 1), b))
                        act.activation(hhl[:, 0, c - 1, :], hid[:, (c - 1) % 2, :], ACT.Copy).then_inc(hid_high, 1)
                act.wait_ge(BANK["up", IC - 1].done, BANK["up", IC - 1].emptied(("up", IC - 1), b))
                act.activation(hhl[:, 0, IC - 1, :], hid[:, (IC - 1) % 2, :], ACT.Copy).then_inc(hid_high, 1)

            def tanh_e(n):
                act.wait_ge(e_g, n)
                act.activation(the[:, :], smax[0].tile[:, :], ACT.Tanh, scale=0.5).then_inc(e_th, 1)

            with act.Fori(0, EXPERTS // RING) as i:
                for u in range(RING):
                    act.wait_ge(e_gd, i * RING + (u + 1))
                    tanh_e(i * RING + u + 1)
            act.wait_ge(slots_made, 1)
            n_over = act.value_load(ctl_i[0:1, 0:1], min_val=0, max_val=OVER)
            with act.Fori(0, OVER) as o:
                with act.If(o < n_over):
                    tanh_e(o + (EXPERTS + 1))

        @block.vector
        def _(dve):
            dve.memset(qa[:, :, :, :].bitcast(F32), 0.0)
            dve.memset(ka[:, :, :].bitcast(F32), 0.0).then_inc(vconsts_made, 1)
            dve.memset(kxt[:, :, :].bitcast(F32), 0.0).then_inc(vconsts_made, 1)
            dve.memset(vx[:, :, :, :], 0.0).then_inc(vconsts_made, 1)
            dve.memset(vb[:, :, :], 0.0).then_inc(vconsts_made, 1)
            dve.wait_ge(vconsts_made, 4)
            dve.memset(ka[:, :, 48:49].bitcast(F32), 1.0).then_inc(vconsts_made, 1)
            for a in range(2):
                dve.memset(vx[64 * a:64 * a + 64, :, a, D:D + 1], 1.0).then_inc(vconsts_made, 1)
            for t in range(QT):
                dve.memset(vb[:, t, 0:VROW].rearrange("p (h d) -> p h d", d=WIDTH)[:, :, D:D + 1], 1.0)\
                    .then_inc(vconsts_made, 1)
            dve.memset(nobody[:, :], NOBODY).then_inc(vconsts_made, 1)
            dve.memset(ones_b[:, :], 1.0).then_inc(vconsts_made, 1)
            dve.wait_ge(consts_made, CONSTS)
            dve.tensor_copy(ident_b[:, :], ident[:, :]).then_inc(vconsts_made, 1)
            dve.wait_ge(in_bias, 16 * len(BCOLS))

            step = [0]

            with dve.Fori(0, B) as b:
                def link(ins):
                    step[0] += 1
                    ins.then_inc(dve_step, 1)
                    dve.wait_ge(dve_step, b * STEPS_PER_BATCH + step[0])

                def filled(key):
                    dve.wait_ge(BANK[key].ready, BANK[key].filled(key, b))
                    return BANK[key].tile

                def layernorm(s, src):
                    for t in range(QT):
                        if s > 1:
                            key = ("pr", s - 1, t)
                            dve.wait_ge(BANK[key].done, BANK[key].emptied(key, b))
                        ins = dve.bn_stats(stats[:, t, :], src[:, t, :])
                    link(ins)
                    dve.sem_inc(passed, 1)
                    for t in range(QT):
                        ins = dve.bn_aggr(mv[:, t, :], stats[:, t, :])
                    link(ins)
                    v, y, i, a, m, c = (nrm[:, n, :] for n in range(6))
                    link(dve.tensor_scalar(v, mv[:, :, 1], EPS, None, ALU.add))
                    link(dve.tensor_scalar(i.bitcast(I32), v.bitcast(I32), 1, None, ALU.logical_shift_right))
                    link(dve.tensor_scalar(y.bitcast(I32), i.bitcast(I32), -1, RSQRT_MAGIC, ALU.mult, ALU.add))
                    for _ in range(3):
                        link(dve.tensor_tensor(a, y, y, ALU.mult))
                        link(dve.tensor_tensor(m, a, v, ALU.mult))
                        link(dve.tensor_scalar(c, m, -0.5, 1.5, ALU.mult, ALU.add))
                        link(dve.tensor_tensor(y, y, c, ALU.mult))

                def normalise(s, src, t):
                    if t >= 2:
                        key = ("xT", s, t - 2)
                        dve.wait_ge(BANK[key].ready, BANK[key].filled(key, b))
                    dve.tensor_scalar(xn[:, t % 2, :], src[:, t, :], mv[:, t, 0:1], nrm[:, 1, t:t + 1],
                                      ALU.subtract, ALU.mult).then_inc(normed, 1)

                def xt_part(s, t):
                    key = ("xT", s, t)
                    ps = filled(key)
                    dve.wait_ge(xt_high, b * 3 * QT + (s - 1) * QT + t + 1)
                    dve.tensor_tensor(xt[:, 1, :, t * P:(t + 1) * P], ps[:, 0:H].rearrange("p (c n) -> p c n", c=HC),
                                      xt[:, 0, :, t * P:(t + 1) * P].bitcast(F32), ALU.subtract)\
                        .then_inc(BANK[key].done, 1)

                def qa_low(t, n):
                    dve.wait_ge(q_high, b * 2 * QT + n + 1)
                    dve.scalar_tensor_tensor(out=qa[:, t, :, 2 * D:3 * D], in0=qk[:, 0:H].rearrange("p (h d) -> p h d", d=D),
                                             scalar=SCALE, in1=qa[:, t, :, 0:D].bitcast(F32), op0=ALU.mult,
                                             op1=ALU.subtract).then_inc(q_low, 1)

                key = ("ctxT",)
                ps = filled(key)
                dve.wait_ge(ctx_high, b + 1)
                for c in range(HC):
                    ins = dve.tensor_tensor(ctxt[:, 1, c, :, :], ps[:, c * SC:(c + 1) * SC].unsqueeze(1)
                                            .broadcast_to([P, 2, SC]), ctxt[:, 0, c, :, :].bitcast(F32), ALU.subtract)
                ins.then_inc(BANK[key].done, 1)
                dve.wait_ge(in_x, 16 * b + 16)
                layernorm(1, x1)
                normalise(1, x1, 0)
                normalise(1, x1, 1)
                key = ("ctxkv",)
                ps = filled(key)
                dve.tensor_tensor(ckv[:, :], ps[:, :], bs["xkv"], ALU.add).then_inc(BANK[key].done, 1)
                dve.wait_ge(BANK[key].done, BANK[key].emptied(key, b))
                dve.wait_ge(cka_high, b + 1)
                dve.tensor_tensor(cka[:, :, D:2 * D], ckv[0:SC, 0:H].rearrange("p (h d) -> p h d", d=D),
                                  cka[:, :, 0:D].bitcast(F32), ALU.subtract).then_inc(cka_low, 1)
                key = ("ctxkA",)
                ps = filled(key)
                for a in range(2):
                    ins = dve.tensor_copy(kxt[64 * a:64 * a + 64, :, 64 * a:64 * a + 64],
                                          ps[64 * a:64 * a + 64, :].rearrange("p (q n) -> p q n", q=PAIRS))
                ins.then_inc(BANK[key].done, 1)
                key = ("ctxkc",)
                ps = filled(key)
                for k in range(2):
                    ins = dve.tensor_tensor(kxc[:, k, :, :], ps[:, k * SC:(k + 1) * SC].unsqueeze(1).broadcast_to([P, 8, SC]),
                                            head_mask[:, :].unsqueeze(2).broadcast_to([P, 8, SC]), ALU.mult)
                ins.then_inc(BANK[key].done, 1)
                dve.wait_ge(ctxv_put, b * 2 + 2)
                xt_part(1, 0)
                xt_part(1, 1)
                for t in range(QT):
                    key = ("qk", t)
                    ps = filled(key)
                    if t > 0:
                        dve.wait_ge(k_low, b * QT + t)
                        ck = ("c", t - 1)
                        dve.wait_ge(BANK[ck].ready, BANK[ck].filled(ck, b))
                    dve.tensor_tensor(qk[:, :], ps[:, :], bs["qkv"][:, 0:2 * H], ALU.add).then_inc(BANK[key].done, 1)
                    key = ("v", t)
                    ps = filled(key)
                    dve.tensor_tensor(vb[:, t, 0:VROW].rearrange("p (h d) -> p h d", d=WIDTH)[:, :, 0:D],
                                      ps[:, 0:H].rearrange("p (h d) -> p h d", d=D),
                                      bs["qkv"][:, 2 * H:3 * H].rearrange("p (h d) -> p h d", d=D), ALU.add)\
                        .then_inc(BANK[key].done, 1)
                    qa_low(t, t)
                    if t + 2 < QT:
                        normalise(1, x1, t + 2)
                        xt_part(1, t + 2)
                    key = ("kA", t, 1)
                    ps = filled(key)
                    dve.tensor_copy(kat[:, 4:8, t * P:(t + 1) * P], ps[:, :].rearrange("p (q n) -> p q n", q=4))\
                        .then_inc(BANK[key].done, 1)

                def maxima(g):
                    for key in max_jobs(g):
                        _, _, t, h, per = key
                        ps = filled(key)
                        n = (t + 1) * P
                        dve.tensor_reduce(nmax[:, t, 4 * g + h:4 * g + h + per], ps[:, 0:per * n]
                                          .rearrange("p (h n) -> p h n", h=per), AX.X, ALU.max, negate=True)\
                            .then_inc(BANK[key].done, 1)
                    dve.wait_ge(BANK[key].done, BANK[key].emptied(key, b))
                    dve.tensor_tensor(qa[:, :, 4 * g:4 * g + 4, 48], nmax[:, :, 4 * g:4 * g + 4],
                                      zero_floor[:, :, :], ALU.min).then_inc(shift_put, 1)

                def pv_out(key, g):
                    n = 4 * (g + 1) if key[0] == "pv" else 4 * GROUPS + g + 1
                    dve.wait_ge(pv_read, b * 5 * GROUPS + n)
                    dve.tensor_copy(ots[:, g, :], pv.tile[:, :]).then_inc(pv.done, 1)

                maxima(0)
                for g in range(GROUPS):
                    if g + 1 < GROUPS:
                        maxima(g + 1)
                    key = ("qA", g, 1)
                    ps = filled(key)
                    dve.tensor_copy(qat[:, 2 * g + 1, :], ps[:, :]).then_inc(BANK[key].done, 1)
                    if g > 0:
                        pv_out(("pv", g - 1), g - 1)
                dve.wait_ge(shift_put, b * GROUPS + GROUPS)
                dve.tensor_scalar(emi[:, :, :], qa[:, :, :, 48].bitcast(F32), 0.0, None, ALU.min).then_inc(emi_made, 1)
                pv_out(("pv", GROUPS - 1), GROUPS - 1)

                def heads(v):
                    return v.rearrange("p (h d) -> p h d", h=HEADS)

                def attention_out(s):
                    for t in range(QT):
                        key = ("oT", s, t)
                        if t > 0:
                            dve.wait_ge(o_made, b * 2 * QT + (s - 1) * QT + t)
                        if s == 1:
                            sk = ("suf", t)
                            sp_ = filled(sk)
                            if t == 0:
                                dve.wait_ge(em_made, b + 1)
                            dve.tensor_tensor(heads(t17[:, :]), heads(sp_[:, 0:VROW]),
                                              em[:, t, :].unsqueeze(2).broadcast_to([P, HEADS, WIDTH]), ALU.mult)\
                                .then_inc(BANK[sk].done, 1)
                            ps = filled(key)
                            dve.wait_ge(BANK[sk].done, BANK[sk].emptied(sk, b))
                            dve.tensor_tensor(heads(num[:, :]), heads(ps[:, :])[:, :, 0:WIDTH], heads(t17[:, :]), ALU.add)\
                                .then_inc(BANK[key].done, 1)
                        else:
                            ps = filled(key)
                            dve.tensor_copy(heads(num[:, :]), heads(ps[:, :])[:, :, 0:WIDTH]).then_inc(BANK[key].done, 1)
                        dve.wait_ge(BANK[key].done, BANK[key].emptied(key, b))
                        link(dve.reciprocal(rec[:, :], heads(num[:, :])[:, :, D]))
                        dve.tensor_tensor(heads(o_all[:, t, :]), heads(num[:, :])[:, :, 0:D],
                                          rec[:, :].unsqueeze(2).broadcast_to([P, HEADS, D]), ALU.mult)\
                            .then_inc(o_made, 1)
                    for t in range(QT):
                        key = ("o2", s, t)
                        ps = filled(key)
                        dve.wait_ge(o_high, b * 2 * QT + (s - 1) * QT + t + 1)
                        dve.tensor_tensor(ohl[:, 1, :, :], ps[:, 0:H].rearrange("p (c n) -> p c n", c=HC),
                                          ohl[:, 0, :, :].bitcast(F32), ALU.subtract).then_inc(BANK[key].done, 1)
                        key = ("pr", s, t)
                        ps = filled(key)
                        dve.wait_ge(xb_made, b * 2 * QT + (s - 1) * QT + t + 1)
                        xo = (x1, x2)[s - 1]
                        dve.tensor_tensor(xo[:, t, :], ps[:, 0:H], xo[:, t, :], ALU.add).then_inc(BANK[key].done, 1)

                attention_out(1)
                layernorm(2, x1)
                for t in range(2):
                    normalise(2, x1, t)
                xt_part(2, 0)
                xt_part(2, 1)
                for t in range(QT):
                    key = ("q2", t)
                    ps = filled(key)
                    if t > 0:
                        ck = ("c2", t - 1)
                        dve.wait_ge(BANK[ck].ready, BANK[ck].filled(ck, b))
                    dve.tensor_tensor(qk[:, 0:H], ps[:, 0:H], bs["xq"], ALU.add).then_inc(BANK[key].done, 1)
                    dve.wait_ge(BANK[key].done, BANK[key].emptied(key, b))
                    qa_low(t, QT + t)
                    if t + 2 < QT:
                        normalise(2, x1, t + 2)
                        xt_part(2, t + 2)
                    for k in range(2):
                        key = ("mx2", t, k)
                        ps = filled(key)
                        dve.tensor_reduce(qa[:, t, 8 * k:8 * k + 8, 48], ps[:, :].rearrange("p (h n) -> p h n", h=8),
                                          AX.X, ALU.max, negate=True).then_inc(BANK[key].done, 1)
                    key = ("qA2", t, 1)
                    ps = filled(key)
                    dve.tensor_copy(qat[:, 4:8, t * P:(t + 1) * P], ps[:, :].rearrange("p (q n) -> p q n", q=4))\
                        .then_inc(BANK[key].done, 1)
                for g in range(GROUPS):
                    pv_out(("pv2", g), g)
                attention_out(2)
                layernorm(3, x2)
                for t in range(2):
                    normalise(3, x2, t)
                for t in range(QT):
                    xt_part(3, t)
                    if t + 2 < QT:
                        normalise(3, x2, t + 2)
                key = ("lgT",)
                ps = filled(key)
                dve.tensor_copy(lga[:, bass.ds(b * QT, QT), :], ps[:, :].rearrange("p (t e) -> p t e", t=QT)[:, :, 0:EXPERTS])
                dve.tensor_reduce(score[:, 0, :], ps[:, :].rearrange("p (t e) -> p t e", t=QT)[:, :, 0:EXPERTS],
                                  AX.X, ALU.max).then_inc(BANK[key].done, 1)
                dve.wait_ge(btanh_made, b + 1)
                link(dve.tensor_scalar(score[:, 2, :], score[:, 1, :], 0.5, 0.5, ALU.mult, ALU.add))
                link(dve.tensor_tensor(nrm[:, 2, :], score[:, 2, :], nrm[:, 1, :], ALU.mult))
                for c in range(IC):
                    key = ("gate", c)
                    ps = filled(key)
                    dve.wait_ge(tanh_made, b * IC + c + 1)
                    if c > 0:
                        dve.wait_ge(BANK["up", c - 1].done, BANK["up", c - 1].emptied(("up", c - 1), b))
                    dve.scalar_tensor_tensor(out=gated[:, :], in0=th[:, c % 2, :], scalar=1.0, in1=ps[:, :],
                                             op0=ALU.add, op1=ALU.mult).then_inc(BANK[key].done, 1)
                    dve.wait_ge(BANK[key].done, BANK[key].emptied(key, b))
                    key = ("up", c)
                    ps = filled(key)
                    if c >= 2:
                        dve.wait_ge(hid_low, b * IC + c - 1)
                    dve.scalar_tensor_tensor(out=hid[:, c % 2, :], in0=gated[:, :], scalar=0.5, in1=ps[:, :],
                                             op0=ALU.mult, op1=ALU.mult).then_inc(BANK[key].done, 1)
                for t in range(QT):
                    dve.tensor_scalar(row[:, t, 0:H], x2[:, t, :], mv[:, t, 0:1], nrm[:, 2, t:t + 1],
                                      ALU.subtract, ALU.mult).then_inc(row_made, 1)
                    key = ("dn", t)
                    ps = filled(key)
                    dve.tensor_tensor(row[:, t, H:2 * H], ps[:, 0:H], x2[:, t, :], ALU.add)\
                        .then_inc(BANK[key].done, 1)
            assert step[0] == STEPS_PER_BATCH, step[0]

            base = B * STEPS_PER_BATCH
            n2 = [0]

            def link2(ins):
                n2[0] += 1
                ins.then_inc(dve_step, 1)
                dve.wait_ge(dve_step, base + n2[0])

            def grid(k, n=TILES * EXPERTS):
                return big[:, k:k + n]

            link2(dve.tensor_reduce(place["mx"], lga[:, :, :], AX.X, ALU.max))
            link2(dve.tensor_tensor(place["a"], lga[:, :, :], place["mx"].unsqueeze(2).broadcast_to([P, TILES, EXPERTS]), ALU.is_equal))
            dsc = desc[:, :].unsqueeze(1).broadcast_to([P, TILES, EXPERTS])
            link2(dve.tensor_tensor(place["b"], place["a"], dsc, ALU.mult))
            link2(dve.tensor_reduce(place["cm"], place["b"], AX.X, ALU.max))
            dve.tensor_tensor(onehot[:, :, :], dsc, place["cm"].unsqueeze(2).broadcast_to([P, TILES, EXPERTS]), ALU.is_equal)\
                .then_inc(oh_made, 1)
            dve.wait_ge(oh_made, 1)
            dve.wait_ge(ranked, 1)
            link2(dve.tensor_tensor(place["a"], onehot[:, :, :], smax[0].tile[:, :].rearrange("p (t e) -> p t e", t=TILES), ALU.mult))
            link2(dve.tensor_reduce(place["rank"], place["a"], AX.X, ALU.add))
            link2(dve.tensor_tensor(place["c15"], place["rank"].unsqueeze(2).broadcast_to([P, TILES, OVER]),
                                    steps128[:, :].unsqueeze(1).broadcast_to([P, TILES, OVER]), ALU.is_ge))
            link2(dve.tensor_reduce(place["chunk"], place["c15"], AX.X, ALU.add))
            link2(dve.tensor_tensor(place["e15"], smax[1].tile[:, 0:EXPERTS].unsqueeze(2).broadcast_to([P, EXPERTS, OVER]),
                                    steps128[:, :].unsqueeze(1).broadcast_to([P, EXPERTS, OVER]), ALU.is_gt))
            link2(dve.tensor_reduce(place["nov"], place["e15"], AX.X, ALU.add))
            link2(dve.tensor_tensor(place["cum"], place["nov"].unsqueeze(1).broadcast_to([P, EXPERTS, EXPERTS]), upto[:, :, :], ALU.mult))
            link2(dve.tensor_reduce(place["end"], place["cum"], AX.X, ALU.add))
            link2(dve.tensor_tensor(place["beg"], place["end"], place["nov"], ALU.subtract))
            link2(dve.tensor_tensor(place["a"], onehot[:, :, :], place["beg"].unsqueeze(1).broadcast_to([P, TILES, EXPERTS]), ALU.mult))
            link2(dve.tensor_reduce(place["ob"], place["a"], AX.X, ALU.add))
            link2(dve.tensor_scalar(place["e"], place["cm"], -1.0, float(EXPERTS), ALU.mult, ALU.add))
            link2(dve.tensor_tensor(place["t1"], place["ob"], place["chunk"], ALU.add))
            link2(dve.tensor_scalar(place["t1"], place["t1"], float(EXPERTS - 1), None, ALU.add))
            link2(dve.tensor_tensor(place["t1"], place["t1"], place["e"], ALU.subtract))
            link2(dve.tensor_scalar(place["t2"], place["chunk"], 1.0, None, ALU.is_ge))
            link2(dve.tensor_tensor(place["t1"], place["t1"], place["t2"], ALU.mult))
            link2(dve.tensor_tensor(place["t1"], place["t1"], place["e"], ALU.add))
            link2(dve.scalar_tensor_tensor(out=place["t2"], in0=place["chunk"], scalar=-float(P), in1=place["rank"], op0=ALU.mult, op1=ALU.add))
            link2(dve.scalar_tensor_tensor(out=place["t3"], in0=place["t2"], scalar=float(SLOTS), in1=place["t1"], op0=ALU.mult, op1=ALU.add))
            link2(dve.tensor_copy(slot_i[:, :], place["t3"]))
            link2(dve.tensor_copy(ctl_i[0:1, 0:1], place["end"][0:1, EXPERTS - 1:EXPERTS]))
            link2(dve.tensor_tensor(place["o15"][0:1, :, :], place["end"][0:1, :].unsqueeze(1).broadcast_to([1, OVER, EXPERTS]),
                                    ovn[0:1, :].unsqueeze(2).broadcast_to([1, OVER, EXPERTS]), ALU.is_le))
            link2(dve.tensor_reduce(place["oe"][0:1, :], place["o15"][0:1, :, :], AX.X, ALU.add))
            link2(dve.tensor_scalar(ctl_i[0:1, 1:16], place["oe"][0:1, :], float(EXPERTS - 1), None, ALU.min))
            dve.memset(gath[:, :, :], 0.0).then_inc(slots_made, 1)

            dve.wait_ge(table_in, 16)

            def load_x(u, n):
                dve.wait_ge(e_t, n)
                dve.tensor_copy(xe[:, u % 2, :], misc[u % 2].tile[:, 0:H]).then_inc(e_x, 1)

            def gate(u, n):
                dve.wait_ge(e_th, n)
                dve.wait_ge(e_h, n)
                dve.scalar_tensor_tensor(out=ge[:, :], in0=the[:, :], scalar=1.0, in1=smax[0].tile[:, :], op0=ALU.add, op1=ALU.mult)\
                    .then_inc(e_gd, 1)
                dve.wait_ge(e_gd, n + 1)
                dve.wait_ge(e_u, n)
                dve.scalar_tensor_tensor(out=he[:, u % 2, :], in0=ge[:, :], scalar=0.5, in1=smax[1].tile[:, :],
                                         op0=ALU.mult, op1=ALU.mult).then_inc(e_h, 1)

            def finish(u, n, turn):
                dve.wait_ge(e_y, n)
                if turn is not None:
                    dve.wait_ge(scattered[u], turn * 16)
                dve.tensor_tensor(outr[:, u, :], sexp[u % 2].tile[:, 0:H], gath[:, u, H:2 * H], ALU.add)\
                    .then_inc(e_o, 1)

            def tiles_in_ring(i, turn):
                load_x(0, i * RING + 1)
                load_x(1, i * RING + 2)
                for u in range(RING):
                    n = i * RING + (u + 1)
                    gate(u, n)
                    if u + 2 < RING:
                        load_x(u + 2, n + 2)
                    if u > 0:
                        finish(u - 1, n - 1, turn)
                finish(RING - 1, i * RING + RING, turn)

            tiles_in_ring(0, None)
            with dve.Fori(1, EXPERTS // RING) as i:
                tiles_in_ring(i, i)
            n_over = dve.value_load(ctl_i[0:1, 0:1], min_val=0, max_val=OVER)
            with dve.Fori(0, OVER) as o:
                with dve.If(o < n_over):
                    dve.wait_ge(scattered[0], o * 16 + 16 * EXPERTS // RING)
                    dve.tensor_copy(idx[:, 0:1], tabs[:, bass.ds(o + EXPERTS, 1)]).then_inc(idx_made, 1)
                    load_x(0, o + (EXPERTS + 1))
                    gate(0, o + (EXPERTS + 1))
                    finish(0, o + (EXPERTS + 1), o + EXPERTS // RING)

        @block.tensor
        def _(pe):
            def product(out_ap, left, right, chunks):
                n = 0
                for c in range(chunks):
                    for a, k in ((0, 0), (0, 1), (1, 0)):
                        n += 1
                        ins = pe.matmul(out_ap, left(a, c), right(k, c), start=(n == 1), stop=(n == 3 * chunks))
                return ins

            pe.wait_ge(w_low, len(WCOLS))
            pe.wait_ge(consts_made, CONSTS)
            pe.wait_ge(vconsts_made, VCONSTS)
            with pe.Fori(0, B) as b:
                def free(key):
                    pe.wait_ge(BANK[key].done, BANK[key].free(key, b))
                    return BANK[key].tile

                def emptied(key):
                    pe.wait_ge(BANK[key].done, BANK[key].emptied(key, b))

                def xT(s, t):
                    key = ("xT", s, t)
                    ps = free(key)
                    pe.wait_ge(normed, b * 3 * QT + (s - 1) * QT + t + 1)
                    for c in range(HC):
                        ins = pe.transpose(ps[:, c * P:(c + 1) * P], xn[:, t % 2, c * P:(c + 1) * P], ident[:, :])
                    ins.then_inc(BANK[key].ready, 1)

                def project(key, t, name, lo, hi):
                    ps = free(key)
                    product(ps[:, 0:hi - lo], lambda a, c: xt[:, a, c, t * P:(t + 1) * P],
                            lambda a, c: w[name][:, a, c, lo:hi], HC).then_inc(BANK[key].ready, 1)

                key = ("ctxT",)
                ps = free(key)
                pe.wait_ge(in_ctx, 16 * b + 16)
                pe.sem_inc(passed, 1)
                for c in range(HC):
                    ins = pe.transpose(ps[:, c * SC:(c + 1) * SC], ctxr[:, c * P:(c + 1) * P], ident[0:SC, 0:SC])
                ins.then_inc(BANK[key].ready, 1)
                emptied(key)
                key = ("ctxkv",)
                ps = free(key)
                product(ps[:, :], lambda a, c: ctxt[:, a, c, :, :].rearrange("p a n -> p (a n)"),
                        lambda a, c: w["xkv"][:, a, c, :], HC).then_inc(BANK[key].ready, 1)
                key = ("ctxkA",)
                ps = free(key)
                pe.wait_ge(cka_low, b + 1)
                pe.sem_inc(passed, 1)
                for p in range(PAIRS):
                    ins = pe.transpose(ps[:, p * SC:(p + 1) * SC],
                                       cka[:, 2 * p:2 * p + 2, :].rearrange("p a n -> p (a n)").bitcast(F32), ident[0:SC, 0:SC])
                ins.then_inc(BANK[key].ready, 1)
                key = ("ctxkc",)
                ps = free(key)
                pe.sem_inc(passed, 1)
                for c in range(2):
                    ins = pe.transpose(ps[:, c * SC:(c + 1) * SC], ckv[0:SC, c * P:(c + 1) * P], ident[0:SC, 0:SC])
                ins.then_inc(BANK[key].ready, 1)

                xT(1, 0)
                xT(1, 1)
                for t in range(QT):
                    emptied(("xT", 1, t))
                    project(("qk", t), t, "qkv", 0, 2 * H)
                    project(("v", t), t, "qkv", 2 * H, 3 * H)
                    if t + 2 < QT:
                        xT(1, t + 2)
                    pe.wait_ge(k_low, b * QT + t + 1)
                    for half in range(2):
                        key = ("kA", t, half)
                        ps = free(key)
                        for p in range(4):
                            h = 8 * half + 2 * p
                            ins = pe.transpose(ps[:, p * P:(p + 1) * P],
                                               ka[:, h:h + 2, :].rearrange("p a n -> p (a n)").bitcast(F32), ident[:, :])
                        ins.then_inc(BANK[key].ready, 1)
                    key = ("c", t)
                    ps = free(key)
                    for p in range(4):
                        ins = pe.transpose(ps[:, p * P:(p + 1) * P], qk[:, p * P:(p + 1) * P], ident[:, :])
                    ins.then_inc(BANK[key].ready, 1)

                def maxima(g):
                    pe.wait_ge(km_made, b * GROUPS + g + 1)
                    for key in max_jobs(g):
                        _, _, t, h, per = key
                        n = (t + 1) * P
                        ps = free(key)
                        pe.matmul(ps[:, 0:per * n], qct[:, g // 2, t * P:(t + 1) * P], km[:, h:h + per, 0:n],
                                  start=True, stop=False, skip_group_check=True)
                        v = ps[:, 0:per * n].rearrange("p (h n) -> p h n", h=per)[:, :, t * P:(t + 1) * P]
                        pe.matmul(v, ident_b[:, :], later_b[:, :].unsqueeze(1).broadcast_to([P, per, P]),
                                  start=False, stop=True, skip_group_check=True).then_inc(BANK[key].ready, 1)

                def scores(g, j):
                    for h in range(4):
                        key = ("sc", g, j, h)
                        hh = 4 * g + h
                        a = 64 * (hh % 2)
                        ps = free(key)
                        for kt, col in EXPJOBS[j]:
                            ins = pe.matmul(ps[:, col:col + S - kt * P], kat[a:a + 64, hh // 2, kt * P:(kt + 1) * P],
                                            qat[a:a + 64, hh // 2, kt * P:S], start=True, stop=True)
                        ins.then_inc(BANK[key].ready, 1)

                def weigh(g, n):
                    kt = KTORDER[n]
                    key = ("pv", g)
                    if n == 0:
                        free(key)
                    pe.wait_ge(masked, b * 4 * GROUPS + 4 * g + n + 1)
                    for h in range(4):
                        hh = 4 * g + h
                        col = h * PCOLS + KTCOL[kt]
                        ins = pe.matmul(pv.tile[32 * h:32 * h + 32, kt * P:S], vb[:, kt, hh * WIDTH:hh * WIDTH + 32],
                                        probs[:, col:col + S - kt * P], start=(n == 0), stop=(n == 3),
                                        skip_group_check=True)
                    ins.then_inc(pv_read, 1)

                maxima(0)
                for g in range(GROUPS):
                    if g + 1 < GROUPS:
                        maxima(g + 1)
                    pe.wait_ge(shift_put, b * GROUPS + g + 1)
                    pe.wait_ge(q_low, b * 2 * QT + QT)
                    for j in range(2):
                        key = ("qA", g, j)
                        ps = free(key)
                        for t in range(QT):
                            h = 4 * g + 2 * j
                            ins = pe.transpose(ps[:, t * P:(t + 1) * P],
                                               qa[:, t, h:h + 2, :].rearrange("p a n -> p (a n)").bitcast(F32), ident[:, :])
                        ins.then_inc(BANK[key].ready, 1)
                    emptied(("qA", g, 0))
                    emptied(("qA", g, 1))
                    if g == 0:
                        for half in range(2):
                            emptied(("kA", QT - 1, half))
                    scores(g, 0)
                    scores(g, 1)
                    weigh(g, 0)
                    scores(g, 2)
                    for n in range(1, 4):
                        weigh(g, n)

                def attention_out(s, name):
                    emptied(("pv" if s == 1 else "pv2", GROUPS - 1))
                    for t in range(QT):
                        if s == 1:
                            key = ("suf", t)
                            ps = free(key)
                            for j in range(t, QT):
                                ins = pe.matmul(ps[:, 0:VROW], later[:, :] if j == t else ones[:, :], vb[:, j, 0:VROW],
                                                start=(j == t), stop=(j == QT - 1))
                            ins.then_inc(BANK[key].ready, 1)
                        key = ("oT", s, t)
                        ps = free(key)
                        for g in range(GROUPS):
                            ins = pe.transpose(ps[:, g * P:(g + 1) * P], ots[:, g, t * P:(t + 1) * P], ident[:, :])
                        ins.then_inc(BANK[key].ready, 1)
                    for t in range(QT):
                        key = ("o2", s, t)
                        ps = free(key)
                        pe.wait_ge(o_made, b * 2 * QT + (s - 1) * QT + t + 1)
                        for c in range(HC):
                            ins = pe.transpose(ps[:, c * P:(c + 1) * P], o_all[:, t, c * P:(c + 1) * P], ident[:, :])
                        ins.then_inc(BANK[key].ready, 1)
                        emptied(key)
                        key = ("pr", s, t)
                        ps = free(key)
                        product(ps[:, 0:H], lambda a, c: ohl[:, a, c, :], lambda a, c: w[name][:, a, c, :], HC)\
                            .then_inc(BANK[key].ready, 1)

                attention_out(1, "o")

                xT(2, 0)
                xT(2, 1)
                for t in range(QT):
                    emptied(("xT", 2, t))
                    project(("q2", t), t, "xq", 0, H)
                    if t + 2 < QT:
                        xT(2, t + 2)
                    emptied(("q2", t))
                    key = ("c2", t)
                    ps = free(key)
                    for p in range(2):
                        ins = pe.transpose(ps[:, p * P:(p + 1) * P], qk[:, p * P:(p + 1) * P], ident[:, :])
                    ins.then_inc(BANK[key].ready, 1)
                    emptied(key)
                    for k in range(2):
                        key = ("mx2", t, k)
                        ps = free(key)
                        pe.matmul(ps[:, :], qct[:, k, t * P:(t + 1) * P], kxc[:, k, :, :].rearrange("p h n -> p (h n)"),
                                  start=True, stop=True).then_inc(BANK[key].ready, 1)
                    pe.wait_ge(q_low, b * 2 * QT + QT + t + 1)
                    for half in range(2):
                        emptied(("mx2", t, half))
                        key = ("qA2", t, half)
                        ps = free(key)
                        for p in range(4):
                            h = 8 * half + 2 * p
                            ins = pe.transpose(ps[:, p * P:(p + 1) * P],
                                               qa[:, t, h:h + 2, :].rearrange("p a n -> p (a n)").bitcast(F32), ident[:, :])
                        ins.then_inc(BANK[key].ready, 1)
                emptied(("qA2", QT - 1, 0))
                emptied(("qA2", QT - 1, 1))
                emptied(("ctxkA",))

                def weigh2(p):
                    key = ("pv2", p // 2)
                    if p % 2 == 0:
                        free(key)
                    if p == 0:
                        pe.wait_ge(ctxv_put, b * 2 + 2)
                    emptied(("sc2", p))
                    a = 64 * (p % 2)
                    ins = pe.matmul(pv.tile[a:a + 64, :], vx[:, p, :, :].rearrange("p a n -> p (a n)"),
                                    probs[:, p * S:(p + 1) * S], start=True, stop=True)
                    if p % 2 == 1:
                        ins.then_inc(pv_read, 1)

                for p in range(PAIRS + 2):
                    if p < PAIRS:
                        key = ("sc2", p)
                        ps = free(key)
                        pe.matmul(ps[:, :], kxt[:, p, :], qat[:, p, :], start=True, stop=True)\
                            .then_inc(BANK[key].ready, 1)
                    if p >= 2:
                        weigh2(p - 2)
                attention_out(2, "xo")

                for t in range(QT):
                    xT(3, t)
                for t in range(QT):
                    emptied(("xT", 3, t))
                key = ("lg",)
                ps = free(key)
                product(ps[:, :], lambda a, c: w["gate"][:, a, c, :], lambda a, c: xt[:, a, c, :], HC)\
                    .then_inc(BANK[key].ready, 1)

                def up(c):
                    for key, lo in ((("gate", c), c * P), (("up", c), INNER + c * P)):
                        ps = free(key)
                        product(ps[:, :], lambda a, k: w["gu"][:, a, k, lo:lo + P], lambda a, k: xt[:, a, k, :], HC)\
                            .then_inc(BANK[key].ready, 1)

                up(0)
                emptied(("lg",))
                key = ("lgT",)
                ps = free(key)
                for t in range(QT):
                    ins = pe.transpose(ps[:, t * P:(t + 1) * P], lgs[:, t * P:(t + 1) * P], ident[:, :])
                ins.then_inc(BANK[key].ready, 1)
                for c in range(1, IC):
                    up(c)
                for t in range(QT):
                    key = ("dn", t)
                    ps = free(key)
                    pe.wait_ge(hid_low, b * IC + IC)
                    product(ps[:, 0:H], lambda a, c: hhl[:, a, c, t * P:(t + 1) * P],
                            lambda a, c: w["dn"][:, a, c, :], IC).then_inc(BANK[key].ready, 1)

            pe.wait_ge(oh_made, 1)
            v = smax[0].tile[:, :].rearrange("p (t e) -> p t e", t=TILES)
            pe.matmul(v, below_b[:, :], onehot[:, :, :], start=True, stop=False, skip_group_check=True)
            for j in range(TILES - 1):
                pe.matmul(v[:, j + 1:TILES, :], ones_b[:, :],
                          onehot[:, j, :].unsqueeze(1).broadcast_to([P, TILES - 1 - j, EXPERTS]),
                          start=False, stop=(j == TILES - 2), skip_group_check=True)
            for j in range(TILES):
                ins = pe.matmul(smax[1].tile[:, 0:EXPERTS], ones_b[:, :], onehot[:, j, :], start=(j == 0),
                                stop=(j == TILES - 1))
            ins.then_inc(ranked, 1)
            pe.wait_ge(slots_made, 1)

            def turn(u, n, i):
                pe.wait_ge(gathered[u], i * 16 + 16)
                for c in range(HC):
                    ins = pe.transpose(misc[u % 2].tile[:, c * P:(c + 1) * P], gath[:, u, c * P:(c + 1) * P], ident[:, :])
                ins.then_inc(e_t, 1)

            def widen(u, slot, n):
                pe.wait_ge(e_x, n)
                for bank_, base_, s_ in ((smax[0], 0, e_g), (smax[1], HC * INNER, e_u)):
                    for c in range(IC):
                        for k in range(HC):
                            at_ = base_ + k * INNER + c * P
                            ins = pe.matmul(bank_.tile[:, c * P:(c + 1) * P], ring[:, slot, at_:at_ + P],
                                            xe[:, u % 2, k * P:(k + 1) * P], start=(k == 0), stop=(k == HC - 1))
                    ins.then_inc(s_, 1)

            def narrow(u, slot, n):
                pe.wait_ge(e_h, n + 1)
                for c in range(IC):
                    at_ = 2 * HC * INNER + c * H
                    ins = pe.matmul(sexp[u % 2].tile[:, 0:H], he[:, u % 2, c * P:(c + 1) * P], ring[:, slot, at_:at_ + H],
                                    start=(c == 0), stop=(c == IC - 1))
                ins.then_inc(e_y, 1)

            with pe.Fori(0, EXPERTS // RING) as i:
                turn(0, i * RING + 1, i)
                turn(1, i * RING + 2, i)
                for u in range(RING):
                    n = i * RING + u + 1
                    pe.wait_ge(e_h, n)
                    pe.wait_ge(in_e[u], i * 16 + 16)
                    widen(u, u, n)
                    if u + 2 < RING:
                        turn(u + 2, n + 2, i)
                    if u > 0:
                        narrow(u - 1, u - 1, n - 1)
                narrow(RING - 1, RING - 1, i * RING + RING)
            n_over = pe.value_load(ctl_i[0:1, 0:1], min_val=0, max_val=OVER)
            with pe.Fori(0, OVER) as o:
                with pe.If(o < n_over):
                    turn(0, o + (EXPERTS + 1), o + EXPERTS // RING)
                    pe.wait_ge(in_e[0], o * 16 + (16 * EXPERTS // RING + 16))
                    widen(0, 0, o + (EXPERTS + 1))
                    narrow(0, 0, o + (EXPERTS + 1))


def kernel(**inputs):
    import numpy as np
    import concourse.bacc as bacc
    from concourse import mybir as _mybir
    from concourse.bass_utils import run_bass_kernel_spmd

    a = {k: np.asarray(v) for k, v in inputs.items()}
    join = lambda *parts: np.concatenate(parts, axis=-1)
    arrays = {
        "x": a["x"].reshape(B * S, H),
        "ctx": a["ctx_1024"].reshape(B * SC, H),
        "w_qkv": join(a["L0_attn_Wq"].T, a["L0_attn_Wk"].T, a["L0_attn_Wv"].T),
        "w_o": a["L0_attn_Wo"].T,
        "w_xq": a["L0_xattn_Wq"].T,
        "w_xkv": join(a["L0_xattn_Wk"].T, a["L0_xattn_Wv"].T),
        "w_xo": a["L0_xattn_Wo"].T,
        "w_gu": join(a["L0_ffn_shared_gate_w"], a["L0_ffn_shared_up_w"]),
        "w_dn": a["L0_ffn_shared_down_w"],
        "w_gate": join(a["L0_ffn_gate_w"], np.zeros((H, P - EXPERTS), np.float32)),
        "b_qkv": join(a["L0_attn_bq"], a["L0_attn_bk"], a["L0_attn_bv"]),
        "b_o": a["L0_attn_bo"],
        "b_xq": a["L0_xattn_bq"],
        "b_xkv": join(a["L0_xattn_bk"], a["L0_xattn_bv"]),
        "b_xo": a["L0_xattn_bo"],
        "w_experts": join(*(w.reshape(EXPERTS, -1, P, w.shape[-1]).transpose(0, 2, 1, 3).reshape(EXPERTS, P, -1)
                            for w in (a["L0_ffn_routed_gate_w"], a["L0_ffn_routed_up_w"], a["L0_ffn_routed_down_w"]))),
    }
    arrays = {k: np.ascontiguousarray(v) for k, v in arrays.items()}
    nc = bacc.Bacc("TRN2", target_bir_lowering=False, num_devices=1)
    aps = {k: nc.dram_tensor(f"in_{k}", v.shape, _mybir.dt.from_np(v.dtype), kind="ExternalInput").ap()
           for k, v in arrays.items()}
    rows = nc.dram_tensor("rows", (B * S, 2 * H), F32, kind="Internal").ap()
    table = nc.dram_tensor("table", (P, SLOTS), I32, kind="Internal").ap()
    out = nc.dram_tensor("out", (B * S, H), F32, kind="ExternalOutput").ap()
    build_decoder(nc, aps["x"], aps["ctx"], {k: aps["w_" + k] for k in WCOLS}, {k: aps["b_" + k] for k in BCOLS},
                  aps["w_experts"], rows, table, out)
    r = run_bass_kernel_spmd(nc, [{f"in_{k}": v for k, v in arrays.items()}], core_ids=[0])
    return r.results[0]["out"].reshape(B, S, H)
```

```python
from contextlib import ExitStack

import numpy as np
import concourse.bass as bass
from concourse import mybir

ALU = mybir.AluOpType
ACT = mybir.ActivationFunctionType
AX = mybir.AxisListType
F32 = mybir.dt.float32
F32R = mybir.dt.float32r
BF16 = mybir.dt.bfloat16
I32 = mybir.dt.int32
U32 = mybir.dt.uint32

P = 128
B, S, H = 4, 512, 256
HEADS, D = 16, 16
SC = 64
EXPERTS, INNER = 32, 512
QT = S // P
TILES = B * QT
HC = H // P
IC = INNER // P
GROUPS = HEADS // 4
PAIRS = HEADS // 2
OVER = TILES - 1
SLOTS = EXPERTS + OVER
RING = 4
EPS = 1e-5
SCALE = D ** -0.5
BIG = 1e30
STEPS_PER_BATCH = 49
VCONSTS = 13
CONSTS = 17
NOBODY = 4096
RSQRT_MAGIC = 0x5F3759DF
WIDTH = D + 1
VROW = HEADS * WIDTH

WCOLS = {"qkv": (HC, 3 * H), "o": (HC, H), "xq": (HC, H), "xkv": (HC, 2 * H), "xo": (HC, H),
         "gu": (HC, 2 * INNER), "dn": (IC, H), "gate": (HC, P)}
BCOLS = {"qkv": 3 * H, "o": H, "xq": H, "xkv": 2 * H, "xo": H}


class Bank:

    def __init__(self, tile, ready, done):
        self.tile, self.ready, self.done, self.order = tile, ready, done, {}

    def free(self, key, b):
        return b * len(self.order) + (self.order[key] + 1)

    def filled(self, key, b):
        return b * len(self.order) + (self.order[key] + 1)

    def emptied(self, key, b):
        return b * len(self.order) + (self.order[key] + 2)

    def cleared(self, b):
        return b * len(self.order) + 1


def projection_jobs():
    order = [("ctxT",), ("xT", 1, 0), ("xT", 1, 1), ("ctxkv",), ("qk", 0), ("v", 0), ("ctxkA",), ("ctxkc",),
             ("qk", 1), ("v", 1), ("xT", 1, 2), ("xT", 1, 3)]
    for t in range(QT):
        order += [("kA", t, 0), ("kA", t, 1), ("c", t)]
        if t + 2 < QT:
            order += [("qk", t + 2), ("v", t + 2)]
    return order


def output_steps():
    return [("o2", 0), ("o2", 1), ("pr", 0), ("o2", 2), ("pr", 1), ("o2", 3), ("pr", 2), ("pr", 3)]


def output_jobs(s):
    return [("oT", s, t) for t in range(QT)] + [(k, s, t) for k, t in output_steps()]


CROSS = [("x", 0), ("x", 1), ("p", 0), ("x", 2), ("p", 1), ("x", 3), ("c", 0), ("p", 2), ("c", 1), ("m", 0),
         ("p", 3), ("c", 2), ("m", 1), ("a", 0), ("c", 3), ("m", 2), ("a", 1), ("m", 3), ("a", 2), ("a", 3)]


def cross_jobs():
    jobs = {"x": lambda t: [("xT", 2, t)], "p": lambda t: [("q2", t)], "c": lambda t: [("c2", t)],
            "m": lambda t: [("mx2", t, k) for k in range(2)], "a": lambda t: [("qA2", t, k) for k in range(2)]}
    return [key for k, t in CROSS for key in jobs[k](t)]


def max_jobs(g):
    n = []
    for t in range(QT):
        per = max(1, 4 // (t + 1)) if t < 2 else 1
        n += [(t, h, per) for h in range(0, 4, per)]
    return [("mx", g, t, h, per) for t, h, per in n]


EXPJOBS = [[(0, 0)], [(1, 0), (3, 3 * P)], [(2, 0)]]
EXPCOLS = [4 * P, 4 * P, 2 * P]
PBASE = [0, 4 * P, 8 * P]
KTCOL = {0: 0, 1: 4 * P, 3: 7 * P, 2: 8 * P}
PCOLS = 10 * P
KTORDER = [0, 1, 3, 2]


def build_decoder(nc, x, ctx_in, weights, biases, experts_w, rows, table, out):
    with ExitStack() as stack:
        memory = {"next": -(-nc.sbuf_base // 32) * 32}
        offset = {}

        def sb(name, shape, dt=F32, over=None, skip=0):
            size = int(np.prod(shape[1:])) * (2 if dt == BF16 else 4)
            if over is None:
                offset[name] = memory["next"]
                memory["next"] += -(-size // 32) * 32
            else:
                offset[name] = offset[over] + skip
            return nc.alloc_sbuf_tensor_at(name, shape, dt, offset=offset[name])

        def sem(name):
            return stack.enter_context(nc.semaphore(name))

        wcols = sum(c * n for c, n in WCOLS.values())
        w_hl = sb("w_hl", [P, 2, wcols], F32R)
        bias = sb("bias", [P, sum(BCOLS.values())])
        x1 = sb("x1", [P, QT, H])
        sufs = sb("sufs", [P, QT, VROW])
        xn = sb("xn", [P, 2, H])
        xt = sb("xt", [P, 2, HC, S], F32R)
        qk = sb("qk", [P, 2 * H])
        qa = sb("qa", [P, QT, HEADS, 64], F32R)
        ka = sb("ka", [P, HEADS, 64], F32R)
        qat = sb("qat", [P, PAIRS, S], F32R)
        kat = sb("kat", [P, PAIRS, S], F32R)
        maxr = sb("maxr", [P, 8, S], F32R)
        probs = sb("probs", [P, 4 * PCOLS])
        vb = sb("vb", [P, QT, VROW + 16])
        ctxr = sb("ctxr", [SC, H])
        ctxt = sb("ctxt", [P, 2, HC, 2, SC], F32R)
        kxt = sb("kxt", [P, PAIRS, P], F32R)
        kxc = sb("kxc", [P, 2, 8, SC], F32R)
        vx = sb("vx", [P, PAIRS, 2, 32])
        stats = sb("stats", [P, QT, 6])
        mv = sb("mv", [P, QT, 2])
        nrm = sb("nrm", [P, 6, QT])
        nmax = sb("nmax", [P, QT, HEADS])
        emi = sb("emi", [P, QT, HEADS])
        em = sb("em", [P, QT, HEADS])
        num = sb("num", [P, VROW])
        rec = sb("rec", [P, HEADS])
        ohl = sb("ohl", [P, 2, 2, HC, P], F32R)
        score = sb("score", [P, 4, QT])
        lga = sb("lga", [P, TILES, EXPERTS])
        ident = sb("ident", [P, P])
        ident_b = sb("ident_b", [P, P], BF16)
        later_b = sb("later_b", [P, P], BF16)
        later = sb("later", [P, P])
        ones = sb("ones", [P, P])
        ones_b = sb("ones_b", [P, P], BF16)
        below_b = sb("below_b", [P, P], BF16)
        head_mask = sb("head_mask", [P, 8])
        zero_floor = sb("zero_floor", [P, QT, 4])
        upto = sb("upto", [P, EXPERTS, EXPERTS], BF16)
        onehot = sb("onehot", [P, TILES, EXPERTS], BF16)
        desc = sb("desc", [P, EXPERTS])
        steps128 = sb("steps128", [P, OVER])
        ovn = sb("ovn", [P, OVER])
        tokens = sb("tokens", [P, TILES], I32)
        nobody = sb("nobody", [P, SLOTS], I32)

        cka = ka[0:SC, :, :]
        x2 = sb("x2", [P, QT, H], over="sufs")
        qk_b = sb("qk_b", [P, 2 * H], over="probs", skip=4 * QT * H)
        ckv = sb("ckv", [P, 2 * H], over="probs", skip=4 * (QT * H + 2 * H))
        self_qk = [qk, qk_b]
        cross_q = [qk[:, 0:H], qk[:, H:2 * H], qk_b[:, 0:H], qk_b[:, H:2 * H]]
        qct = maxr[:, 0:2, :]
        kct = maxr[:, 2:4, :]
        km = maxr[:, 4:8, :]
        th = sb("th", [P, 2, S], over="maxr")
        gated = sb("gated", [P, S], over="maxr", skip=4 * 2 * S)
        hid = sb("hid", [P, 2, S], over="maxr", skip=4 * 4 * S)
        lgs = sb("lgs", [P, S], over="maxr", skip=4 * 6 * S)
        ots = sb("ots", [P, GROUPS, S], over="xt")
        hhl = sb("hhl", [P, 2, IC, S], F32R, over="probs")
        row = sb("row", [P, QT, 2 * H], over="kat")
        raw = sb("raw", [P, PAIRS * S], over="qat")
        raw2 = sb("raw2", [P, PAIRS * S], over="kat")
        w, at = {}, 0
        wraw = {}
        for name, (c, n) in WCOLS.items():
            w[name] = w_hl[:, :, at:at + c * n].rearrange("p a (c n) -> p a c n", c=c)
            w[name + "_flat"] = (at, c * n)
            at += c * n
        bs, bat = {}, 0
        for name, n in BCOLS.items():
            bs[name] = bias[:, bat:bat + n]
            bat += n
        room = {0: 0, 1: 0}
        for name in ("qkv", "gu", "o", "xq", "xkv", "xo", "dn", "gate"):
            c, n = WCOLS[name]
            k = 0 if room[0] + c * n <= PAIRS * S else 1
            wraw[name] = (raw, raw2)[k][:, room[k]:room[k] + c * n]
            room[k] += c * n
        assert max(room.values()) <= PAIRS * S

        o_all = sb("o_all", [P, QT, H], over="probs")
        ring = sb("ring", [P, RING, 3 * HC * INNER], over="w_hl")
        tabs = sb("tabs", [P, SLOTS], I32)
        slot_i = sb("slot_i", [P, TILES], I32)
        ctl_i = sb("ctl_i", [1, 16], I32)
        big = sb("big", [P, QT * HEADS * 64], over="qa")
        idx = sb("idx", [P, 1], I32)
        gath = sb("gath", [P, RING, 2 * H], over="qat")
        outr = sb("outr", [P, RING, H], over="qat", skip=4 * RING * 2 * H)
        xe = sb("xe", [P, 2, H], over="kat")
        the = sb("the", [P, INNER], over="kat", skip=4 * 512)
        ge = sb("ge", [P, INNER], over="kat", skip=4 * 1024)
        he = sb("he", [P, 2, INNER], over="kat", skip=4 * 1536)

        place = {}
        at = 0
        for name, shape in {"a": (TILES, EXPERTS), "b": (TILES, EXPERTS), "c15": (TILES, OVER), "e15": (EXPERTS, OVER),
                            "cum": (EXPERTS, EXPERTS), "mx": (TILES,), "cm": (TILES,), "rank": (TILES,),
                            "chunk": (TILES,), "nov": (EXPERTS,), "end": (EXPERTS,), "beg": (EXPERTS,),
                            "ob": (TILES,), "e": (TILES,), "t1": (TILES,), "t2": (TILES,), "t3": (TILES,),
                            "o15": (OVER, EXPERTS), "oe": (OVER,)}.items():
            n = shape[0] * (shape[1] if len(shape) > 1 else 1)
            v = big[:, at:at + n]
            place[name] = v if len(shape) == 1 else v.rearrange("p (a b) -> p a b", a=shape[0])
            at += n
        assert at <= QT * HEADS * 64

        def bank(name):
            tile = stack.enter_context(nc.psum_tensor(name, [P, 512], F32))
            return Bank(tile, sem(name + "_ready"), sem(name + "_done"))

        misc = [bank(f"misc{i}") for i in range(2)]
        smax = [bank(f"smax{i}") for i in range(2)]
        sexp = [bank(f"sexp{i}") for i in range(3)]
        pv = bank("pv")

        BANK = {}

        def put(banks, keys):
            for i, key in enumerate(keys):
                k = banks[i % len(banks)]
                BANK[key] = k
                k.order[key] = len(k.order)

        every = [*misc, *smax, *sexp]
        put(every, projection_jobs())
        put(smax, [j for g in range(GROUPS) for j in max_jobs(g)])
        put(sexp, [("sc", g, j, h) for g in range(GROUPS) for j in range(3) for h in range(4)])
        put(misc, [("suf", t) for t in range(QT)] + [("qA", g, k) for g in range(GROUPS) for k in range(2)])
        put([pv], [("pv", g) for g in range(GROUPS)])
        put(every, output_jobs(1) + cross_jobs())
        put([*smax, *sexp], [("sc2", p) for p in range(PAIRS)])
        put(misc, [("pv2", g) for g in range(GROUPS)])
        put(every, output_jobs(2) + [("xT", 3, t) for t in range(QT)] + [("lg",)])
        put(smax, [("gate", c) for c in range(IC)])
        put(sexp, [("up", c) for c in range(IC)])
        put(misc, [("lgT",)])
        put([*misc, *sexp[1:]], [("dn", t) for t in range(QT)])

        in_bias = sem("in_bias")
        in_w = sem("in_w")
        in_x = sem("in_x")
        in_ctx = sem("in_ctx")
        consts_made = sem("consts_made")
        vconsts_made = sem("vconsts_made")
        w_high = sem("w_high")
        w_low = sem("w_low")
        normed = sem("normed")
        xt_high = sem("xt_high")
        stats_made = sem("stats_made")
        dve_step = sem("dve_step")
        ctx_high = sem("ctx_high")
        ctxv_put = sem("ctxv_put")
        cka_high = sem("cka_high")
        cka_low = sem("cka_low")
        k_high = sem("k_high")
        k_low = sem("k_low")
        q_high = sem("q_high")
        q_low = sem("q_low")
        km_made = sem("km_made")
        sufs_put = sem("sufs_put")
        sufs_made = sem("sufs_made")
        shift_put = sem("shift_put")
        emi_made = sem("emi_made")
        em_made = sem("em_made")
        masked = sem("masked")
        pv_read = sem("pv_read")
        xb_made = sem("xb_made")
        o_made = sem("o_made")
        o_high = sem("o_high")
        tanh_made = sem("tanh_made")
        hid_high = sem("hid_high")
        hid_low = sem("hid_low")
        btanh_made = sem("btanh_made")
        row_made = sem("row_made")
        row_out = sem("row_out")
        table_set = sem("table_set")
        oh_made = sem("oh_made")
        ranked = sem("ranked")
        slots_made = sem("slots_made")
        table_put = sem("table_put")
        table_in = sem("table_in")
        idx_made = sem("idx_made")
        in_e = [sem(f"in_e{u}") for u in range(RING)]
        gathered = [sem(f"gathered{u}") for u in range(RING)]
        e_t = sem("e_t")
        e_x = sem("e_x")
        e_g = sem("e_g")
        e_u = sem("e_u")
        e_th = sem("e_th")
        e_gd = sem("e_gd")
        e_h = sem("e_h")
        e_y = sem("e_y")
        e_o = sem("e_o")
        scattered = [sem(f"scattered{u}") for u in range(RING)]

        passed = sem("passed")
        block = stack.enter_context(nc.Block())

        @block.sync
        def _(sp):
            for k in (*misc, *smax, *sexp, pv):
                sp.sem_inc(k.done, 1)
            sp.sem_inc(row_out, 16)
            for k in (e_gd, e_h):
                sp.sem_inc(k, 1)
            for name, n in BCOLS.items():
                sp.dma_start(bs[name], biases[name].partition_broadcast(P)).then_inc(in_bias, 16)
            for name, (c, n) in WCOLS.items():
                sp.dma_start(wraw[name].rearrange("p (c n) -> p c n", c=c),
                             weights[name].rearrange("(c p) n -> p c n", p=P)).then_inc(in_w, 16)
            sp.wait_ge(vconsts_made, VCONSTS)
            sp.dma_start(table, nobody[:, :]).then_inc(table_set, 16)
            with sp.Fori(0, B) as b:
                for t in range(QT):
                    key = ("dn", t)
                    sp.wait_ge(row_made, b * QT + t + 1)
                    sp.sem_inc(passed, 1)
                    sp.wait_ge(BANK[key].done, BANK[key].emptied(key, b))
                    sp.sem_inc(passed, 1)
                    sp.dma_start(rows.rearrange("(b t p) h -> b t p h", b=B, p=P)[b, t], row[:, t, :])\
                        .then_inc(row_out, 16)
            sp.wait_ge(table_put, 16 * TILES)
            sp.dma_start(tabs[:, :], table).then_inc(table_in, 16)
            k = BANK["dn", QT - 1]
            sp.wait_ge(k.ready, k.filled(("dn", QT - 1), B - 1))
            k = BANK["dn", QT - 2]
            sp.wait_ge(k.ready, k.filled(("dn", QT - 2), B - 1))
            for u in range(RING):
                sp.dma_start(ring[:, u, :], experts_w[u]).then_inc(in_e[u], 16)
            with sp.Fori(1, EXPERTS // RING) as i:
                for u in range(RING):
                    sp.wait_ge(e_y, i * RING + (u + 1 - RING))
                    sp.sem_inc(passed, 1)
                    sp.dma_start(ring[:, u, :], experts_w[i * RING + u]).then_inc(in_e[u], 16)
            sp.wait_ge(e_y, EXPERTS)
            n_over = sp.value_load(ctl_i[0:1, 0:1], min_val=0, max_val=OVER)
            with sp.Fori(0, OVER) as o:
                with sp.If(o < n_over):
                    e = sp.value_load(ctl_i[0:1, bass.ds(o + 1, 1)], min_val=0, max_val=EXPERTS - 1)
                    sp.wait_ge(e_y, o + EXPERTS)
                    sp.dma_start(ring[:, 0, :], experts_w[e]).then_inc(in_e[0], 16)

        @block.gpsimd
        def _(pool):
            pool.memset(ones[:, :], 1.0).then_inc(consts_made, 1)
            pool.memset(ident[:, :], 0.0).then_inc(consts_made, 1)
            pool.memset(zero_floor[:, :, :], 0.0).then_inc(consts_made, 1)
            pool.memset(later_b[:, :], 0.0).then_inc(consts_made, 1)
            pool.memset(upto[:, :, :], 1.0).then_inc(consts_made, 1)
            pool.wait_ge(consts_made, 5)
            pool.affine_select(out=ident[:, :], in_=ident[:, :], compare_op=ALU.not_equal, fill=1.0, base=0,
                               pattern=[[-1, P]], channel_multiplier=1).then_inc(consts_made, 1)
            pool.affine_select(out=later[:, :], in_=ones[:, :], compare_op=ALU.is_ge, fill=0.0, base=-32,
                               pattern=[[-32, 4], [0, 32]], channel_multiplier=1).then_inc(consts_made, 1)
            pool.affine_select(out=later_b[:, :], in_=later_b[:, :], compare_op=ALU.is_ge, fill=-BIG, base=0,
                               pattern=[[-32, 4], [0, 32]], channel_multiplier=1).then_inc(consts_made, 1)
            pool.affine_select(out=zero_floor[:, QT - 1, :], in_=zero_floor[:, QT - 1, :], compare_op=ALU.is_ge,
                               fill=BIG, base=95, pattern=[[0, 4]], channel_multiplier=-1).then_inc(consts_made, 1)
            pool.affine_select(out=head_mask[:, :], in_=ones[:, 0:8], compare_op=ALU.is_ge, fill=0.0, base=0,
                               pattern=[[-D, 8]], channel_multiplier=1).then_inc(consts_made, 1)
            pool.affine_select(out=below_b[:, :], in_=ones[:, :], compare_op=ALU.is_ge, fill=0.0, base=-1,
                               pattern=[[1, P]], channel_multiplier=-1).then_inc(consts_made, 1)
            pool.iota(tokens[:, :], pattern=[[P, TILES]], base=0, channel_multiplier=1).then_inc(consts_made, 1)
            pool.affine_select(out=upto[:, :, :], in_=upto[:, :, :], compare_op=ALU.is_ge, fill=0.0, base=0,
                               pattern=[[1, EXPERTS], [-1, EXPERTS]], channel_multiplier=0).then_inc(consts_made, 1)
            for v, first, step_ in ((desc, EXPERTS, -1), (steps128, P, P), (ovn, 0, 1)):
                pool.iota(v[:, :], pattern=[[step_, v.shape[1]]], base=first, channel_multiplier=0,
                          allow_small_or_imprecise_dtypes=True).then_inc(consts_made, 1)
            pool.wait_ge(consts_made, CONSTS - 1)
            pool.affine_select(out=head_mask[:, :], in_=head_mask[:, :], compare_op=ALU.is_ge, fill=0.0, base=D - 1,
                               pattern=[[D, 8]], channel_multiplier=-1).then_inc(consts_made, 1)
            for n, name in enumerate(WCOLS):
                at, cols = w[name + "_flat"]
                pool.wait_ge(w_high, n + 1)
                pool.tensor_tensor(w_hl[:, 1, at:at + cols], wraw[name],
                                   w_hl[:, 0, at:at + cols].bitcast(F32), ALU.subtract).then_inc(w_low, 1)
            pool.wait_ge(in_bias, 16 * len(BCOLS))
            zero = pool.to_reg(0.0)
            with pool.Fori(0, B) as b:
                for t in range(QT):
                    pool.wait_ge(k_high, b * QT + t + 1)
                    k = BANK["qk", t]
                    pool.wait_ge(k.done, k.emptied(("qk", t), b))
                    pool.tensor_tensor(ka[:, :, D:2 * D], self_qk[t % 2][:, H:2 * H].rearrange("p (h d) -> p h d", d=D),
                                       ka[:, :, 0:D].bitcast(F32), ALU.subtract).then_inc(k_low, 1)

                for g in range(GROUPS):
                    for n, kt in enumerate(KTORDER):
                        job = [0, 1, 1, 2][n]
                        for h in range(1, 4):
                            key = ("sc", g, job, h)
                            pool.wait_ge(BANK[key].done, BANK[key].emptied(key, b))
                            pool.sem_inc(passed, 1)
                        v = probs.rearrange("p (h n) -> p h n", h=4)[:, :, KTCOL[kt]:KTCOL[kt] + P]
                        pool.affine_select(out=v, in_=v, compare_op=ALU.is_ge, fill=zero, base=31,
                                           pattern=[[0, 4], [32, 4], [0, 32]], channel_multiplier=-1)\
                            .then_inc(masked, 1)
                pool.wait_ge(normed, b * 3 * QT + QT)
                for t in range(QT):
                    pool.tensor_tensor(x1[:, t, :], x1[:, t, :], bs["o"], ALU.add).then_inc(xb_made, 1)
                for t in range(QT):
                    key = ("pr", 1, t)
                    pool.wait_ge(BANK[key].done, BANK[key].emptied(key, b))
                    pool.tensor_tensor(x2[:, t, :], x1[:, t, :], bs["xo"], ALU.add).then_inc(xb_made, 1)
                for c in range(IC):
                    pool.wait_ge(hid_high, b * IC + c + 1)
                    pool.tensor_tensor(hhl[:, 1, c, :], hid[:, c % 2, :], hhl[:, 0, c, :].bitcast(F32),
                                       ALU.subtract).then_inc(hid_low, 1)
            pool.wait_ge(table_set, 16)
            pool.wait_ge(slots_made, 1)
            for i in range(TILES):
                pool.indirect_dma_start(out=table.rearrange("p (s o) -> (p s) o", o=1), out_offset=bass.IndirectOffsetOnAxis(ap=slot_i[:, i:i + 1].bitcast(U32), axis=0),
                                        in_=tokens[:, i:i + 1], in_offset=None).then_inc(table_put, 16)
            pool.wait_ge(row_out, 16 * TILES + 16)

            def gather(index, u):
                pool.indirect_dma_start(out=gath[:, u, :], out_offset=None, in_=rows,
                                        in_offset=bass.IndirectOffsetOnAxis(ap=index.bitcast(U32), axis=0),
                                        bounds_check=TILES * P - 1, oob_is_err=False).then_inc(gathered[u], 16)

            def scatter(index, u):
                pool.indirect_dma_start(out=out, in_=outr[:, u, :], in_offset=None,
                                        out_offset=bass.IndirectOffsetOnAxis(ap=index.bitcast(U32), axis=0),
                                        bounds_check=TILES * P - 1, oob_is_err=False).then_inc(scattered[u], 16)

            pool.wait_ge(table_in, 16)
            for t in range(RING):
                gather(tabs[:, t:t + 1], t)
            for t in range(EXPERTS):
                pool.wait_ge(e_o, t + 1)
                scatter(tabs[:, t:t + 1], t % RING)
                if t + RING < EXPERTS:
                    gather(tabs[:, t + RING:t + RING + 1], t % RING)
            for u in range(RING):
                pool.wait_ge(scattered[u], 16 * EXPERTS // RING)
            n_over = pool.value_load(ctl_i[0:1, 0:1], min_val=0, max_val=OVER)
            with pool.Fori(0, OVER) as o:
                with pool.If(o < n_over):
                    pool.wait_ge(idx_made, o + 1)
                    pool.sem_inc(passed, 1)
                    gather(idx[:, 0:1], 0)
                    pool.wait_ge(e_o, o + (EXPERTS + 1))
                    pool.sem_inc(passed, 1)
                    scatter(idx[:, 0:1], 0)
                    pool.wait_ge(scattered[0], o * 16 + (16 * EXPERTS // RING + 16))

        @block.scalar
        def _(act):
            for n, name in enumerate(WCOLS):
                at, cols = w[name + "_flat"]
                act.wait_ge(in_w, 16 * len(WCOLS))
                act.activation(w_hl[:, 0, at:at + cols], wraw[name], ACT.Copy).then_inc(w_high, 1)
            with act.Fori(0, B) as b:
                def filled(key):
                    act.wait_ge(BANK[key].ready, BANK[key].filled(key, b))
                    return BANK[key].tile

                def xt_part(s, t):
                    ps = filled(("xT", s, t))
                    act.activation(xt[:, 0, :, t * P:(t + 1) * P], ps[:, 0:H].rearrange("p (c n) -> p c n", c=HC),
                                   ACT.Copy).then_inc(xt_high, 1)

                def qa_high(t, key, q):
                    act.wait_ge(BANK[key].done, BANK[key].emptied(key, b))
                    act.activation(qa[:, t, :, 0:2 * D].rearrange("p h (a d) -> p h a d", a=2),
                                   q.rearrange("p (h d) -> p h d", d=D).unsqueeze(2)
                                   .broadcast_to([P, HEADS, 2, D]), ACT.Copy, scale=SCALE).then_inc(q_high, 1)

                for key in (("lg",), ("lgT",)):
                    act.wait_ge(BANK[key].done, BANK[key].cleared(b))
                    act.sem_inc(passed, 1)
                act.dma_start(x1[:, :, :], x.rearrange("(b t p) h -> b p t h", b=B, p=P)[b])\
                    .then_inc(in_x, 16)
                k = BANK["ctxT",]
                act.wait_ge(k.done, k.cleared(b))
                act.sem_inc(passed, 1)
                act.dma_start(ctxr[:, :], ctx_in.rearrange("(b s) h -> b s h", b=B)[b]).then_inc(in_ctx, 16)
                ps = filled(("ctxT",))
                for c in range(HC):
                    ins = act.activation(ctxt[:, 0, c, :, :], ps[:, c * SC:(c + 1) * SC].unsqueeze(1)
                                         .broadcast_to([P, 2, SC]), ACT.Copy)
                ins.then_inc(ctx_high, 1)
                xt_part(1, 0)
                xt_part(1, 1)
                k = BANK["ctxkv",]
                act.wait_ge(k.done, k.emptied(("ctxkv",), b))
                act.wait_ge(row_out, b * 16 * QT + 16)
                act.activation(cka[:, :, :].rearrange("p h (a d) -> p h a d", a=4)[:, :, 0:4:2, :],
                               ckv[0:SC, 0:H].rearrange("p (h d) -> p h d", d=D).unsqueeze(2)
                               .broadcast_to([SC, HEADS, 2, D]), ACT.Copy).then_inc(cka_high, 1)
                for a in range(2):
                    ins = act.activation(vx[64 * a:64 * a + 64, :, a, 0:D],
                                         ckv[64 * a:64 * a + 64, H:2 * H].rearrange("p (q a d) -> p q a d", a=2, d=D)[:, :, a, :],
                                         ACT.Copy)
                    ins.then_inc(ctxv_put, 1)

                def ka_high(t):
                    key = ("qk", t)
                    act.wait_ge(BANK[key].done, BANK[key].emptied(key, b))
                    key = ("kA", t - 1, 1) if t > 0 else ("ctxkA",)
                    act.wait_ge(BANK[key].ready, BANK[key].filled(key, b))
                    act.activation(ka[:, :, :].rearrange("p h (a d) -> p h a d", a=4)[:, :, 0:4:2, :],
                                   self_qk[t % 2][:, H:2 * H].rearrange("p (h d) -> p h d", d=D).unsqueeze(2)
                                   .broadcast_to([P, HEADS, 2, D]), ACT.Copy).then_inc(k_high, 1)

                def put_keys(t):
                    key = ("kA", t, 0)
                    ps = filled(key)
                    act.activation(kat[:, 0:4, t * P:(t + 1) * P], ps[:, :].rearrange("p (q n) -> p q n", q=4),
                                   ACT.Copy).then_inc(BANK[key].done, 1)
                    key = ("c", t)
                    ps = filled(key)
                    act.activation(qct[:, :, t * P:(t + 1) * P], ps[:, 0:2 * P].rearrange("p (q n) -> p q n", q=2),
                                   ACT.Copy, scale=SCALE)
                    act.activation(kct[:, :, t * P:(t + 1) * P], ps[:, 2 * P:4 * P].rearrange("p (q n) -> p q n", q=2),
                                   ACT.Copy).then_inc(BANK[key].done, 1)

                ka_high(0)
                qa_high(0, ("qk", 0), self_qk[0][:, 0:H])
                qa_high(1, ("qk", 1), self_qk[1][:, 0:H])
                xt_part(1, 2)
                xt_part(1, 3)
                for t in range(QT):
                    put_keys(t)
                    if t + 1 < QT:
                        ka_high(t + 1)
                    if t + 2 < QT:
                        qa_high(t + 2, ("qk", t + 2), self_qk[t % 2][:, 0:H])

                def mask_keys(g):
                    if g == 0:
                        for t in range(QT):
                            k = BANK["c", t]
                            act.wait_ge(k.done, k.emptied(("c", t), b))
                    else:
                        for j in max_jobs(g - 1)[-2:]:
                            act.wait_ge(BANK[j].ready, BANK[j].filled(j, b))
                    for i in range(4):
                        h = 4 * g + i
                        ins = act.activation(km[:, i, :], kct[:, h // 8, :].bitcast(F32), ACT.Copy,
                                             scale=head_mask[:, h % 8:h % 8 + 1])
                    ins.then_inc(km_made, 1)

                mask_keys(0)
                for t in range(QT):
                    key = ("suf", t)
                    ps = filled(key)
                    act.activation(sufs[:, t, :], ps[:, 0:VROW], ACT.Copy).then_inc(BANK[key].done, 1)
                mask_keys(1)
                for g in range(GROUPS):
                    if 0 < g < GROUPS - 1:
                        mask_keys(g + 1)
                    key = ("qA", g, 0)
                    ps = filled(key)
                    act.activation(qat[:, 2 * g, :], ps[:, :], ACT.Copy).then_inc(BANK[key].done, 1)
                    for j in range(3):
                        if g > 0:
                            act.wait_ge(pv_read, b * 4 * GROUPS + 4 * (g - 1) + [1, 3, 4][j])
                        for h in range(4):
                            key = ("sc", g, j, h)
                            ps = filled(key)
                            act.activation(probs[:, h * PCOLS + PBASE[j]:h * PCOLS + PBASE[j] + EXPCOLS[j]],
                                           ps[:, 0:EXPCOLS[j]], ACT.Exp).then_inc(BANK[key].done, 1)
                act.wait_ge(emi_made, b + 1)
                act.activation(em[:, :, :], emi[:, :, :], ACT.Exp).then_inc(em_made, 1)

                def o_part(s, t):
                    if t >= 2:
                        key = ("pr", s, t - 2)
                        act.wait_ge(BANK[key].ready, BANK[key].filled(key, b))
                    key = ("o2", s, t)
                    ps = filled(key)
                    act.activation(ohl[:, t % 2, 0, :, :], ps[:, 0:H].rearrange("p (c n) -> p c n", c=HC), ACT.Copy)\
                        .then_inc(o_high, 1)

                for t in range(QT):
                    o_part(1, t)

                def put_q(t):
                    key = ("c2", t)
                    ps = filled(key)
                    act.activation(qct[:, :, t * P:(t + 1) * P], ps[:, 0:2 * P].rearrange("p (q n) -> p q n", q=2),
                                   ACT.Copy, scale=SCALE).then_inc(BANK[key].done, 1)

                def put_qat(t):
                    key = ("qA2", t, 0)
                    ps = filled(key)
                    act.activation(qat[:, 0:4, t * P:(t + 1) * P], ps[:, :].rearrange("p (q n) -> p q n", q=4),
                                   ACT.Copy).then_inc(BANK[key].done, 1)

                for k, t in CROSS:
                    if k == "x":
                        xt_part(2, t)
                    elif k == "p":
                        qa_high(t, ("q2", t), cross_q[t])
                    elif k == "c":
                        put_q(t)
                    elif k == "a":
                        put_qat(t)
                for p in range(PAIRS):
                    key = ("sc2", p)
                    ps = filled(key)
                    act.activation(probs[:, p * S:(p + 1) * S], ps[:, :], ACT.Exp).then_inc(BANK[key].done, 1)
                for t in range(QT):
                    o_part(2, t)
                for t in range(QT):
                    xt_part(3, t)
                key = ("lg",)
                ps = filled(key)
                act.activation(lgs[:, :], ps[:, :], ACT.Copy).then_inc(BANK[key].done, 1)
                key = ("lgT",)
                act.wait_ge(BANK[key].done, BANK[key].emptied(key, b))
                act.activation(score[:, 1, :], score[:, 0, :], ACT.Tanh, scale=0.5).then_inc(btanh_made, 1)
                for c in range(IC):
                    ps = filled(("gate", c))
                    if c >= 2:
                        act.wait_ge(BANK["gate", c - 2].done, BANK["gate", c - 2].emptied(("gate", c - 2), b))
                    act.activation(th[:, c % 2, :], ps[:, :], ACT.Tanh, scale=0.5).then_inc(tanh_made, 1)
                    if c > 0:
                        act.wait_ge(BANK["up", c - 1].done, BANK["up", c - 1].emptied(("up", c - 1), b))
                        act.activation(hhl[:, 0, c - 1, :], hid[:, (c - 1) % 2, :], ACT.Copy).then_inc(hid_high, 1)
                act.wait_ge(BANK["up", IC - 1].done, BANK["up", IC - 1].emptied(("up", IC - 1), b))
                act.activation(hhl[:, 0, IC - 1, :], hid[:, (IC - 1) % 2, :], ACT.Copy).then_inc(hid_high, 1)

            def tanh_e(n):
                act.wait_ge(e_g, n)
                act.activation(the[:, :], smax[0].tile[:, :], ACT.Tanh, scale=0.5).then_inc(e_th, 1)

            with act.Fori(0, EXPERTS // RING) as i:
                for u in range(RING):
                    act.wait_ge(e_gd, i * RING + (u + 1))
                    tanh_e(i * RING + u + 1)
            act.wait_ge(slots_made, 1)
            n_over = act.value_load(ctl_i[0:1, 0:1], min_val=0, max_val=OVER)
            with act.Fori(0, OVER) as o:
                with act.If(o < n_over):
                    tanh_e(o + (EXPERTS + 1))

        @block.vector
        def _(dve):
            dve.memset(qa[:, :, :, :].bitcast(F32), 0.0)
            dve.memset(ka[:, :, :].bitcast(F32), 0.0).then_inc(vconsts_made, 1)
            dve.memset(kxt[:, :, :].bitcast(F32), 0.0).then_inc(vconsts_made, 1)
            dve.memset(vx[:, :, :, :], 0.0).then_inc(vconsts_made, 1)
            dve.memset(vb[:, :, :], 0.0).then_inc(vconsts_made, 1)
            dve.wait_ge(vconsts_made, 4)
            dve.memset(ka[:, :, 48:49].bitcast(F32), 1.0).then_inc(vconsts_made, 1)
            for a in range(2):
                dve.memset(vx[64 * a:64 * a + 64, :, a, D:D + 1], 1.0).then_inc(vconsts_made, 1)
            for t in range(QT):
                dve.memset(vb[:, t, 0:VROW].rearrange("p (h d) -> p h d", d=WIDTH)[:, :, D:D + 1], 1.0)\
                    .then_inc(vconsts_made, 1)
            dve.memset(nobody[:, :], NOBODY).then_inc(vconsts_made, 1)
            dve.memset(ones_b[:, :], 1.0).then_inc(vconsts_made, 1)
            dve.wait_ge(consts_made, CONSTS)
            dve.tensor_copy(ident_b[:, :], ident[:, :]).then_inc(vconsts_made, 1)
            dve.wait_ge(in_bias, 16 * len(BCOLS))

            step = [0]

            with dve.Fori(0, B) as b:
                def link(ins):
                    step[0] += 1
                    ins.then_inc(dve_step, 1)
                    dve.wait_ge(dve_step, b * STEPS_PER_BATCH + step[0])

                def filled(key):
                    dve.wait_ge(BANK[key].ready, BANK[key].filled(key, b))
                    return BANK[key].tile

                def statistics(src, t):
                    dve.bn_stats(stats[:, t, :], src[:, t, :]).then_inc(stats_made, 1)

                def layernorm(s):
                    dve.wait_ge(stats_made, b * 3 * QT + s * QT)
                    dve.sem_inc(passed, 1)
                    for t in range(QT):
                        ins = dve.bn_aggr(mv[:, t, :], stats[:, t, :])
                    link(ins)
                    v, y, i, a, m = (nrm[:, n, :] for n in range(5))
                    link(dve.tensor_scalar(v, mv[:, :, 1], EPS, None, ALU.add))
                    link(dve.tensor_scalar(i.bitcast(I32), v.bitcast(I32), 1, None, ALU.logical_shift_right))
                    link(dve.tensor_scalar(y.bitcast(I32), i.bitcast(I32), -1, RSQRT_MAGIC, ALU.mult, ALU.add))
                    for _ in range(3):
                        link(dve.tensor_tensor(a, y, y, ALU.mult))
                        link(dve.scalar_tensor_tensor(out=m, in0=a, scalar=-0.5, in1=v, op0=ALU.mult, op1=ALU.mult))
                        link(dve.scalar_tensor_tensor(out=y, in0=m, scalar=1.5, in1=y, op0=ALU.add, op1=ALU.mult))

                def normalise(s, src, t):
                    if t >= 2:
                        key = ("xT", s, t - 2)
                        dve.wait_ge(BANK[key].ready, BANK[key].filled(key, b))
                    dve.tensor_scalar(xn[:, t % 2, :], src[:, t, :], mv[:, t, 0:1], nrm[:, 1, t:t + 1],
                                      ALU.subtract, ALU.mult).then_inc(normed, 1)

                def xt_part(s, t):
                    key = ("xT", s, t)
                    ps = filled(key)
                    dve.wait_ge(xt_high, b * 3 * QT + (s - 1) * QT + t + 1)
                    dve.tensor_tensor(xt[:, 1, :, t * P:(t + 1) * P], ps[:, 0:H].rearrange("p (c n) -> p c n", c=HC),
                                      xt[:, 0, :, t * P:(t + 1) * P].bitcast(F32), ALU.subtract)\
                        .then_inc(BANK[key].done, 1)

                def qa_low(t, n, q):
                    dve.wait_ge(q_high, b * 2 * QT + n + 1)
                    dve.scalar_tensor_tensor(out=qa[:, t, :, 2 * D:3 * D], in0=q.rearrange("p (h d) -> p h d", d=D),
                                             scalar=SCALE, in1=qa[:, t, :, 0:D].bitcast(F32), op0=ALU.mult,
                                             op1=ALU.subtract).then_inc(q_low, 1)

                key = ("ctxT",)
                ps = filled(key)
                dve.wait_ge(ctx_high, b + 1)
                for c in range(HC):
                    ins = dve.tensor_tensor(ctxt[:, 1, c, :, :], ps[:, c * SC:(c + 1) * SC].unsqueeze(1)
                                            .broadcast_to([P, 2, SC]), ctxt[:, 0, c, :, :].bitcast(F32), ALU.subtract)
                ins.then_inc(BANK[key].done, 1)
                dve.wait_ge(in_x, 16 * b + 16)
                dve.sem_inc(passed, 1)
                for t in range(QT):
                    statistics(x1, t)
                layernorm(1)
                normalise(1, x1, 0)
                normalise(1, x1, 1)
                xt_part(1, 0)
                normalise(1, x1, 2)
                xt_part(1, 1)
                normalise(1, x1, 3)
                key = ("ctxkv",)
                ps = filled(key)
                dve.tensor_tensor(ckv[:, :], ps[:, :], bs["xkv"], ALU.add).then_inc(BANK[key].done, 1)
                dve.wait_ge(BANK[key].done, BANK[key].emptied(key, b))
                dve.wait_ge(cka_high, b + 1)
                dve.tensor_tensor(cka[:, :, D:2 * D], ckv[0:SC, 0:H].rearrange("p (h d) -> p h d", d=D),
                                  cka[:, :, 0:D].bitcast(F32), ALU.subtract).then_inc(cka_low, 1)

                def put_projections(t):
                    key = ("qk", t)
                    ps = filled(key)
                    if t >= 2:
                        dve.wait_ge(k_low, b * QT + t - 1)
                        ck = ("c", t - 2)
                        dve.wait_ge(BANK[ck].ready, BANK[ck].filled(ck, b))
                    dve.tensor_tensor(self_qk[t % 2][:, :], ps[:, :], bs["qkv"][:, 0:2 * H], ALU.add)\
                        .then_inc(BANK[key].done, 1)
                    key = ("v", t)
                    ps = filled(key)
                    dve.tensor_tensor(vb[:, t, 0:VROW].rearrange("p (h d) -> p h d", d=WIDTH)[:, :, 0:D],
                                      ps[:, 0:H].rearrange("p (h d) -> p h d", d=D),
                                      bs["qkv"][:, 2 * H:3 * H].rearrange("p (h d) -> p h d", d=D), ALU.add)\
                        .then_inc(BANK[key].done, 1)
                    qa_low(t, t, self_qk[t % 2][:, 0:H])

                put_projections(0)
                key = ("ctxkA",)
                ps = filled(key)
                for a in range(2):
                    ins = dve.tensor_copy(kxt[64 * a:64 * a + 64, :, 64 * a:64 * a + 64],
                                          ps[64 * a:64 * a + 64, :].rearrange("p (q n) -> p q n", q=PAIRS))
                ins.then_inc(BANK[key].done, 1)
                key = ("ctxkc",)
                ps = filled(key)
                for k in range(2):
                    ins = dve.tensor_tensor(kxc[:, k, :, :], ps[:, k * SC:(k + 1) * SC].unsqueeze(1).broadcast_to([P, 8, SC]),
                                            head_mask[:, :].unsqueeze(2).broadcast_to([P, 8, SC]), ALU.mult)
                ins.then_inc(BANK[key].done, 1)
                dve.wait_ge(ctxv_put, b * 2 + 2)
                put_projections(1)
                xt_part(1, 2)
                xt_part(1, 3)
                for t in range(QT):
                    key = ("kA", t, 1)
                    ps = filled(key)
                    dve.tensor_copy(kat[:, 4:8, t * P:(t + 1) * P], ps[:, :].rearrange("p (q n) -> p q n", q=4))\
                        .then_inc(BANK[key].done, 1)
                    if t + 2 < QT:
                        put_projections(t + 2)

                def maxima(g):
                    for key in max_jobs(g):
                        _, _, t, h, per = key
                        ps = filled(key)
                        n = (t + 1) * P
                        dve.tensor_reduce(nmax[:, t, 4 * g + h:4 * g + h + per], ps[:, 0:per * n]
                                          .rearrange("p (h n) -> p h n", h=per), AX.X, ALU.max, negate=True)\
                            .then_inc(BANK[key].done, 1)
                    dve.wait_ge(BANK[key].done, BANK[key].emptied(key, b))
                    dve.tensor_tensor(qa[:, :, 4 * g:4 * g + 4, 48], nmax[:, :, 4 * g:4 * g + 4],
                                      zero_floor[:, :, :], ALU.min).then_inc(shift_put, 1)

                def pv_out(key, g):
                    if key[0] == "pv":
                        dve.wait_ge(pv_read, b * 4 * GROUPS + 4 * (g + 1))
                    else:
                        filled(key)
                    dve.tensor_copy(ots[:, g, :], BANK[key].tile[:, :]).then_inc(BANK[key].done, 1)

                def heads(v):
                    return v.rearrange("p (h d) -> p h d", h=HEADS)

                maxima(0)
                for g in range(GROUPS):
                    key = ("qA", g, 1)
                    ps = filled(key)
                    dve.tensor_copy(qat[:, 2 * g + 1, :], ps[:, :]).then_inc(BANK[key].done, 1)
                    if g > 0:
                        pv_out(("pv", g - 1), g - 1)
                    if g + 1 < GROUPS:
                        maxima(g + 1)
                dve.wait_ge(shift_put, b * GROUPS + GROUPS)
                dve.tensor_scalar(emi[:, :, :], qa[:, :, :, 48].bitcast(F32), 0.0, None, ALU.min).then_inc(emi_made, 1)
                for t in range(QT):
                    key = ("suf", t)
                    dve.wait_ge(BANK[key].done, BANK[key].emptied(key, b))
                dve.wait_ge(em_made, b + 1)
                dve.tensor_tensor(sufs.rearrange("p t (h d) -> p (t h) d", d=WIDTH),
                                  sufs.rearrange("p t (h d) -> p (t h) d", d=WIDTH),
                                  em.rearrange("p t h -> p (t h)").unsqueeze(2).broadcast_to([P, QT * HEADS, WIDTH]),
                                  ALU.mult).then_inc(sufs_made, 1)
                pv_out(("pv", GROUPS - 1), GROUPS - 1)

                def attention_out(s):
                    def normed_out(t):
                        key = ("oT", s, t)
                        if t > 0:
                            dve.wait_ge(o_made, b * 2 * QT + (s - 1) * QT + t)
                        ps = filled(key)
                        if s == 1:
                            if t == 0:
                                dve.wait_ge(sufs_made, b + 1)
                            dve.tensor_tensor(heads(num[:, :]), heads(ps[:, :])[:, :, 0:WIDTH], heads(sufs[:, t, :]), ALU.add)\
                                .then_inc(BANK[key].done, 1)
                        else:
                            dve.tensor_copy(heads(num[:, :]), heads(ps[:, :])[:, :, 0:WIDTH]).then_inc(BANK[key].done, 1)
                        dve.wait_ge(BANK[key].done, BANK[key].emptied(key, b))
                        link(dve.reciprocal(rec[:, :], heads(num[:, :])[:, :, D]))
                        dve.tensor_tensor(heads(o_all[:, t, :]), heads(num[:, :])[:, :, 0:D],
                                          rec[:, :].unsqueeze(2).broadcast_to([P, HEADS, D]), ALU.mult)\
                            .then_inc(o_made, 1)

                    normed_out(0)
                    normed_out(1)
                    for k, t in output_steps():
                        key = (k, s, t)
                        ps = filled(key)
                        if k == "o2":
                            dve.wait_ge(o_high, b * 2 * QT + (s - 1) * QT + t + 1)
                            dve.tensor_tensor(ohl[:, t % 2, 1, :, :], ps[:, 0:H].rearrange("p (c n) -> p c n", c=HC),
                                              ohl[:, t % 2, 0, :, :].bitcast(F32), ALU.subtract).then_inc(BANK[key].done, 1)
                            if t + 2 < QT:
                                normed_out(t + 2)
                        else:
                            dve.wait_ge(xb_made, b * 2 * QT + (s - 1) * QT + t + 1)
                            xo = (x1, x2)[s - 1]
                            dve.tensor_tensor(xo[:, t, :], ps[:, 0:H], xo[:, t, :], ALU.add).then_inc(BANK[key].done, 1)
                            if t > 0:
                                before = ("pr", s, t - 1)
                                dve.wait_ge(BANK[before].done, BANK[before].emptied(before, b))
                                statistics(xo, t - 1)
                    dve.wait_ge(BANK[key].done, BANK[key].emptied(key, b))
                    statistics(xo, QT - 1)
                    layernorm(s + 1)

                attention_out(1)
                normalise(2, x1, 0)
                normalise(2, x1, 1)
                for k, t in CROSS:
                    if k == "x":
                        xt_part(2, t)
                        if t + 2 < QT:
                            normalise(2, x1, t + 2)
                    elif k == "p":
                        key = ("q2", t)
                        ps = filled(key)
                        dve.tensor_tensor(cross_q[t], ps[:, 0:H], bs["xq"], ALU.add).then_inc(BANK[key].done, 1)
                        dve.wait_ge(BANK[key].done, BANK[key].emptied(key, b))
                        qa_low(t, QT + t, cross_q[t])
                    elif k == "m":
                        for half in range(2):
                            key = ("mx2", t, half)
                            ps = filled(key)
                            dve.tensor_reduce(qa[:, t, 8 * half:8 * half + 8, 48], ps[:, :].rearrange("p (h n) -> p h n", h=8),
                                              AX.X, ALU.max, negate=True).then_inc(BANK[key].done, 1)
                    elif k == "a":
                        key = ("qA2", t, 1)
                        ps = filled(key)
                        dve.tensor_copy(qat[:, 4:8, t * P:(t + 1) * P], ps[:, :].rearrange("p (q n) -> p q n", q=4))\
                            .then_inc(BANK[key].done, 1)
                for g in range(GROUPS):
                    pv_out(("pv2", g), g)
                attention_out(2)
                for t in range(2):
                    normalise(3, x2, t)
                for t in range(QT):
                    xt_part(3, t)
                    if t + 2 < QT:
                        normalise(3, x2, t + 2)
                key = ("lgT",)
                ps = filled(key)
                dve.tensor_copy(lga[:, bass.ds(b * QT, QT), :], ps[:, :].rearrange("p (t e) -> p t e", t=QT)[:, :, 0:EXPERTS])
                dve.tensor_reduce(score[:, 0, :], ps[:, :].rearrange("p (t e) -> p t e", t=QT)[:, :, 0:EXPERTS],
                                  AX.X, ALU.max).then_inc(BANK[key].done, 1)
                dve.wait_ge(btanh_made, b + 1)
                link(dve.tensor_scalar(score[:, 2, :], score[:, 1, :], 0.5, 0.5, ALU.mult, ALU.add))
                link(dve.tensor_tensor(nrm[:, 2, :], score[:, 2, :], nrm[:, 1, :], ALU.mult))
                for t in range(QT):
                    dve.tensor_scalar(row[:, t, 0:H], x2[:, t, :], mv[:, t, 0:1], nrm[:, 2, t:t + 1],
                                      ALU.subtract, ALU.mult).then_inc(row_made, 1)
                for c in range(IC):
                    key = ("gate", c)
                    ps = filled(key)
                    dve.wait_ge(tanh_made, b * IC + c + 1)
                    if c > 0:
                        dve.wait_ge(BANK["up", c - 1].done, BANK["up", c - 1].emptied(("up", c - 1), b))
                    dve.scalar_tensor_tensor(out=gated[:, :], in0=th[:, c % 2, :], scalar=1.0, in1=ps[:, :],
                                             op0=ALU.add, op1=ALU.mult).then_inc(BANK[key].done, 1)
                    dve.wait_ge(BANK[key].done, BANK[key].emptied(key, b))
                    key = ("up", c)
                    ps = filled(key)
                    if c >= 2:
                        dve.wait_ge(hid_low, b * IC + c - 1)
                    dve.scalar_tensor_tensor(out=hid[:, c % 2, :], in0=gated[:, :], scalar=0.5, in1=ps[:, :],
                                             op0=ALU.mult, op1=ALU.mult).then_inc(BANK[key].done, 1)
                for t in range(QT):
                    key = ("dn", t)
                    ps = filled(key)
                    dve.tensor_tensor(row[:, t, H:2 * H], ps[:, 0:H], x2[:, t, :], ALU.add)\
                        .then_inc(BANK[key].done, 1)
            assert step[0] == STEPS_PER_BATCH, step[0]

            base = B * STEPS_PER_BATCH
            n2 = [0]

            def link2(ins):
                n2[0] += 1
                ins.then_inc(dve_step, 1)
                dve.wait_ge(dve_step, base + n2[0])

            def grid(k, n=TILES * EXPERTS):
                return big[:, k:k + n]

            link2(dve.tensor_reduce(place["mx"], lga[:, :, :], AX.X, ALU.max))
            link2(dve.tensor_tensor(place["a"], lga[:, :, :], place["mx"].unsqueeze(2).broadcast_to([P, TILES, EXPERTS]), ALU.is_equal))
            dsc = desc[:, :].unsqueeze(1).broadcast_to([P, TILES, EXPERTS])
            link2(dve.tensor_tensor(place["b"], place["a"], dsc, ALU.mult))
            link2(dve.tensor_reduce(place["cm"], place["b"], AX.X, ALU.max))
            dve.tensor_tensor(onehot[:, :, :], dsc, place["cm"].unsqueeze(2).broadcast_to([P, TILES, EXPERTS]), ALU.is_equal)\
                .then_inc(oh_made, 1)
            dve.wait_ge(oh_made, 1)
            dve.wait_ge(ranked, 1)
            link2(dve.tensor_tensor(place["a"], onehot[:, :, :], smax[0].tile[:, :].rearrange("p (t e) -> p t e", t=TILES), ALU.mult))
            link2(dve.tensor_reduce(place["rank"], place["a"], AX.X, ALU.add))
            link2(dve.tensor_tensor(place["c15"], place["rank"].unsqueeze(2).broadcast_to([P, TILES, OVER]),
                                    steps128[:, :].unsqueeze(1).broadcast_to([P, TILES, OVER]), ALU.is_ge))
            link2(dve.tensor_reduce(place["chunk"], place["c15"], AX.X, ALU.add))
            link2(dve.tensor_tensor(place["e15"], smax[1].tile[:, 0:EXPERTS].unsqueeze(2).broadcast_to([P, EXPERTS, OVER]),
                                    steps128[:, :].unsqueeze(1).broadcast_to([P, EXPERTS, OVER]), ALU.is_gt))
            link2(dve.tensor_reduce(place["nov"], place["e15"], AX.X, ALU.add))
            link2(dve.tensor_tensor(place["cum"], place["nov"].unsqueeze(1).broadcast_to([P, EXPERTS, EXPERTS]), upto[:, :, :], ALU.mult))
            link2(dve.tensor_reduce(place["end"], place["cum"], AX.X, ALU.add))
            link2(dve.tensor_tensor(place["beg"], place["end"], place["nov"], ALU.subtract))
            link2(dve.tensor_tensor(place["a"], onehot[:, :, :], place["beg"].unsqueeze(1).broadcast_to([P, TILES, EXPERTS]), ALU.mult))
            link2(dve.tensor_reduce(place["ob"], place["a"], AX.X, ALU.add))
            link2(dve.tensor_scalar(place["e"], place["cm"], -1.0, float(EXPERTS), ALU.mult, ALU.add))
            link2(dve.tensor_tensor(place["t1"], place["ob"], place["chunk"], ALU.add))
            link2(dve.tensor_scalar(place["t1"], place["t1"], float(EXPERTS - 1), None, ALU.add))
            link2(dve.tensor_tensor(place["t1"], place["t1"], place["e"], ALU.subtract))
            link2(dve.tensor_scalar(place["t2"], place["chunk"], 1.0, None, ALU.is_ge))
            link2(dve.tensor_tensor(place["t1"], place["t1"], place["t2"], ALU.mult))
            link2(dve.tensor_tensor(place["t1"], place["t1"], place["e"], ALU.add))
            link2(dve.scalar_tensor_tensor(out=place["t2"], in0=place["chunk"], scalar=-float(P), in1=place["rank"], op0=ALU.mult, op1=ALU.add))
            link2(dve.scalar_tensor_tensor(out=place["t3"], in0=place["t2"], scalar=float(SLOTS), in1=place["t1"], op0=ALU.mult, op1=ALU.add))
            link2(dve.tensor_copy(slot_i[:, :], place["t3"]))
            link2(dve.tensor_copy(ctl_i[0:1, 0:1], place["end"][0:1, EXPERTS - 1:EXPERTS]))
            link2(dve.tensor_tensor(place["o15"][0:1, :, :], place["end"][0:1, :].unsqueeze(1).broadcast_to([1, OVER, EXPERTS]),
                                    ovn[0:1, :].unsqueeze(2).broadcast_to([1, OVER, EXPERTS]), ALU.is_le))
            link2(dve.tensor_reduce(place["oe"][0:1, :], place["o15"][0:1, :, :], AX.X, ALU.add))
            link2(dve.tensor_scalar(ctl_i[0:1, 1:16], place["oe"][0:1, :], float(EXPERTS - 1), None, ALU.min))
            dve.memset(gath[:, :, :], 0.0).then_inc(slots_made, 1)

            dve.wait_ge(table_in, 16)

            def load_x(u, n):
                dve.wait_ge(e_t, n)
                dve.tensor_copy(xe[:, u % 2, :], misc[u % 2].tile[:, 0:H]).then_inc(e_x, 1)

            def gate(u, n):
                dve.wait_ge(e_th, n)
                dve.wait_ge(e_h, n)
                dve.scalar_tensor_tensor(out=ge[:, :], in0=the[:, :], scalar=1.0, in1=smax[0].tile[:, :], op0=ALU.add, op1=ALU.mult)\
                    .then_inc(e_gd, 1)
                dve.wait_ge(e_gd, n + 1)
                dve.wait_ge(e_u, n)
                dve.scalar_tensor_tensor(out=he[:, u % 2, :], in0=ge[:, :], scalar=0.5, in1=smax[1].tile[:, :],
                                         op0=ALU.mult, op1=ALU.mult).then_inc(e_h, 1)

            def finish(u, n, turn):
                dve.wait_ge(e_y, n)
                if turn is not None:
                    dve.wait_ge(scattered[u], turn * 16)
                dve.tensor_tensor(outr[:, u, :], sexp[u % 2].tile[:, 0:H], gath[:, u, H:2 * H], ALU.add)\
                    .then_inc(e_o, 1)

            def tiles_in_ring(i, turn):
                load_x(0, i * RING + 1)
                load_x(1, i * RING + 2)
                for u in range(RING):
                    n = i * RING + (u + 1)
                    gate(u, n)
                    if u + 2 < RING:
                        load_x(u + 2, n + 2)
                    if u > 0:
                        finish(u - 1, n - 1, turn)
                finish(RING - 1, i * RING + RING, turn)

            tiles_in_ring(0, None)
            with dve.Fori(1, EXPERTS // RING) as i:
                tiles_in_ring(i, i)
            n_over = dve.value_load(ctl_i[0:1, 0:1], min_val=0, max_val=OVER)
            with dve.Fori(0, OVER) as o:
                with dve.If(o < n_over):
                    dve.wait_ge(scattered[0], o * 16 + 16 * EXPERTS // RING)
                    dve.tensor_copy(idx[:, 0:1], tabs[:, bass.ds(o + EXPERTS, 1)]).then_inc(idx_made, 1)
                    load_x(0, o + (EXPERTS + 1))
                    gate(0, o + (EXPERTS + 1))
                    finish(0, o + (EXPERTS + 1), o + EXPERTS // RING)

        @block.tensor
        def _(pe):
            def product(out_ap, left, right, chunks):
                n = 0
                for c in range(chunks):
                    for a, k in ((0, 0), (0, 1), (1, 0)):
                        n += 1
                        ins = pe.matmul(out_ap, left(a, c), right(k, c), start=(n == 1), stop=(n == 3 * chunks))
                return ins

            pe.wait_ge(w_low, len(WCOLS))
            pe.wait_ge(consts_made, CONSTS)
            pe.wait_ge(vconsts_made, VCONSTS)
            with pe.Fori(0, B) as b:
                def free(key):
                    pe.wait_ge(BANK[key].done, BANK[key].free(key, b))
                    return BANK[key].tile

                def emptied(*keys, then=None):
                    for n, key in enumerate(keys):
                        if all(BANK[k] is not BANK[key] for k in (*keys[n + 1:], *([then] if then else []))):
                            pe.wait_ge(BANK[key].done, BANK[key].emptied(key, b))

                def xT(s, t):
                    key = ("xT", s, t)
                    ps = free(key)
                    pe.wait_ge(normed, b * 3 * QT + (s - 1) * QT + t + 1)
                    for c in range(HC):
                        ins = pe.transpose(ps[:, c * P:(c + 1) * P], xn[:, t % 2, c * P:(c + 1) * P], ident[:, :])
                    ins.then_inc(BANK[key].ready, 1)

                def project(key, t, name, lo, hi):
                    ps = free(key)
                    product(ps[:, 0:hi - lo], lambda a, c: xt[:, a, c, t * P:(t + 1) * P],
                            lambda a, c: w[name][:, a, c, lo:hi], HC).then_inc(BANK[key].ready, 1)

                def keys_T(t):
                    pe.wait_ge(k_low, b * QT + t + 1)
                    for half in range(2):
                        key = ("kA", t, half)
                        ps = free(key)
                        for p in range(4):
                            h = 8 * half + 2 * p
                            ins = pe.transpose(ps[:, p * P:(p + 1) * P],
                                               ka[:, h:h + 2, :].rearrange("p a n -> p (a n)").bitcast(F32), ident[:, :])
                        ins.then_inc(BANK[key].ready, 1)
                    key = ("c", t)
                    ps = free(key)
                    for p in range(4):
                        ins = pe.transpose(ps[:, p * P:(p + 1) * P], self_qk[t % 2][:, p * P:(p + 1) * P], ident[:, :])
                    ins.then_inc(BANK[key].ready, 1)

                def project_qkv(t):
                    emptied(("xT", 1, t), then=("qk", t))
                    project(("qk", t), t, "qkv", 0, 2 * H)
                    project(("v", t), t, "qkv", 2 * H, 3 * H)

                key = ("ctxT",)
                ps = free(key)
                pe.wait_ge(in_ctx, 16 * b + 16)
                pe.sem_inc(passed, 1)
                for c in range(HC):
                    ins = pe.transpose(ps[:, c * SC:(c + 1) * SC], ctxr[:, c * P:(c + 1) * P], ident[0:SC, 0:SC])
                ins.then_inc(BANK[key].ready, 1)
                xT(1, 0)
                xT(1, 1)
                emptied(("ctxT",), then=("ctxkv",))
                key = ("ctxkv",)
                ps = free(key)
                product(ps[:, :], lambda a, c: ctxt[:, a, c, :, :].rearrange("p a n -> p (a n)"),
                        lambda a, c: w["xkv"][:, a, c, :], HC).then_inc(BANK[key].ready, 1)
                project_qkv(0)
                key = ("ctxkA",)
                ps = free(key)
                pe.wait_ge(cka_low, b + 1)
                pe.sem_inc(passed, 1)
                for p in range(PAIRS):
                    ins = pe.transpose(ps[:, p * SC:(p + 1) * SC],
                                       cka[:, 2 * p:2 * p + 2, :].rearrange("p a n -> p (a n)").bitcast(F32), ident[0:SC, 0:SC])
                ins.then_inc(BANK[key].ready, 1)
                key = ("ctxkc",)
                ps = free(key)
                pe.sem_inc(passed, 1)
                for c in range(2):
                    ins = pe.transpose(ps[:, c * SC:(c + 1) * SC], ckv[0:SC, c * P:(c + 1) * P], ident[0:SC, 0:SC])
                ins.then_inc(BANK[key].ready, 1)

                project_qkv(1)
                xT(1, 2)
                xT(1, 3)
                for t in range(QT):
                    keys_T(t)
                    if t + 2 < QT:
                        project_qkv(t + 2)

                def maximum(key):
                    _, g, t, h, per = key
                    n = (t + 1) * P
                    ps = free(key)
                    pe.matmul(ps[:, 0:per * n], qct[:, g // 2, t * P:(t + 1) * P], km[:, h:h + per, 0:n],
                              start=True, stop=False, skip_group_check=True)
                    v = ps[:, 0:per * n].rearrange("p (h n) -> p h n", h=per)[:, :, t * P:(t + 1) * P]
                    pe.matmul(v, ident_b[:, :], later_b[:, :].unsqueeze(1).broadcast_to([P, per, P]),
                              start=False, stop=True, skip_group_check=True).then_inc(BANK[key].ready, 1)

                def score(g, j, h):
                    key = ("sc", g, j, h)
                    hh = 4 * g + h
                    a = 64 * (hh % 2)
                    ps = free(key)
                    for kt, col in EXPJOBS[j]:
                        ins = pe.matmul(ps[:, col:col + S - kt * P], kat[a:a + 64, hh // 2, kt * P:(kt + 1) * P],
                                        qat[a:a + 64, hh // 2, kt * P:S], start=True, stop=True)
                    ins.then_inc(BANK[key].ready, 1)

                def weigh(g, n):
                    kt = KTORDER[n]
                    key = ("pv", g)
                    if n == 0:
                        free(key)
                    pe.wait_ge(masked, b * 4 * GROUPS + 4 * g + n + 1)
                    for h in range(4):
                        hh = 4 * g + h
                        col = h * PCOLS + KTCOL[kt]
                        ins = pe.matmul(pv.tile[32 * h:32 * h + 32, kt * P:S], vb[:, kt, hh * WIDTH:hh * WIDTH + 32],
                                        probs[:, col:col + S - kt * P], start=(n == 0), stop=(n == 3),
                                        skip_group_check=True)
                    ins.then_inc(pv_read, 1)

                for t in range(QT):
                    key = ("suf", t)
                    if t == 0:
                        emptied(*(("v", j) for j in range(QT)), then=key)
                    ps = free(key)
                    for j in range(t, QT):
                        ins = pe.matmul(ps[:, 0:VROW], later[:, :] if j == t else ones[:, :], vb[:, j, 0:VROW],
                                        start=(j == t), stop=(j == QT - 1))
                    ins.then_inc(BANK[key].ready, 1)
                pe.wait_ge(km_made, b * GROUPS + 1)
                for key in max_jobs(0):
                    maximum(key)
                pe.wait_ge(q_low, b * 2 * QT + QT)
                for g in range(GROUPS):
                    pe.wait_ge(shift_put, b * GROUPS + g + 1)
                    for j in range(2):
                        key = ("qA", g, j)
                        ps = free(key)
                        for t in range(QT):
                            h = 4 * g + 2 * j
                            ins = pe.transpose(ps[:, t * P:(t + 1) * P],
                                               qa[:, t, h:h + 2, :].rearrange("p a n -> p (a n)").bitcast(F32), ident[:, :])
                        ins.then_inc(BANK[key].ready, 1)
                    if g > 0:
                        weigh(g - 1, 2)
                        weigh(g - 1, 3)
                    keys = [("kA", QT - 1, half) for half in range(2)] if g == 0 else []
                    emptied(*keys, ("qA", g, 0), ("qA", g, 1), then=("sc", g, 0, 0))
                    ahead = max_jobs(g + 1) if g + 1 < GROUPS else []
                    if ahead:
                        pe.wait_ge(km_made, b * GROUPS + g + 2)
                    for n in range(12):
                        score(g, n // 4, n % 4)
                        if n < len(ahead):
                            maximum(ahead[n])
                        if n == 8:
                            weigh(g, 0)
                    weigh(g, 1)
                weigh(GROUPS - 1, 2)
                weigh(GROUPS - 1, 3)

                def attention_out(s, name):
                    emptied(*(("pv" if s == 1 else "pv2", g) for g in range(GROUPS)), then=("oT", s, 0))
                    for t in range(QT):
                        key = ("oT", s, t)
                        ps = free(key)
                        for g in range(GROUPS):
                            ins = pe.transpose(ps[:, g * P:(g + 1) * P], ots[:, g, t * P:(t + 1) * P], ident[:, :])
                        ins.then_inc(BANK[key].ready, 1)
                    for k, t in output_steps():
                        key = (k, s, t)
                        if k == "o2":
                            ps = free(key)
                            pe.wait_ge(o_made, b * 2 * QT + (s - 1) * QT + t + 1)
                            for c in range(HC):
                                ins = pe.transpose(ps[:, c * P:(c + 1) * P], o_all[:, t, c * P:(c + 1) * P], ident[:, :])
                            ins.then_inc(BANK[key].ready, 1)
                        else:
                            emptied(("o2", s, t), then=key)
                            ps = free(key)
                            product(ps[:, 0:H], lambda a, c: ohl[:, t % 2, a, c, :], lambda a, c: w[name][:, a, c, :], HC)\
                                .then_inc(BANK[key].ready, 1)

                attention_out(1, "o")

                def transpose_q(t):
                    emptied(("q2", t), then=("c2", t))
                    key = ("c2", t)
                    ps = free(key)
                    for p in range(2):
                        ins = pe.transpose(ps[:, p * P:(p + 1) * P], cross_q[t][:, p * P:(p + 1) * P], ident[:, :])
                    ins.then_inc(BANK[key].ready, 1)

                def maximum2(t):
                    emptied(("c2", t), then=("mx2", t, 0))
                    for k in range(2):
                        key = ("mx2", t, k)
                        ps = free(key)
                        pe.matmul(ps[:, :], qct[:, k, t * P:(t + 1) * P], kxc[:, k, :, :].rearrange("p h n -> p (h n)"),
                                  start=True, stop=True).then_inc(BANK[key].ready, 1)

                def transpose_qa(t):
                    pe.wait_ge(q_low, b * 2 * QT + QT + t + 1)
                    for half in range(2):
                        emptied(("mx2", t, half), then=("qA2", t, half))
                        key = ("qA2", t, half)
                        ps = free(key)
                        for p in range(4):
                            h = 8 * half + 2 * p
                            ins = pe.transpose(ps[:, p * P:(p + 1) * P],
                                               qa[:, t, h:h + 2, :].rearrange("p a n -> p (a n)").bitcast(F32), ident[:, :])
                        ins.then_inc(BANK[key].ready, 1)

                for k, t in CROSS:
                    if k == "x":
                        xT(2, t)
                    elif k == "p":
                        emptied(("xT", 2, t), then=("q2", t))
                        project(("q2", t), t, "xq", 0, H)
                    elif k == "c":
                        transpose_q(t)
                    elif k == "m":
                        maximum2(t)
                    elif k == "a":
                        transpose_qa(t)
                emptied(("ctxkA",), *(("qA2", t, half) for t in range(QT) for half in range(2)), then=("sc2", 0))

                def weigh2(p):
                    key = ("pv2", p // 2)
                    if p % 2 == 0:
                        free(key)
                    if p == 0:
                        pe.wait_ge(ctxv_put, b * 2 + 2)
                    emptied(("sc2", p))
                    a = 64 * (p % 2)
                    ins = pe.matmul(BANK[key].tile[a:a + 64, :], vx[:, p, :, :].rearrange("p a n -> p (a n)"),
                                    probs[:, p * S:(p + 1) * S], start=True, stop=True)
                    if p % 2 == 1:
                        ins.then_inc(BANK[key].ready, 1)

                for p in range(PAIRS + 2):
                    if p < PAIRS:
                        key = ("sc2", p)
                        ps = free(key)
                        pe.matmul(ps[:, :], kxt[:, p, :], qat[:, p, :], start=True, stop=True)\
                            .then_inc(BANK[key].ready, 1)
                    if p >= 2:
                        weigh2(p - 2)
                attention_out(2, "xo")

                for t in range(QT):
                    xT(3, t)
                emptied(*(("xT", 3, t) for t in range(QT)), then=("lg",))
                key = ("lg",)
                ps = free(key)
                product(ps[:, :], lambda a, c: w["gate"][:, a, c, :], lambda a, c: xt[:, a, c, :], HC)\
                    .then_inc(BANK[key].ready, 1)

                def up(c):
                    for key, lo in ((("gate", c), c * P), (("up", c), INNER + c * P)):
                        ps = free(key)
                        product(ps[:, :], lambda a, k: w["gu"][:, a, k, lo:lo + P], lambda a, k: xt[:, a, k, :], HC)\
                            .then_inc(BANK[key].ready, 1)

                up(0)
                emptied(("lg",))
                key = ("lgT",)
                ps = free(key)
                for t in range(QT):
                    ins = pe.transpose(ps[:, t * P:(t + 1) * P], lgs[:, t * P:(t + 1) * P], ident[:, :])
                ins.then_inc(BANK[key].ready, 1)
                for c in range(1, IC):
                    up(c)
                for c in range(IC):
                    pe.wait_ge(hid_low, b * IC + c + 1)
                    for t in range(QT):
                        key = ("dn", t)
                        ps = free(key) if c == 0 else BANK[key].tile
                        for n, (a, k) in enumerate(((0, 0), (0, 1), (1, 0))):
                            ins = pe.matmul(ps[:, 0:H], hhl[:, a, c, t * P:(t + 1) * P], w["dn"][:, k, c, :],
                                            start=(c == 0 and n == 0), stop=(c == IC - 1 and n == 2))
                        if c == IC - 1:
                            ins.then_inc(BANK[key].ready, 1)

            pe.wait_ge(oh_made, 1)
            v = smax[0].tile[:, :].rearrange("p (t e) -> p t e", t=TILES)
            pe.matmul(v, below_b[:, :], onehot[:, :, :], start=True, stop=False, skip_group_check=True)
            for j in range(TILES - 1):
                pe.matmul(v[:, j + 1:TILES, :], ones_b[:, :],
                          onehot[:, j, :].unsqueeze(1).broadcast_to([P, TILES - 1 - j, EXPERTS]),
                          start=False, stop=(j == TILES - 2), skip_group_check=True)
            for j in range(TILES):
                ins = pe.matmul(smax[1].tile[:, 0:EXPERTS], ones_b[:, :], onehot[:, j, :], start=(j == 0),
                                stop=(j == TILES - 1))
            ins.then_inc(ranked, 1)
            pe.wait_ge(slots_made, 1)

            def turn(u, n, i):
                pe.wait_ge(gathered[u], i * 16 + 16)
                for c in range(HC):
                    ins = pe.transpose(misc[u % 2].tile[:, c * P:(c + 1) * P], gath[:, u, c * P:(c + 1) * P], ident[:, :])
                ins.then_inc(e_t, 1)

            def widen(u, slot, n):
                pe.wait_ge(e_x, n)
                for bank_, base_, s_ in ((smax[0], 0, e_g), (smax[1], HC * INNER, e_u)):
                    for c in range(IC):
                        for k in range(HC):
                            at_ = base_ + k * INNER + c * P
                            ins = pe.matmul(bank_.tile[:, c * P:(c + 1) * P], ring[:, slot, at_:at_ + P],
                                            xe[:, u % 2, k * P:(k + 1) * P], start=(k == 0), stop=(k == HC - 1))
                    ins.then_inc(s_, 1)

            def narrow(u, slot, n):
                pe.wait_ge(e_h, n + 1)
                for c in range(IC):
                    at_ = 2 * HC * INNER + c * H
                    ins = pe.matmul(sexp[u % 2].tile[:, 0:H], he[:, u % 2, c * P:(c + 1) * P], ring[:, slot, at_:at_ + H],
                                    start=(c == 0), stop=(c == IC - 1))
                ins.then_inc(e_y, 1)

            with pe.Fori(0, EXPERTS // RING) as i:
                turn(0, i * RING + 1, i)
                turn(1, i * RING + 2, i)
                for u in range(RING):
                    n = i * RING + u + 1
                    pe.wait_ge(e_h, n)
                    pe.wait_ge(in_e[u], i * 16 + 16)
                    widen(u, u, n)
                    if u + 2 < RING:
                        turn(u + 2, n + 2, i)
                    if u > 0:
                        narrow(u - 1, u - 1, n - 1)
                narrow(RING - 1, RING - 1, i * RING + RING)
            n_over = pe.value_load(ctl_i[0:1, 0:1], min_val=0, max_val=OVER)
            with pe.Fori(0, OVER) as o:
                with pe.If(o < n_over):
                    turn(0, o + (EXPERTS + 1), o + EXPERTS // RING)
                    pe.wait_ge(in_e[0], o * 16 + (16 * EXPERTS // RING + 16))
                    widen(0, 0, o + (EXPERTS + 1))
                    narrow(0, 0, o + (EXPERTS + 1))


def kernel(**inputs):
    import numpy as np
    import concourse.bacc as bacc
    from concourse import mybir as _mybir
    from concourse.bass_utils import run_bass_kernel_spmd

    a = {k: np.asarray(v) for k, v in inputs.items()}
    join = lambda *parts: np.concatenate(parts, axis=-1)
    arrays = {
        "x": a["x"].reshape(B * S, H),
        "ctx": a["ctx_1024"].reshape(B * SC, H),
        "w_qkv": join(a["L0_attn_Wq"].T, a["L0_attn_Wk"].T, a["L0_attn_Wv"].T),
        "w_o": a["L0_attn_Wo"].T,
        "w_xq": a["L0_xattn_Wq"].T,
        "w_xkv": join(a["L0_xattn_Wk"].T, a["L0_xattn_Wv"].T),
        "w_xo": a["L0_xattn_Wo"].T,
        "w_gu": join(a["L0_ffn_shared_gate_w"], a["L0_ffn_shared_up_w"]),
        "w_dn": a["L0_ffn_shared_down_w"],
        "w_gate": join(a["L0_ffn_gate_w"], np.zeros((H, P - EXPERTS), np.float32)),
        "b_qkv": join(a["L0_attn_bq"], a["L0_attn_bk"], a["L0_attn_bv"]),
        "b_o": a["L0_attn_bo"],
        "b_xq": a["L0_xattn_bq"],
        "b_xkv": join(a["L0_xattn_bk"], a["L0_xattn_bv"]),
        "b_xo": a["L0_xattn_bo"],
        "w_experts": join(*(w.reshape(EXPERTS, -1, P, w.shape[-1]).transpose(0, 2, 1, 3).reshape(EXPERTS, P, -1)
                            for w in (a["L0_ffn_routed_gate_w"], a["L0_ffn_routed_up_w"], a["L0_ffn_routed_down_w"]))),
    }
    arrays = {k: np.ascontiguousarray(v) for k, v in arrays.items()}
    nc = bacc.Bacc("TRN2", target_bir_lowering=False, num_devices=1)
    aps = {k: nc.dram_tensor(f"in_{k}", v.shape, _mybir.dt.from_np(v.dtype), kind="ExternalInput").ap()
           for k, v in arrays.items()}
    rows = nc.dram_tensor("rows", (B * S, 2 * H), F32, kind="Internal").ap()
    table = nc.dram_tensor("table", (P, SLOTS), I32, kind="Internal").ap()
    out = nc.dram_tensor("out", (B * S, H), F32, kind="ExternalOutput").ap()
    build_decoder(nc, aps["x"], aps["ctx"], {k: aps["w_" + k] for k in WCOLS}, {k: aps["b_" + k] for k in BCOLS},
                  aps["w_experts"], rows, table, out)
    r = run_bass_kernel_spmd(nc, [{f"in_{k}": v for k, v in arrays.items()}], core_ids=[0])
    return r.results[0]["out"].reshape(B, S, H)
```

```python
from contextlib import ExitStack, nullcontext

import numpy as np
import concourse.bass as bass
from concourse import mybir

ALU = mybir.AluOpType
ACT = mybir.ActivationFunctionType
AX = mybir.AxisListType
F32 = mybir.dt.float32
F32R = mybir.dt.float32r
BF16 = mybir.dt.bfloat16
I32 = mybir.dt.int32
U32 = mybir.dt.uint32

P = 128
B, S, H = 4, 512, 256
HEADS, D = 16, 16
SC = 64
EXPERTS, INNER = 32, 512
QT = S // P
TILES = B * QT
HC = H // P
IC = INNER // P
GROUPS = HEADS // 4
PAIRS = HEADS // 2
OVER = TILES - 1
CHUNKS = TILES
COLUMNS = CHUNKS * EXPERTS
DEPTH = 8
RING = 4
EPS = 1e-5
SCALE = D ** -0.5
BIG = 1e30
STEPS_PER_BATCH = 55
VCONSTS = 14
CONSTS = 18
NOBODY = 2 * B * S
RSQRT_MAGIC = 0x5F3759DF
WIDTH = D + 1
VROW = HEADS * WIDTH

WCOLS = {"qkv": (HC, 3 * H), "o": (HC, H), "xq": (HC, H), "xkv": (HC, 2 * H), "xo": (HC, H),
         "gu": (HC, 2 * INNER), "dn": (IC, H), "gate": (HC, P)}
WORDER = ("xkv", "qkv", "gu", "o", "xq", "xo", "gate", "dn")
GPSIMD_SPLITS = ("gu", "dn")
WPARTS = {"qkv": ((0, H, SCALE), (H, 3 * H, 1.0)), "xq": ((0, H, SCALE),)}
BCOLS = {"qkv": 3 * H, "o": H, "xq": H, "xkv": 2 * H, "xo": H}


class Bank:

    def __init__(self, tile, ready, done):
        self.tile, self.ready, self.done, self.order = tile, ready, done, {}

    def free(self, key, b):
        return b * len(self.order) + (self.order[key] + 1)

    def filled(self, key, b):
        return b * len(self.order) + (self.order[key] + 1)

    def emptied(self, key, b):
        return b * len(self.order) + (self.order[key] + 2)

    def cleared(self, b):
        return b * len(self.order) + 1


def projection_jobs():
    order = [("xT", 1, 0), ("xT", 1, 1), ("qk", 0), ("v", 0), ("qk", 1), ("v", 1), ("xT", 1, 2), ("xT", 1, 3)]
    for t in range(QT):
        if t == QT - 1:
            order += [("suf", QT - 1), ("suf", QT - 2)]
        order += [("kA", t, 0), ("kA", t, 1), ("c", t)]
        if t + 2 < QT:
            order += [("qk", t + 2), ("v", t + 2)]
    return order


def output_steps():
    return [("o2", 0), ("o2", 1), ("pr", 0), ("o2", 2), ("pr", 1), ("o2", 3), ("pr", 2), ("pr", 3)]


def output_jobs(s):
    jobs = [("oT", s, t) for t in range(QT)] + [(k, s, t) for k, t in output_steps()]
    return [("ctxT",), *jobs, ("ctxkv",)] if s == 1 else jobs


CROSS = [("x", 0), ("x", 1), ("j", 0), ("p", 0), ("x", 2), ("p", 1), ("x", 3), ("c", 0), ("k", 0), ("p", 2), ("c", 1), ("m", 0),
         ("p", 3), ("c", 2), ("m", 1), ("a", 0), ("c", 3), ("m", 2), ("a", 1), ("m", 3), ("a", 2), ("a", 3)]


def cross_jobs():
    jobs = {"j": lambda t: [("ctxkc",)], "k": lambda t: [("ctxkA",)], "x": lambda t: [("xT", 2, t)], "p": lambda t: [("q2", t)], "c": lambda t: [("c2", t)],
            "m": lambda t: [("mx2", t, k) for k in range(2)], "a": lambda t: [("qA2", t, k) for k in range(2)]}
    return [key for k, t in CROSS for key in jobs[k](t)]


def max_jobs(g):
    n = []
    for t in range(QT):
        per = max(1, 4 // (t + 1)) if t < 2 else 1
        n += [(t, h, per) for h in range(0, 4, per)]
    return [("mx", g, t, h, per) for t, h, per in n]


EXPJOBS = [[(0, 0)], [(1, 0), (3, 3 * P)], [(2, 0)]]
EXPCOLS = [4 * P, 4 * P, 2 * P]
PBASE = [0, 4 * P, 8 * P]
KTCOL = {0: 0, 1: 4 * P, 3: 7 * P, 2: 8 * P}
PCOLS = 10 * P
KTORDER = [0, 1, 3, 2]


def build_decoder(nc, x, ctx_in, weights, biases, experts_w, rows, table, out):
    with ExitStack() as stack:
        memory = {"next": -(-nc.sbuf_base // 32) * 32}
        offset = {}

        def sb(name, shape, dt=F32, over=None, skip=0):
            size = int(np.prod(shape[1:])) * (2 if dt == BF16 else 4)
            if over is None:
                offset[name] = memory["next"]
                memory["next"] += -(-size // 32) * 32
            else:
                offset[name] = offset[over] + skip
            return nc.alloc_sbuf_tensor_at(name, shape, dt, offset=offset[name])

        def sem(name):
            return stack.enter_context(nc.semaphore(name))

        wcols = sum(c * n for c, n in WCOLS.values())
        w_hl = sb("w_hl", [P, 2, wcols], F32R)
        bias = sb("bias", [P, sum(BCOLS.values())])
        x1 = sb("x1", [P, QT, H])
        sufs = sb("sufs", [P, QT, VROW])
        xn = sb("xn", [P, 2, H])
        xt = sb("xt", [P, 2, HC, S], F32R)
        qk = sb("qk", [P, 2 * H])
        qa = sb("qa", [P, QT, HEADS, 64], F32R)
        ka = sb("ka", [P, HEADS, 64], F32R)
        qat = sb("qat", [P, PAIRS, S], F32R)
        kat = sb("kat", [P, PAIRS, S], F32R)
        maxr = sb("maxr", [P, 8, S], F32R)
        probs = sb("probs", [P, 4 * PCOLS])
        vb = sb("vb", [P, QT, VROW + 16])
        ctxr = sb("ctxr", [SC, H])
        ctxt = sb("ctxt", [P, 2, HC, 2, SC], F32R)
        kxt = sb("kxt", [P, PAIRS, P], F32R)
        kxc = sb("kxc", [P, 2, 8, SC], F32R)
        kcx = sb("kcx", [P, 2, SC])
        vx = sb("vx", [P, PAIRS, 2, 32])
        stats = sb("stats", [P, QT, 6])
        mv = sb("mv", [P, QT, 2])
        nrm = sb("nrm", [P, 6, QT])
        nmax = sb("nmax", [P, QT, HEADS])
        emi = sb("emi", [P, QT, HEADS])
        em = sb("em", [P, QT, HEADS])
        num = sb("num", [P, VROW])
        rec = sb("rec", [P, HEADS])
        ohl = sb("ohl", [P, 2, 2, HC, P], F32R)
        score = sb("score", [P, 4, QT])
        best = sb("best", [P, QT, EXPERTS])
        ranks = sb("ranks", [P, QT, EXPERTS])
        reached = sb("reached", [P, QT, OVER])
        route = sb("route", [P, 5, QT])
        count = sb("count", [P, EXPERTS])
        slot_i = sb("slot_i", [P, QT], I32)
        ident = sb("ident", [P, P])
        ident_b = sb("ident_b", [P, P], BF16)
        later_b = sb("later_b", [P, P], BF16)
        later = sb("later", [P, P])
        ones = sb("ones", [P, P])
        ones_b = sb("ones_b", [P, P], BF16)
        below_b = sb("below_b", [P, P], BF16)
        head_mask = sb("head_mask", [P, 8])
        zero_floor = sb("zero_floor", [P, QT, 4])
        upto = sb("upto", [P, EXPERTS, EXPERTS], BF16)
        onehot = sb("onehot", [P, QT, EXPERTS], BF16)
        desc = sb("desc", [P, EXPERTS])
        steps128 = sb("steps128", [P, OVER])
        ovn = sb("ovn", [P, OVER])
        tokens = sb("tokens", [P, QT], I32)
        nobody = sb("nobody", [P, COLUMNS], I32, over="probs")

        cka = ka[0:SC, :, :]
        x2 = sb("x2", [P, QT, H], over="sufs")
        qk_b = sb("qk_b", [P, 2 * H], over="probs", skip=4 * QT * H)
        ckv = sb("ckv", [P, 2 * H], over="probs", skip=4 * (QT * H + 2 * H))
        self_qk = [qk, qk_b]
        cross_q = [qk[:, 0:H], qk[:, H:2 * H], qk_b[:, 0:H], qk_b[:, H:2 * H]]
        qct = maxr[:, 0:2, :]
        kct = maxr[:, 2:4, :]
        km = maxr[:, 4:8, :]
        th = sb("th", [P, 2, S], over="maxr")
        gated = sb("gated", [P, S], over="maxr", skip=4 * 2 * S)
        hid = sb("hid", [P, 2, S], over="maxr", skip=4 * 4 * S)
        lgs = sb("lgs", [P, S], over="maxr", skip=4 * 6 * S)
        vsum = sb("vsum", [P, 2, VROW], over="xt")
        ots = sb("ots", [P, GROUPS, S], over="xt")
        hhl = sb("hhl", [P, 2, IC, S], F32R, over="probs")
        row = sb("row", [P, QT, 2 * H], over="kat")
        raw = sb("raw", [P, PAIRS * S], over="qat")
        raw2 = sb("raw2", [P, PAIRS * S], over="kat")
        w, at = {}, 0
        wraw = {}
        for name, (c, n) in WCOLS.items():
            w[name] = w_hl[:, :, at:at + c * n].rearrange("p a (c n) -> p a c n", c=c)
            w[name + "_flat"] = (at, c * n)
            at += c * n
        bs, bat = {}, 0
        for name, n in BCOLS.items():
            bs[name] = bias[:, bat:bat + n]
            bat += n
        room = {0: 0, 1: 0}
        for name in ("qkv", "gu", "o", "xq", "xkv", "xo", "dn", "gate"):
            c, n = WCOLS[name]
            k = 0 if room[0] + c * n <= PAIRS * S else 1
            wraw[name] = (raw, raw2)[k][:, room[k]:room[k] + c * n]
            room[k] += c * n
        assert max(room.values()) <= PAIRS * S

        def weight_parts(name):
            c, n = WCOLS[name]
            raw_ = wraw[name].rearrange("p (c n) -> p c n", c=c)
            return [(raw_[:, :, lo:hi], (w[name][:, 0, :, lo:hi], w[name][:, 1, :, lo:hi]), scale)
                    for lo, hi, scale in WPARTS.get(name, ((0, n, 1.0),))]

        o_all = sb("o_all", [P, QT, H], over="probs")
        ring = sb("ring", [P, RING, 3 * HC * INNER], over="w_hl")
        tabs = sb("tabs", [P, EXPERTS], I32)
        ctl_i = sb("ctl_i", [1, 1 + 2 * TILES], I32)
        big = sb("big", [P, QT * HEADS * 64], over="qa")
        idx = sb("idx", [P, 2], I32)
        gath = sb("gath", [P, DEPTH, 2 * H], over="qat")
        outr = sb("outr", [P, RING, H], over="kat", skip=4 * 2560)
        xe = sb("xe", [P, 2, H], over="kat")
        the = sb("the", [P, INNER], over="kat", skip=4 * 512)
        ge = sb("ge", [P, INNER], over="kat", skip=4 * 1024)
        he = sb("he", [P, 2, INNER], over="kat", skip=4 * 1536)

        place = {}
        at = 0
        for name, shape in {"e15": (EXPERTS, OVER), "cum": (EXPERTS, EXPERTS), "nov": (EXPERTS,), "end": (EXPERTS,),
                            "o15": (OVER, EXPERTS), "n15": (OVER, EXPERTS), "oe": (OVER,), "on": (OVER,),
                            "oc": (OVER,)}.items():
            n = shape[0] * (shape[1] if len(shape) > 1 else 1)
            v = big[:, at:at + n]
            place[name] = v if len(shape) == 1 else v.rearrange("p (a b) -> p a b", a=shape[0])
            at += n
        assert at <= QT * HEADS * 64

        def bank(name):
            tile = stack.enter_context(nc.psum_tensor(name, [P, 512], F32))
            return Bank(tile, sem(name + "_ready"), sem(name + "_done"))

        misc = [bank(f"misc{i}") for i in range(2)]
        smax = [bank(f"smax{i}") for i in range(2)]
        sexp = [bank(f"sexp{i}") for i in range(3)]
        pv = bank("pv")

        BANK = {}

        def put(banks, keys):
            for i, key in enumerate(keys):
                k = banks[i % len(banks)]
                BANK[key] = k
                k.order[key] = len(k.order)

        every = [*misc, *smax, *sexp]
        put([*sexp, *misc], projection_jobs())
        put(smax, [j for g in range(GROUPS) for j in max_jobs(g)])
        put(sexp, [("sc", g, j, h) for g in range(GROUPS) for j in range(3) for h in range(4)])
        put(misc, [("suf", 1), ("suf", 0)] + [("qA", g, k) for g in range(GROUPS) for k in range(2)])
        put([pv], [("pv", g) for g in range(GROUPS)])
        put(every, output_jobs(1) + cross_jobs())
        put([*smax, *sexp], [("sc2", p) for p in range(PAIRS)])
        put(misc, [("pv2", g) for g in range(GROUPS)])
        put(every, output_jobs(2) + [("xT", 3, t) for t in range(QT)])
        put(every, [("lg",)])
        put(smax, [("gate", c) for c in range(IC)])
        put(sexp, [("up", c) for c in range(IC)])
        put(misc, [("lgT",), ("rank",)])
        put([*misc, *sexp[1:]], [("dn", t) for t in range(QT)])

        in_bias = sem("in_bias")
        bias_scaled = sem("bias_scaled")
        in_w = {n: sem("in_w_" + n) for n in WORDER}
        in_x = sem("in_x")
        in_ctx = sem("in_ctx")
        consts_made = sem("consts_made")
        vconsts_made = sem("vconsts_made")
        w_high = sem("w_high")
        w_low = sem("w_low")
        gu_low = sem("gu_low")
        normed = sem("normed")
        xt_high = sem("xt_high")
        stats_made = sem("stats_made")
        dve_step = sem("dve_step")
        ctx_high = sem("ctx_high")
        ctxv_put = sem("ctxv_put")
        cka_high = sem("cka_high")
        cka_low = sem("cka_low")
        k_high = sem("k_high")
        k_low = sem("k_low")
        q_high = sem("q_high")
        q_low = sem("q_low")
        km0_made = sem("km0_made")
        km_made = sem("km_made")
        vsum_made = sem("vsum_made")
        kxc_made = sem("kxc_made")
        sufs_made = sem("sufs_made")
        shift_put = sem("shift_put")
        emi_made = sem("emi_made")
        em_made = sem("em_made")
        masked = sem("masked")
        pv_read = sem("pv_read")
        xb_made = sem("xb_made")
        o_made = sem("o_made")
        o_high = sem("o_high")
        tanh_made = sem("tanh_made")
        hid_high = sem("hid_high")
        hid_low = sem("hid_low")
        btanh_made = sem("btanh_made")
        row_made = sem("row_made")
        row_out = sem("row_out")
        table_set = sem("table_set")
        oh_made = sem("oh_made")
        slots_made = sem("slots_made")
        slots_used = sem("slots_used")
        zeroed = sem("zeroed")
        ctl_made = sem("ctl_made")
        over_in = [sem(f"over_in{k}") for k in range(2)]
        over_out = [sem(f"over_out{k}") for k in range(2)]
        table_put = sem("table_put")
        table_in = sem("table_in")
        in_e = [sem(f"in_e{u}") for u in range(RING)]
        gathered = [sem(f"gathered{u}") for u in range(DEPTH)]
        e_t = sem("e_t")
        e_x = sem("e_x")
        e_g = sem("e_g")
        e_u = sem("e_u")
        e_th = sem("e_th")
        e_gd = sem("e_gd")
        e_h = sem("e_h")
        e_y = sem("e_y")
        e_o = sem("e_o")
        scattered = [sem(f"scattered{u}") for u in range(RING)]

        gate_bank, up_bank = (smax[0], sexp[2]), (smax[1], pv)

        passed = sem("passed")
        block = stack.enter_context(nc.Block())

        @block.sync
        def _(sp):
            for k in (*misc, *smax, *sexp, pv):
                sp.sem_inc(k.done, 1)
            sp.sem_inc(row_out, 16)
            for k in (e_gd, e_h, e_h, slots_used, *over_out):
                sp.sem_inc(k, 1)
            for n, name in enumerate(WORDER):
                sp.dma_start(wraw[name].rearrange("p (c n) -> p c n", c=WCOLS[name][0]),
                             weights[name].rearrange("(c p) n -> p c n", p=P)).then_inc(in_w[name], 16)
                if n == 1:
                    for bname in BCOLS:
                        sp.dma_start(bs[bname], biases[bname].partition_broadcast(P)).then_inc(in_bias, 16)
            sp.wait_ge(vconsts_made, VCONSTS)
            sp.dma_start(table, nobody[:, :]).then_inc(table_set, 16)
            with sp.Fori(0, B) as b:
                for t in range(QT):
                    key = ("dn", t)
                    sp.wait_ge(row_made, b * QT + t + 1)
                    sp.sem_inc(passed, 1)
                    sp.wait_ge(BANK[key].done, BANK[key].emptied(key, b))
                    sp.sem_inc(passed, 1)
                    sp.dma_start(rows.rearrange("(b t p) h -> b t p h", b=B, p=P)[b, t], row[:, t, :])\
                        .then_inc(row_out, 16)
            sp.wait_ge(table_put, 16 * TILES)
            sp.dma_start(tabs[:, :], table[:, 0:EXPERTS]).then_inc(table_in, 16)
            for key in (("dn", QT - 1), ("dn", QT - 2)):
                k = BANK[key]
                sp.wait_ge(k.ready, k.filled(key, B - 1))
            for u in range(1, RING):
                sp.wait_ge(gathered[u], 16)
                sp.dma_start(ring[:, u, :], experts_w[u]).then_inc(in_e[u], 16)
            with sp.Fori(1, EXPERTS // RING) as i:
                for u in range(RING):
                    sp.wait_ge(e_y, i * RING + (u + 1 - RING))
                    sp.sem_inc(passed, 1)
                    sp.dma_start(ring[:, u, :], experts_w[i * RING + u]).then_inc(in_e[u], 16)
            sp.wait_ge(ctl_made, 1)
            n_over = sp.value_load(ctl_i[0:1, 0:1], min_val=0, max_val=OVER)
            with sp.Fori(0, -(-OVER // 2)) as i:
                with sp.If(i * 2 < n_over):
                    for k in range(2):
                        with sp.If(i * 2 + 1 < n_over) if k else nullcontext():
                            column = sp.value_load(ctl_i[0:1, bass.ds(i * 2 + (1 + TILES + k), 1)], min_val=0, max_val=COLUMNS - 1)
                            sp.wait_ge(over_out[k], i + 1)
                            sp.sem_inc(passed, 1)
                            sp.dma_start(idx[:, k:k + 1], table[:, bass.ds(column, 1)], allow_slow_non_contiguous=True)\
                                .then_inc(over_in[k], 16)
                    for k in range(2):
                        with sp.If(i * 2 + 1 < n_over) if k else nullcontext():
                            e = sp.value_load(ctl_i[0:1, bass.ds(i * 2 + (1 + k), 1)], min_val=0, max_val=EXPERTS - 1)
                            sp.wait_ge(e_y, i * 2 + (EXPERTS - 1 + k))
                            sp.sem_inc(passed, 1)
                            sp.dma_start(ring[:, k, :], experts_w[e]).then_inc(in_e[k], 16)

        @block.gpsimd
        def _(pool):
            pool.memset(ones[:, :], 1.0).then_inc(consts_made, 1)
            pool.memset(ident[:, :], 0.0).then_inc(consts_made, 1)
            pool.memset(zero_floor[:, :, :], 0.0).then_inc(consts_made, 1)
            pool.memset(later_b[:, :], 0.0).then_inc(consts_made, 1)
            pool.memset(upto[:, :, :], 1.0).then_inc(consts_made, 1)
            pool.wait_ge(consts_made, 5)
            pool.affine_select(out=ident[:, :], in_=ident[:, :], compare_op=ALU.not_equal, fill=1.0, base=0,
                               pattern=[[-1, P]], channel_multiplier=1).then_inc(consts_made, 1)
            pool.affine_select(out=later[:, :], in_=ones[:, :], compare_op=ALU.is_ge, fill=0.0, base=-32,
                               pattern=[[-32, 4], [0, 32]], channel_multiplier=1).then_inc(consts_made, 1)
            pool.affine_select(out=later_b[:, :], in_=later_b[:, :], compare_op=ALU.is_ge, fill=-BIG, base=0,
                               pattern=[[-32, 4], [0, 32]], channel_multiplier=1).then_inc(consts_made, 1)
            pool.affine_select(out=zero_floor[:, QT - 1, :], in_=zero_floor[:, QT - 1, :], compare_op=ALU.is_ge,
                               fill=BIG, base=95, pattern=[[0, 4]], channel_multiplier=-1).then_inc(consts_made, 1)
            pool.affine_select(out=head_mask[:, :], in_=ones[:, 0:8], compare_op=ALU.is_ge, fill=0.0, base=0,
                               pattern=[[-D, 8]], channel_multiplier=1).then_inc(consts_made, 1)
            pool.affine_select(out=below_b[:, :], in_=ones[:, :], compare_op=ALU.is_ge, fill=0.0, base=-1,
                               pattern=[[1, P]], channel_multiplier=-1).then_inc(consts_made, 1)
            pool.iota(tokens[:, :], pattern=[[P, QT]], base=-S, channel_multiplier=1).then_inc(consts_made, 1)
            pool.affine_select(out=upto[:, :, :], in_=upto[:, :, :], compare_op=ALU.is_ge, fill=0.0, base=0,
                               pattern=[[1, EXPERTS], [-1, EXPERTS]], channel_multiplier=0).then_inc(consts_made, 1)
            for v, first, step_ in ((desc, EXPERTS, -1), (steps128, P, P), (ovn, 0, 1)):
                pool.iota(v[:, :], pattern=[[step_, v.shape[1]]], base=first, channel_multiplier=0,
                          allow_small_or_imprecise_dtypes=True).then_inc(consts_made, 1)
            pool.wait_ge(consts_made, CONSTS - 2)
            pool.affine_select(out=head_mask[:, :], in_=head_mask[:, :], compare_op=ALU.is_ge, fill=0.0, base=D - 1,
                               pattern=[[D, 8]], channel_multiplier=-1).then_inc(consts_made, 1)
            pool.memset(qa[:, :, :, :].bitcast(F32), 0.0).then_inc(consts_made, 1)
            for name in GPSIMD_SPLITS:
                at, cols = w[name + "_flat"]
                pool.wait_ge(w_high, WORDER.index(name) + 1)
                pool.tensor_tensor(w_hl[:, 1, at:at + cols], wraw[name],
                                   w_hl[:, 0, at:at + cols].bitcast(F32), ALU.subtract).then_inc(gu_low, 1)
            pool.wait_ge(in_bias, 16 * len(BCOLS))
            zero = pool.to_reg(0.0)
            pool.wait_ge(table_set, 16)
            with pool.Fori(0, B) as b:
                def qa_low(t, n, q):
                    pool.wait_ge(q_high, b * 2 * QT + n + 1)
                    pool.sem_inc(passed, 1)
                    pool.tensor_tensor(qa[:, t, :, 2 * D:3 * D], q.rearrange("p (h d) -> p h d", d=D),
                                       qa[:, t, :, 0:D].bitcast(F32), ALU.subtract).then_inc(q_low, 1)

                def ka_low(t):
                    pool.wait_ge(k_high, b * QT + t + 1)
                    k = BANK["qk", t]
                    pool.wait_ge(k.done, k.emptied(("qk", t), b))
                    pool.tensor_tensor(ka[:, :, D:2 * D], self_qk[t % 2][:, H:2 * H].rearrange("p (h d) -> p h d", d=D),
                                       ka[:, :, 0:D].bitcast(F32), ALU.subtract).then_inc(k_low, 1)

                for t in range(QT + 1):
                    if t < QT:
                        ka_low(t)
                    if t > 0:
                        k = BANK["c", t - 1]
                        pool.wait_ge(k.done, k.emptied(("c", t - 1), b))
                        pool.sem_inc(passed, 1)
                        cols = slice((t - 1) * P, t * P)
                        pool.tensor_tensor(km[:, :, cols], kct[:, 0, cols].bitcast(F32).unsqueeze(1).broadcast_to([P, 4, P]),
                                           head_mask[:, 0:4].unsqueeze(2).broadcast_to([P, 4, P]), ALU.mult)\
                            .then_inc(km0_made, 1)
                    if t < QT:
                        qa_low(t, t, self_qk[t % 2][:, 0:H])
                for n, other in ((1, vb[:, 3, 0:VROW]), (0, vsum[:, 1, :])):
                    if n == 1:
                        for t in range(1, QT):
                            k = BANK["v", t]
                            pool.wait_ge(k.done, k.emptied(("v", t), b))
                            pool.sem_inc(passed, 1)
                    else:
                        pool.wait_ge(vsum_made, b * 2 + 1)
                    pool.tensor_tensor(vsum[:, n, :], vb[:, n + 1, 0:VROW], other, ALU.add).then_inc(vsum_made, 1)

                for g in range(GROUPS):
                    for n, kt in enumerate(KTORDER):
                        job = [0, 1, 1, 2][n]
                        for h in range(1, 4):
                            key = ("sc", g, job, h)
                            pool.wait_ge(BANK[key].done, BANK[key].emptied(key, b))
                            pool.sem_inc(passed, 1)
                        v = probs.rearrange("p (h n) -> p h n", h=4)[:, :, KTCOL[kt]:KTCOL[kt] + P]
                        pool.affine_select(out=v, in_=v, compare_op=ALU.is_ge, fill=zero, base=31,
                                           pattern=[[0, 4], [32, 4], [0, 32]], channel_multiplier=-1)\
                            .then_inc(masked, 1)
                pool.wait_ge(normed, b * 3 * QT + QT)
                for t in range(QT):
                    pool.tensor_tensor(x1[:, t, :], x1[:, t, :], bs["o"], ALU.add).then_inc(xb_made, 1)
                for t in range(QT):
                    key = ("pr", 1, t)
                    pool.wait_ge(BANK[key].done, BANK[key].emptied(key, b))
                    pool.tensor_tensor(x2[:, t, :], x1[:, t, :], bs["xo"], ALU.add).then_inc(xb_made, 1)
                k = BANK["ctxkc",]
                pool.wait_ge(k.done, k.emptied(("ctxkc",), b))
                pool.sem_inc(passed, 1)
                for k in range(2):
                    pool.tensor_tensor(kxc[:, k, :, :], kcx[:, k, :].unsqueeze(1).broadcast_to([P, 8, SC]),
                                       head_mask[:, :].unsqueeze(2).broadcast_to([P, 8, SC]), ALU.mult).then_inc(kxc_made, 1)
                pool.wait_ge(cka_high, b + 1)
                pool.sem_inc(passed, 1)
                pool.tensor_tensor(cka[:, :, D:2 * D], ckv[0:SC, 0:H].rearrange("p (h d) -> p h d", d=D),
                                   cka[:, :, 0:D].bitcast(F32), ALU.subtract).then_inc(cka_low, 1)
                for t in range(QT):
                    qa_low(t, QT + t, cross_q[t])
                for c in range(IC):
                    pool.wait_ge(hid_high, b * IC + c + 1)
                    pool.tensor_tensor(hhl[:, 1, c, :], hid[:, c % 2, :], hhl[:, 0, c, :].bitcast(F32),
                                       ALU.subtract).then_inc(hid_low, 1)
                pool.wait_ge(slots_made, b + 1)
                pool.sem_inc(passed, 1)
                for t in range(QT):
                    pool.indirect_dma_start(out=table.rearrange("p (s o) -> (p s) o", o=1),
                                            out_offset=bass.IndirectOffsetOnAxis(ap=slot_i[:, t:t + 1].bitcast(U32), axis=0),
                                            in_=tokens[:, t:t + 1], in_offset=None).then_inc(table_put, 16)
                pool.wait_ge(table_put, b * 16 * QT + 16 * QT)
                pool.sem_inc(slots_used, 1)
            pool.wait_ge(zeroed, 1)
            pool.wait_ge(row_out, 16 * TILES + 16)

            def gather(index, u):
                pool.indirect_dma_start(out=gath[:, u, :], out_offset=None, in_=rows,
                                        in_offset=bass.IndirectOffsetOnAxis(ap=index.bitcast(U32), axis=0),
                                        bounds_check=TILES * P - 1, oob_is_err=False).then_inc(gathered[u], 16)

            def scatter(index, u):
                pool.indirect_dma_start(out=out, in_=outr[:, u, :], in_offset=None,
                                        out_offset=bass.IndirectOffsetOnAxis(ap=index.bitcast(U32), axis=0),
                                        bounds_check=TILES * P - 1, oob_is_err=False).then_inc(scattered[u], 16)

            pool.wait_ge(table_in, 16)
            for t in range(DEPTH):
                gather(tabs[:, t:t + 1], t)
            for t in range(EXPERTS):
                pool.wait_ge(e_o, t + 1)
                if t + DEPTH < EXPERTS:
                    gather(tabs[:, t + DEPTH:t + DEPTH + 1], t % DEPTH)
                scatter(tabs[:, t:t + 1], t % RING)
                if t == EXPERTS - 3:
                    pool.wait_ge(ctl_made, 1)
                    n_over = pool.value_load(ctl_i[0:1, 0:1], min_val=0, max_val=OVER)
                    for k in range(2):
                        with pool.If(n_over > k):
                            pool.wait_ge(over_in[k], 16)
                            gather(idx[:, k:k + 1], k)
            for u in range(RING):
                pool.wait_ge(scattered[u], 16 * EXPERTS // RING)
            with pool.Fori(0, -(-OVER // 2)) as i:
                with pool.If(i * 2 < n_over):
                    for k in range(2):
                        with pool.If(i * 2 + 1 < n_over) if k else nullcontext():
                            pool.wait_ge(e_o, i * 2 + (EXPERTS + 1 + k))
                            pool.sem_inc(passed, 1)
                            scatter(idx[:, k:k + 1], k)
                            pool.wait_ge(scattered[k], i * 16 + (16 * EXPERTS // RING + 16))
                            pool.sem_inc(over_out[k], 1)
                    for k in range(2):
                        with pool.If(i * 2 + (2 + k) < n_over):
                            pool.wait_ge(over_in[k], i * 16 + 32)
                            pool.sem_inc(passed, 1)
                            gather(idx[:, k:k + 1], k)

        @block.scalar
        def _(act):
            def load_batch(b):
                act.dma_start(x1[:, :, :], x.rearrange("(b t p) h -> b p t h", b=B, p=P)[b]).then_inc(in_x, 16)
                act.dma_start(ctxr[:, :], ctx_in.rearrange("(b s) h -> b s h", b=B)[b]).then_inc(in_ctx, 16)

            load_batch(0)
            for name in WORDER:
                at, cols = w[name + "_flat"]
                act.wait_ge(in_w[name], 16)
                for raw_, (high, _), scale in weight_parts(name):
                    ins = act.activation(high, raw_, ACT.Copy, scale=scale)
                ins.then_inc(w_high, 1)
            act.wait_ge(consts_made, CONSTS)
            with act.Fori(0, B) as b:
                def filled(key):
                    act.wait_ge(BANK[key].ready, BANK[key].filled(key, b))
                    return BANK[key].tile

                def xt_part(s, t):
                    ps = filled(("xT", s, t))
                    act.activation(xt[:, 0, :, t * P:(t + 1) * P], ps[:, 0:H].rearrange("p (c n) -> p c n", c=HC),
                                   ACT.Copy).then_inc(xt_high, 1)

                def qa_high(t, key, q):
                    act.wait_ge(BANK[key].done, BANK[key].emptied(key, b))
                    act.activation(qa[:, t, :, 0:2 * D].rearrange("p h (a d) -> p h a d", a=2),
                                   q.rearrange("p (h d) -> p h d", d=D).unsqueeze(2)
                                   .broadcast_to([P, HEADS, 2, D]), ACT.Copy).then_inc(q_high, 1)

                xt_part(1, 0)
                xt_part(1, 1)

                def ka_high(t):
                    key = ("qk", t)
                    act.wait_ge(BANK[key].done, BANK[key].emptied(key, b))
                    if t > 0:
                        key = ("kA", t - 1, 1)
                        act.wait_ge(BANK[key].ready, BANK[key].filled(key, b))
                    else:
                        act.wait_ge(BANK["ctxkA",].done, BANK["ctxkA",].cleared(b))
                        act.wait_ge(row_out, b * 16 * QT + 16)
                    act.activation(ka[:, :, :].rearrange("p h (a d) -> p h a d", a=4)[:, :, 0:4:2, :],
                                   self_qk[t % 2][:, H:2 * H].rearrange("p (h d) -> p h d", d=D).unsqueeze(2)
                                   .broadcast_to([P, HEADS, 2, D]), ACT.Copy).then_inc(k_high, 1)

                def put_keys(t):
                    key = ("kA", t, 0)
                    ps = filled(key)
                    act.activation(kat[:, 0:4, t * P:(t + 1) * P], ps[:, :].rearrange("p (q n) -> p q n", q=4),
                                   ACT.Copy).then_inc(BANK[key].done, 1)
                    key = ("c", t)
                    ps = filled(key)
                    act.activation(maxr[:, 0:4, t * P:(t + 1) * P], ps[:, :].rearrange("p (q n) -> p q n", q=4),
                                   ACT.Copy).then_inc(BANK[key].done, 1)

                ka_high(0)
                qa_high(0, ("qk", 0), self_qk[0][:, 0:H])
                qa_high(1, ("qk", 1), self_qk[1][:, 0:H])
                xt_part(1, 2)
                xt_part(1, 3)
                for t in range(QT):
                    if t == QT - 1:
                        for j in (QT - 1, QT - 2):
                            key = ("suf", j)
                            ps = filled(key)
                            act.activation(sufs[:, j, :], ps[:, 0:VROW], ACT.Copy).then_inc(BANK[key].done, 1)
                    put_keys(t)
                    if t + 1 < QT:
                        ka_high(t + 1)
                    if t + 2 < QT:
                        qa_high(t + 2, ("qk", t + 2), self_qk[t % 2][:, 0:H])

                def mask_keys(g):
                    for j in max_jobs(g - 1)[-2:]:
                        act.wait_ge(BANK[j].ready, BANK[j].filled(j, b))
                    for i in range(2):
                        h = 4 * g + i
                        ins = act.activation(km[:, i, :], kct[:, h // 8, :].bitcast(F32), ACT.Copy,
                                             scale=head_mask[:, h % 8:h % 8 + 1])
                    ins.then_inc(km_made, 1)

                for t in (1, 0):
                    key = ("suf", t)
                    ps = filled(key)
                    act.activation(sufs[:, t, :], ps[:, 0:VROW], ACT.Copy).then_inc(BANK[key].done, 1)
                mask_keys(1)
                for g in range(GROUPS):
                    if 0 < g < GROUPS - 1:
                        mask_keys(g + 1)
                    key = ("qA", g, 0)
                    ps = filled(key)
                    act.activation(qat[:, 2 * g, :], ps[:, :], ACT.Copy).then_inc(BANK[key].done, 1)
                    for j in range(3):
                        if g > 0:
                            act.wait_ge(pv_read, b * 4 * GROUPS + 4 * (g - 1) + [1, 3, 4][j])
                        for h in range(4):
                            key = ("sc", g, j, h)
                            ps = filled(key)
                            act.activation(probs[:, h * PCOLS + PBASE[j]:h * PCOLS + PBASE[j] + EXPCOLS[j]],
                                           ps[:, 0:EXPCOLS[j]], ACT.Exp).then_inc(BANK[key].done, 1)
                act.wait_ge(emi_made, b + 1)
                act.activation(em[:, :, :], emi[:, :, :], ACT.Exp).then_inc(em_made, 1)
                ps = filled(("ctxT",))
                for c in range(HC):
                    ins = act.activation(ctxt[:, 0, c, :, :], ps[:, c * SC:(c + 1) * SC].unsqueeze(1)
                                         .broadcast_to([P, 2, SC]), ACT.Copy)
                ins.then_inc(ctx_high, 1)

                def o_part(s, t):
                    if t >= 2:
                        key = ("pr", s, t - 2)
                        act.wait_ge(BANK[key].ready, BANK[key].filled(key, b))
                    key = ("o2", s, t)
                    ps = filled(key)
                    act.activation(ohl[:, t % 2, 0, :, :], ps[:, 0:H].rearrange("p (c n) -> p c n", c=HC), ACT.Copy)\
                        .then_inc(o_high, 1)

                for t in range(QT):
                    o_part(1, t)

                def put_q(t):
                    key = ("c2", t)
                    ps = filled(key)
                    act.activation(qct[:, :, t * P:(t + 1) * P], ps[:, 0:2 * P].rearrange("p (q n) -> p q n", q=2),
                                   ACT.Copy).then_inc(BANK[key].done, 1)

                def put_qat(t):
                    for half in range(2):
                        key = ("qA2", t, half)
                        ps = filled(key)
                        act.activation(qat[:, 4 * half:4 * half + 4, t * P:(t + 1) * P],
                                       ps[:, :].rearrange("p (q n) -> p q n", q=4), ACT.Copy).then_inc(BANK[key].done, 1)

                def put_context():
                    k = BANK["ctxkv",]
                    act.wait_ge(k.done, k.emptied(("ctxkv",), b))
                    act.activation(cka[:, :, :].rearrange("p h (a d) -> p h a d", a=4)[:, :, 0:4:2, :],
                                   ckv[0:SC, 0:H].rearrange("p (h d) -> p h d", d=D).unsqueeze(2)
                                   .broadcast_to([SC, HEADS, 2, D]), ACT.Copy).then_inc(cka_high, 1)
                    for a in range(2):
                        ins = act.activation(vx[64 * a:64 * a + 64, :, a, 0:D],
                                             ckv[64 * a:64 * a + 64, H:2 * H].rearrange("p (q a d) -> p q a d", a=2, d=D)[:, :, a, :],
                                             ACT.Copy)
                        ins.then_inc(ctxv_put, 1)

                for k, t in CROSS:
                    if k == "x":
                        xt_part(2, t)
                    elif k == "p":
                        qa_high(t, ("q2", t), cross_q[t])
                    elif k == "c":
                        put_q(t)
                    elif k == "a":
                        put_qat(t)
                    elif k == "j":
                        key = ("ctxkc",)
                        ps = filled(key)
                        act.activation(kcx[:, :, :], ps[:, 0:2 * SC].rearrange("p (k n) -> p k n", k=2), ACT.Copy)\
                            .then_inc(BANK[key].done, 1)
                        put_context()
                for p in range(PAIRS):
                    key = ("sc2", p)
                    ps = filled(key)
                    act.activation(probs[:, p * S:(p + 1) * S], ps[:, :], ACT.Exp).then_inc(BANK[key].done, 1)
                for t in range(QT):
                    o_part(2, t)
                for t in range(QT):
                    xt_part(3, t)
                with act.If(b < B - 1):
                    load_batch(nc.s_assert_within(b + 1, 1, B - 1, skip_runtime_bounds_check_because="b < B - 1 here"))
                with act.If(b > B - 2):
                    key = ("pr", 2, QT - 1)
                    act.wait_ge(BANK[key].ready, BANK[key].filled(key, b))
                    act.sem_inc(passed, 1)
                    act.dma_start(ring[:, 0, :], experts_w[0]).then_inc(in_e[0], 16)
                key = ("lg",)
                ps = filled(key)
                act.activation(lgs[:, :], ps[:, :], ACT.Copy).then_inc(BANK[key].done, 1)
                for c in range(IC):
                    ps = filled(("gate", c))
                    if c >= 2:
                        act.wait_ge(BANK["gate", c - 2].done, BANK["gate", c - 2].emptied(("gate", c - 2), b))
                    act.activation(th[:, c % 2, :], ps[:, :], ACT.Tanh, scale=0.5).then_inc(tanh_made, 1)
                    if c > 0:
                        act.wait_ge(BANK["up", c - 1].done, BANK["up", c - 1].emptied(("up", c - 1), b))
                        act.activation(hhl[:, 0, c - 1, :], hid[:, (c - 1) % 2, :], ACT.Copy).then_inc(hid_high, 1)
                    if c == 0:
                        key = ("lgT",)
                        act.wait_ge(BANK[key].done, BANK[key].emptied(key, b))
                        act.activation(score[:, 1, :], score[:, 0, :], ACT.Tanh, scale=0.5).then_inc(btanh_made, 1)
                act.wait_ge(BANK["up", IC - 1].done, BANK["up", IC - 1].emptied(("up", IC - 1), b))
                act.activation(hhl[:, 0, IC - 1, :], hid[:, (IC - 1) % 2, :], ACT.Copy).then_inc(hid_high, 1)

            def tanh_e(k, n):
                act.wait_ge(e_g, n)
                act.activation(the[:, :], gate_bank[k].tile[:, :], ACT.Tanh, scale=0.5).then_inc(e_th, 1)

            with act.Fori(0, EXPERTS // 2) as i:
                for k in range(2):
                    act.wait_ge(e_gd, i * 2 + (k + 1))
                    tanh_e(k, i * 2 + (k + 1))
            act.wait_ge(ctl_made, 1)
            n_over = act.value_load(ctl_i[0:1, 0:1], min_val=0, max_val=OVER)
            with act.Fori(0, -(-OVER // 2)) as i:
                with act.If(i * 2 < n_over):
                    for k in range(2):
                        with act.If(i * 2 + 1 < n_over) if k else nullcontext():
                            act.wait_ge(e_gd, i * 2 + (EXPERTS + 1 + k))
                            tanh_e(k, i * 2 + (EXPERTS + 1 + k))

        @block.vector
        def _(dve):
            dve.memset(ka[:, :, :].bitcast(F32), 0.0).then_inc(vconsts_made, 1)
            dve.memset(kxt[:, :, :].bitcast(F32), 0.0).then_inc(vconsts_made, 1)
            dve.memset(vx[:, :, :, :], 0.0).then_inc(vconsts_made, 1)
            dve.memset(vb[:, :, :], 0.0).then_inc(vconsts_made, 1)
            dve.wait_ge(vconsts_made, 4)
            dve.memset(ka[:, :, 48:49].bitcast(F32), 1.0).then_inc(vconsts_made, 1)
            for a in range(2):
                dve.memset(vx[64 * a:64 * a + 64, :, a, D:D + 1], 1.0).then_inc(vconsts_made, 1)
            for t in range(QT):
                dve.memset(vb[:, t, 0:VROW].rearrange("p (h d) -> p h d", d=WIDTH)[:, :, D:D + 1], 1.0)\
                    .then_inc(vconsts_made, 1)
            dve.memset(nobody[:, :], NOBODY).then_inc(vconsts_made, 1)
            dve.memset(ones_b[:, :], 1.0).then_inc(vconsts_made, 1)
            dve.memset(count[:, :], 0.0).then_inc(vconsts_made, 1)
            dve.wait_ge(consts_made, CONSTS)
            dve.tensor_copy(ident_b[:, :], ident[:, :]).then_inc(vconsts_made, 1)
            step = [0]

            def link(b, ins):
                step[0] += 1
                ins.then_inc(dve_step, 1)
                dve.wait_ge(dve_step, b * STEPS_PER_BATCH + step[0])

            def statistics(src, t):
                dve.bn_stats(stats[:, t, :], src[:, t, :]).then_inc(stats_made, 1)

            def layernorm(b, made):
                dve.wait_ge(stats_made, made)
                dve.sem_inc(passed, 1)
                for t in range(QT):
                    ins = dve.bn_aggr(mv[:, t, :], stats[:, t, :])
                link(b, ins)
                v, y, i, a, m = (nrm[:, n, :] for n in range(5))
                link(b, dve.tensor_scalar(v, mv[:, :, 1], EPS, None, ALU.add))
                link(b, dve.tensor_scalar(i.bitcast(I32), v.bitcast(I32), 1, None, ALU.logical_shift_right))
                link(b, dve.tensor_scalar(y.bitcast(I32), i.bitcast(I32), -1, RSQRT_MAGIC, ALU.mult, ALU.add))
                f = 3.0 / 8.0
                link(b, dve.tensor_tensor(a, y, y, ALU.mult))
                link(b, dve.tensor_tensor(m, a, v, ALU.mult))
                link(b, dve.scalar_tensor_tensor(out=a, in0=m, scalar=-10.0 / 3.0, in1=m, op0=ALU.add, op1=ALU.mult))
                link(b, dve.scalar_tensor_tensor(out=y, in0=a, scalar=5.0, in1=y, op0=ALU.add, op1=ALU.mult))
                link(b, dve.tensor_tensor(a, y, y, ALU.mult))
                link(b, dve.scalar_tensor_tensor(out=m, in0=a, scalar=-0.5 * f ** 3, in1=v, op0=ALU.mult, op1=ALU.mult))
                link(b, dve.scalar_tensor_tensor(out=y, in0=m, scalar=1.5 * f, in1=y, op0=ALU.add, op1=ALU.mult))

            def scale_rows(src, t):
                dve.tensor_scalar(xn[:, t % 2, :], src[:, t, :], mv[:, t, 0:1], nrm[:, 1, t:t + 1],
                                  ALU.subtract, ALU.mult).then_inc(normed, 1)

            def begin_statistics(rows_in):
                dve.wait_ge(in_x, rows_in)
                dve.sem_inc(passed, 1)
                for t in range(QT):
                    statistics(x1, t)

            def begin_batch(b, made):
                layernorm(b, made)
                scale_rows(x1, 0)
                scale_rows(x1, 1)

            begin_statistics(16)
            begin_batch(0, QT)
            first_steps = step[0]
            for name in WORDER:
                if name not in GPSIMD_SPLITS:
                    at, cols = w[name + "_flat"]
                    dve.wait_ge(w_high, WORDER.index(name) + 1)
                    for raw_, (high, low), scale in weight_parts(name):
                        if scale == 1.0:
                            ins = dve.tensor_tensor(low, raw_, high.bitcast(F32), ALU.subtract)
                        else:
                            ins = dve.scalar_tensor_tensor(out=low, in0=raw_, scalar=scale, in1=high.bitcast(F32),
                                                           op0=ALU.mult, op1=ALU.subtract)
                    ins.then_inc(w_low, 1)
            dve.wait_ge(in_bias, 16 * len(BCOLS))
            for v in (bs["qkv"][:, 0:H], bs["xq"]):
                dve.tensor_scalar(v, v, SCALE, None, ALU.mult).then_inc(bias_scaled, 1)
            dve.wait_ge(bias_scaled, 2)

            dve.wait_ge(table_set, 16)

            with dve.Fori(0, B) as b:
                def filled(key):
                    dve.wait_ge(BANK[key].ready, BANK[key].filled(key, b))
                    return BANK[key].tile

                def normalise(s, src, t):
                    if t >= 2:
                        key = ("xT", s, t - 2)
                        dve.wait_ge(BANK[key].ready, BANK[key].filled(key, b))
                    scale_rows(src, t)

                def xt_part(s, t):
                    key = ("xT", s, t)
                    ps = filled(key)
                    dve.wait_ge(xt_high, b * 3 * QT + (s - 1) * QT + t + 1)
                    dve.tensor_tensor(xt[:, 1, :, t * P:(t + 1) * P], ps[:, 0:H].rearrange("p (c n) -> p c n", c=HC),
                                      xt[:, 0, :, t * P:(t + 1) * P].bitcast(F32), ALU.subtract)\
                        .then_inc(BANK[key].done, 1)

                xt_part(1, 0)
                normalise(1, x1, 2)
                xt_part(1, 1)
                normalise(1, x1, 3)
                def put_projections(t):
                    key = ("qk", t)
                    ps = filled(key)
                    if t >= 2:
                        dve.wait_ge(q_low, b * 2 * QT + t - 1)
                        ck = ("c", t - 2)
                        dve.wait_ge(BANK[ck].ready, BANK[ck].filled(ck, b))
                    dve.tensor_tensor(self_qk[t % 2][:, :], ps[:, :], bs["qkv"][:, 0:2 * H], ALU.add)\
                        .then_inc(BANK[key].done, 1)
                    key = ("v", t)
                    ps = filled(key)
                    dve.tensor_tensor(vb[:, t, 0:VROW].rearrange("p (h d) -> p h d", d=WIDTH)[:, :, 0:D],
                                      ps[:, 0:H].rearrange("p (h d) -> p h d", d=D),
                                      bs["qkv"][:, 2 * H:3 * H].rearrange("p (h d) -> p h d", d=D), ALU.add)\
                        .then_inc(BANK[key].done, 1)

                def maximum(key):
                    _, g, t, h, per = key
                    ps = filled(key)
                    n = (t + 1) * P
                    dve.tensor_reduce(nmax[:, t, 4 * g + h:4 * g + h + per], ps[:, 0:per * n]
                                      .rearrange("p (h n) -> p h n", h=per), AX.X, ALU.max, negate=True)\
                        .then_inc(BANK[key].done, 1)

                put_projections(0)
                put_projections(1)
                xt_part(1, 2)
                xt_part(1, 3)
                for t in range(QT):
                    key = ("kA", t, 1)
                    ps = filled(key)
                    dve.tensor_copy(kat[:, 4:8, t * P:(t + 1) * P], ps[:, :].rearrange("p (q n) -> p q n", q=4))\
                        .then_inc(BANK[key].done, 1)
                    for key in max_jobs(0):
                        if key[2] == t - 1:
                            maximum(key)
                    if t + 2 < QT:
                        put_projections(t + 2)

                def maxima(g):
                    for key in max_jobs(g):
                        if g > 0 or key[2] == QT - 1:
                            maximum(key)
                    dve.wait_ge(BANK[key].done, BANK[key].emptied(key, b))
                    dve.tensor_tensor(qa[:, :, 4 * g:4 * g + 4, 48], nmax[:, :, 4 * g:4 * g + 4],
                                      zero_floor[:, :, :], ALU.min).then_inc(shift_put, 1)

                def mask_keys(g):
                    for i in range(2, 4):
                        h = 4 * g + i
                        ins = dve.tensor_scalar(km[:, i, :], kct[:, h // 8, :].bitcast(F32),
                                                head_mask[:, h % 8:h % 8 + 1], None, ALU.mult)
                    ins.then_inc(km_made, 1)

                def pv_out(key, g):
                    if key[0] == "pv":
                        dve.wait_ge(pv_read, b * 4 * GROUPS + 4 * (g + 1))
                    else:
                        filled(key)
                    dve.tensor_copy(ots[:, g, :], BANK[key].tile[:, :]).then_inc(BANK[key].done, 1)

                def heads(v):
                    return v.rearrange("p (h d) -> p h d", h=HEADS)

                maxima(0)
                for g in range(GROUPS):
                    if g + 1 < GROUPS:
                        mask_keys(g + 1)
                    key = ("qA", g, 1)
                    ps = filled(key)
                    dve.tensor_copy(qat[:, 2 * g + 1, :], ps[:, :]).then_inc(BANK[key].done, 1)
                    if g > 0:
                        pv_out(("pv", g - 1), g - 1)
                    if g + 1 < GROUPS:
                        maxima(g + 1)
                dve.wait_ge(shift_put, b * GROUPS + GROUPS)
                dve.tensor_scalar(emi[:, :, :], qa[:, :, :, 48].bitcast(F32), 0.0, None, ALU.min).then_inc(emi_made, 1)
                for t in range(QT):
                    key = ("suf", t)
                    dve.wait_ge(BANK[key].done, BANK[key].emptied(key, b))
                dve.wait_ge(em_made, b + 1)
                dve.tensor_tensor(sufs.rearrange("p t (h d) -> p (t h) d", d=WIDTH),
                                  sufs.rearrange("p t (h d) -> p (t h) d", d=WIDTH),
                                  em.rearrange("p t h -> p (t h)").unsqueeze(2).broadcast_to([P, QT * HEADS, WIDTH]),
                                  ALU.mult).then_inc(sufs_made, 1)
                pv_out(("pv", GROUPS - 1), GROUPS - 1)

                def attention_out(s):
                    def normed_out(t):
                        key = ("oT", s, t)
                        ps = filled(key)
                        if s == 1:
                            if t == 0:
                                dve.wait_ge(sufs_made, b + 1)
                            else:
                                dve.wait_ge(o_made, b * QT + t)
                            dve.tensor_tensor(heads(num[:, :]), heads(ps[:, :])[:, :, 0:WIDTH], heads(sufs[:, t, :]), ALU.add)\
                                .then_inc(BANK[key].done, 1)
                            dve.wait_ge(BANK[key].done, BANK[key].emptied(key, b))
                            total, made = heads(num[:, :]), o_made
                        else:
                            if t > 0:
                                before = ("oT", s, t - 1)
                                dve.wait_ge(BANK[before].done, BANK[before].emptied(before, b))
                            total, made = heads(ps[:, :]), BANK[key].done
                        link(b, dve.reciprocal(rec[:, :], total[:, :, D]))
                        dve.tensor_tensor(heads(o_all[:, t, :]), total[:, :, 0:D],
                                          rec[:, :].unsqueeze(2).broadcast_to([P, HEADS, D]), ALU.mult).then_inc(made, 1)

                    if s == 1:
                        key = ("ctxT",)
                        ps = filled(key)
                        dve.wait_ge(ctx_high, b + 1)
                        for c in range(HC):
                            ins = dve.tensor_tensor(ctxt[:, 1, c, :, :], ps[:, c * SC:(c + 1) * SC].unsqueeze(1)
                                                    .broadcast_to([P, 2, SC]), ctxt[:, 0, c, :, :].bitcast(F32), ALU.subtract)
                        ins.then_inc(BANK[key].done, 1)
                    normed_out(0)
                    normed_out(1)
                    for k, t in output_steps():
                        key = (k, s, t)
                        ps = filled(key)
                        if k == "o2":
                            dve.wait_ge(o_high, b * 2 * QT + (s - 1) * QT + t + 1)
                            dve.tensor_tensor(ohl[:, t % 2, 1, :, :], ps[:, 0:H].rearrange("p (c n) -> p c n", c=HC),
                                              ohl[:, t % 2, 0, :, :].bitcast(F32), ALU.subtract).then_inc(BANK[key].done, 1)
                            if t + 2 < QT:
                                normed_out(t + 2)
                        else:
                            dve.wait_ge(xb_made, b * 2 * QT + (s - 1) * QT + t + 1)
                            xo = (x1, x2)[s - 1]
                            dve.tensor_tensor(xo[:, t, :], ps[:, 0:H], xo[:, t, :], ALU.add).then_inc(BANK[key].done, 1)
                            if t > 0:
                                before = ("pr", s, t - 1)
                                dve.wait_ge(BANK[before].done, BANK[before].emptied(before, b))
                                statistics(xo, t - 1)
                    dve.wait_ge(BANK[key].done, BANK[key].emptied(key, b))
                    statistics(xo, QT - 1)
                    layernorm(b, b * 3 * QT + (s + 1) * QT)

                attention_out(1)
                normalise(2, x1, 0)
                normalise(2, x1, 1)
                key = ("ctxkv",)
                ps = filled(key)
                dve.tensor_tensor(ckv[:, :], ps[:, :], bs["xkv"], ALU.add).then_inc(BANK[key].done, 1)
                for k, t in CROSS:
                    if k == "x":
                        xt_part(2, t)
                        if t + 2 < QT:
                            normalise(2, x1, t + 2)
                    elif k == "p":
                        key = ("q2", t)
                        ps = filled(key)
                        dve.tensor_tensor(cross_q[t], ps[:, 0:H], bs["xq"], ALU.add).then_inc(BANK[key].done, 1)
                    elif k == "k":
                        key = ("ctxkA",)
                        ps = filled(key)
                        for a in range(2):
                            ins = dve.tensor_copy(kxt[64 * a:64 * a + 64, :, 64 * a:64 * a + 64],
                                                  ps[64 * a:64 * a + 64, :].rearrange("p (q n) -> p q n", q=PAIRS))
                        ins.then_inc(BANK[key].done, 1)
                    elif k == "m":
                        for half in range(2):
                            key = ("mx2", t, half)
                            ps = filled(key)
                            dve.tensor_reduce(qa[:, t, 8 * half:8 * half + 8, 48], ps[:, :].rearrange("p (h n) -> p h n", h=8),
                                              AX.X, ALU.max, negate=True).then_inc(BANK[key].done, 1)
                for g in range(GROUPS):
                    pv_out(("pv2", g), g)
                attention_out(2)
                for t in range(2):
                    normalise(3, x2, t)
                for t in range(QT):
                    xt_part(3, t)
                    if t + 2 < QT:
                        normalise(3, x2, t + 2)
                most, rank, chunk, at_, slot_f = (route[:, n, :] for n in range(5))
                dsc = desc[:, :].unsqueeze(1).broadcast_to([P, QT, EXPERTS])

                def find_experts():
                    key = ("lgT",)
                    ps = filled(key)
                    lg = ps[:, :].rearrange("p (t e) -> p t e", t=QT)[:, :, 0:EXPERTS]
                    link(b, dve.tensor_reduce(score[:, 0, :], lg, AX.X, ALU.max))
                    dve.tensor_tensor(best[:, :, :], lg, score[:, 0, :].unsqueeze(2).broadcast_to([P, QT, EXPERTS]), ALU.is_equal)\
                        .then_inc(BANK[key].done, 1)
                    dve.wait_ge(BANK[key].done, BANK[key].emptied(key, b))
                    link(b, dve.tensor_tensor(best[:, :, :], best[:, :, :], dsc, ALU.mult))
                    link(b, dve.tensor_reduce(most, best[:, :, :], AX.X, ALU.max))
                    dve.tensor_tensor(onehot[:, :, :], dsc, most.unsqueeze(2).broadcast_to([P, QT, EXPERTS]), ALU.is_equal)\
                        .then_inc(oh_made, 1)
                    dve.wait_ge(btanh_made, b + 1)
                    link(b, dve.tensor_scalar(score[:, 2, :], score[:, 1, :], 0.5, 0.5, ALU.mult, ALU.add))
                    link(b, dve.tensor_tensor(nrm[:, 2, :], score[:, 2, :], nrm[:, 1, :], ALU.mult))
                    for t in range(QT):
                        dve.tensor_scalar(row[:, t, 0:H], x2[:, t, :], mv[:, t, 0:1], nrm[:, 2, t:t + 1],
                                          ALU.subtract, ALU.mult).then_inc(row_made, 1)

                def find_ranks():
                    key = ("rank",)
                    ps = filled(key)
                    dve.wait_ge(oh_made, b + 1)
                    link(b, dve.tensor_tensor(ranks[:, :, :], ps[:, 0:QT * EXPERTS].rearrange("p (t e) -> p t e", t=QT),
                                           count[:, :].unsqueeze(1).broadcast_to([P, QT, EXPERTS]), ALU.add))
                    dve.tensor_tensor(count[:, :], count[:, :], ps[:, QT * EXPERTS:(QT + 1) * EXPERTS], ALU.add)\
                        .then_inc(BANK[key].done, 1)
                    link(b, dve.tensor_tensor(ranks[:, :, :], ranks[:, :, :], onehot[:, :, :], ALU.mult))
                    link(b, dve.tensor_reduce(rank, ranks[:, :, :], AX.X, ALU.add))

                def find_slots():
                    link(b, dve.tensor_tensor(reached[:, :, :], rank.unsqueeze(2).broadcast_to([P, QT, OVER]),
                                           steps128[:, :].unsqueeze(1).broadcast_to([P, QT, OVER]), ALU.is_ge))
                    link(b, dve.tensor_reduce(chunk, reached[:, :, :], AX.X, ALU.add))
                    link(b, dve.scalar_tensor_tensor(out=at_, in0=rank, scalar=float(COLUMNS), in1=most, op0=ALU.mult, op1=ALU.subtract))
                    link(b, dve.scalar_tensor_tensor(out=slot_f, in0=chunk, scalar=float(EXPERTS - P * COLUMNS), in1=at_,
                                                  op0=ALU.mult, op1=ALU.add))
                    dve.wait_ge(slots_used, b + 1)
                    link(b, dve.tensor_scalar(slot_i[:, :], slot_f, float(EXPERTS), None, ALU.add))
                    link(b, dve.tensor_scalar(tokens[:, :], tokens[:, :], S, None, ALU.add))
                    dve.sem_inc(slots_made, 1)

                for c in range(IC):
                    key = ("gate", c)
                    ps = filled(key)
                    dve.wait_ge(tanh_made, b * IC + c + 1)
                    if c > 0:
                        dve.wait_ge(BANK["up", c - 1].done, BANK["up", c - 1].emptied(("up", c - 1), b))
                    dve.scalar_tensor_tensor(out=gated[:, :], in0=th[:, c % 2, :], scalar=1.0, in1=ps[:, :],
                                             op0=ALU.add, op1=ALU.mult).then_inc(BANK[key].done, 1)
                    dve.wait_ge(BANK[key].done, BANK[key].emptied(key, b))
                    key = ("up", c)
                    ps = filled(key)
                    if c >= 2:
                        dve.wait_ge(hid_low, b * IC + c - 1)
                    dve.scalar_tensor_tensor(out=hid[:, c % 2, :], in0=gated[:, :], scalar=0.5, in1=ps[:, :],
                                             op0=ALU.mult, op1=ALU.mult).then_inc(BANK[key].done, 1)
                    if c == 0:
                        find_experts()
                    elif c == 1:
                        with dve.If(b < B - 1):
                            begin_statistics(b * 16 + 32)
                    elif c == 2:
                        find_ranks()
                with dve.If(b < B - 1):
                    begin_batch(b, b * 3 * QT + 4 * QT)
                with dve.If(b > B - 2):
                    dve.sem_inc(dve_step, first_steps)
                find_slots()
                for t in range(QT):
                    key = ("dn", t)
                    ps = filled(key)
                    dve.tensor_tensor(row[:, t, H:2 * H], ps[:, 0:H], x2[:, t, :], ALU.add)\
                        .then_inc(BANK[key].done, 1)
            assert step[0] - first_steps == STEPS_PER_BATCH, step[0] - first_steps

            dve.memset(gath[:, :, :], 0.0).then_inc(zeroed, 1)

            base = B * STEPS_PER_BATCH + first_steps
            n2 = [0]

            def link2(ins):
                n2[0] += 1
                ins.then_inc(dve_step, 1)
                dve.wait_ge(dve_step, base + n2[0])

            link2(dve.tensor_tensor(place["e15"], count[:, :].unsqueeze(2).broadcast_to([P, EXPERTS, OVER]),
                                    steps128[:, :].unsqueeze(1).broadcast_to([P, EXPERTS, OVER]), ALU.is_gt))
            link2(dve.tensor_reduce(place["nov"], place["e15"], AX.X, ALU.add))
            link2(dve.tensor_tensor(place["cum"], place["nov"].unsqueeze(1).broadcast_to([P, EXPERTS, EXPERTS]), upto[:, :, :], ALU.mult))
            link2(dve.tensor_reduce(place["end"], place["cum"], AX.X, ALU.add))
            link2(dve.tensor_copy(ctl_i[0:1, 0:1], place["end"][0:1, EXPERTS - 1:EXPERTS]))
            def find_overflow_tiles():
                link2(dve.tensor_tensor(place["o15"][0:1, :, :], place["end"][0:1, :].unsqueeze(1).broadcast_to([1, OVER, EXPERTS]),
                                        ovn[0:1, :].unsqueeze(2).broadcast_to([1, OVER, EXPERTS]), ALU.is_le))
                link2(dve.tensor_reduce(place["oe"][0:1, :], place["o15"][0:1, :, :], AX.X, ALU.add))
                link2(dve.tensor_scalar(ctl_i[0:1, 1:1 + OVER], place["oe"][0:1, :], float(EXPERTS - 1), None, ALU.min))
                link2(dve.tensor_tensor(place["n15"][0:1, :, :], place["o15"][0:1, :, :],
                                        place["nov"][0:1, :].unsqueeze(1).broadcast_to([1, OVER, EXPERTS]), ALU.mult))
                link2(dve.tensor_reduce(place["on"][0:1, :], place["n15"][0:1, :, :], AX.X, ALU.add))
                link2(dve.tensor_tensor(place["on"][0:1, :], ovn[0:1, :], place["on"][0:1, :], ALU.subtract))
                link2(dve.scalar_tensor_tensor(out=place["oc"][0:1, :], in0=place["on"][0:1, :], scalar=float(EXPERTS),
                                               in1=place["oe"][0:1, :], op0=ALU.mult, op1=ALU.add))
                dve.tensor_scalar(ctl_i[0:1, 1 + TILES:1 + TILES + OVER], place["oc"][0:1, :], float(EXPERTS), float(COLUMNS - 1),
                                  ALU.add, ALU.min).then_inc(ctl_made, 1)
                dve.wait_ge(ctl_made, 1)

            def load_x(u, n):
                dve.wait_ge(e_t, n)
                dve.tensor_copy(xe[:, u % 2, :], misc[u % 2].tile[:, 0:H]).then_inc(e_x, 1)

            def gate(u, n):
                dve.wait_ge(e_th, n)
                dve.wait_ge(e_h, n + 1)
                dve.scalar_tensor_tensor(out=ge[:, :], in0=the[:, :], scalar=1.0, in1=gate_bank[u % 2].tile[:, :],
                                         op0=ALU.add, op1=ALU.mult).then_inc(e_gd, 1)
                dve.wait_ge(e_gd, n + 1)
                dve.wait_ge(e_u, n)
                dve.scalar_tensor_tensor(out=he[:, u % 2, :], in0=ge[:, :], scalar=0.5, in1=up_bank[u % 2].tile[:, :],
                                         op0=ALU.mult, op1=ALU.mult).then_inc(e_h, 1)

            def finish(u, n, before):
                dve.wait_ge(e_y, n)
                if before is not None:
                    dve.wait_ge(scattered[u % RING], before)
                dve.tensor_tensor(outr[:, u % RING, :], sexp[u % 2].tile[:, 0:H], gath[:, u, H:2 * H], ALU.add)\
                    .then_inc(e_o, 1)

            def expert_tiles(i, first=False, last=False):
                for u in range(DEPTH):
                    n = i * DEPTH + (u + 1)
                    gate(u, n)
                    if u + 2 < DEPTH or not last:
                        load_x((u + 2) % DEPTH, n + 2)
                    if u > 0 or not first:
                        turns = (u - 1) // RING
                        before = None if first and turns < 1 else i * (16 * DEPTH // RING) + 16 * turns
                        finish((u - 1) % DEPTH, n - 1, before)

            load_x(0, 1)
            load_x(1, 2)
            find_overflow_tiles()
            expert_tiles(0, first=True)
            with dve.Fori(1, EXPERTS // DEPTH - 1) as i:
                expert_tiles(i)
            expert_tiles(EXPERTS // DEPTH - 1, last=True)
            finish(DEPTH - 1, EXPERTS, 16 * (EXPERTS // RING - 1))
            n_over = dve.value_load(ctl_i[0:1, 0:1], min_val=0, max_val=OVER)
            with dve.Fori(0, -(-OVER // 2)) as i:
                with dve.If(i * 2 < n_over):
                    for step_ in (load_x, gate, finish):
                        for k in range(2):
                            with dve.If(i * 2 + 1 < n_over) if k else nullcontext():
                                n = i * 2 + (EXPERTS + 1 + k)
                                if step_ is finish:
                                    finish(k, n, i * 16 + 16 * EXPERTS // RING)
                                else:
                                    step_(k, n)

        @block.tensor
        def _(pe):
            def product(out_ap, left, right, chunks):
                n = 0
                for c in range(chunks):
                    for a, k in ((0, 0), (0, 1), (1, 0)):
                        n += 1
                        ins = pe.matmul(out_ap, left(a, c), right(k, c), start=(n == 1), stop=(n == 3 * chunks))
                return ins

            def has(name):
                if name in GPSIMD_SPLITS:
                    pe.wait_ge(gu_low, GPSIMD_SPLITS.index(name) + 1)
                else:
                    pe.wait_ge(w_low, [n for n in WORDER if n not in GPSIMD_SPLITS].index(name) + 1)

            pe.wait_ge(consts_made, CONSTS - 1)
            pe.wait_ge(vconsts_made, VCONSTS)
            with pe.Fori(0, B) as b:
                def free(key):
                    pe.wait_ge(BANK[key].done, BANK[key].free(key, b))
                    return BANK[key].tile

                def emptied(*keys, then=None):
                    for n, key in enumerate(keys):
                        if all(BANK[k] is not BANK[key] for k in (*keys[n + 1:], *([then] if then else []))):
                            pe.wait_ge(BANK[key].done, BANK[key].emptied(key, b))

                def xT(s, t):
                    key = ("xT", s, t)
                    ps = free(key)
                    pe.wait_ge(normed, b * 3 * QT + (s - 1) * QT + t + 1)
                    for c in range(HC):
                        ins = pe.transpose(ps[:, c * P:(c + 1) * P], xn[:, t % 2, c * P:(c + 1) * P], ident[:, :])
                    ins.then_inc(BANK[key].ready, 1)

                def project(key, t, name, lo, hi):
                    ps = free(key)
                    product(ps[:, 0:hi - lo], lambda a, c: xt[:, a, c, t * P:(t + 1) * P],
                            lambda a, c: w[name][:, a, c, lo:hi], HC).then_inc(BANK[key].ready, 1)

                def keys_T(t):
                    pe.wait_ge(k_low, b * QT + t + 1)
                    for half in range(2):
                        key = ("kA", t, half)
                        ps = free(key)
                        for p in range(4):
                            h = 8 * half + 2 * p
                            ins = pe.transpose(ps[:, p * P:(p + 1) * P],
                                               ka[:, h:h + 2, :].rearrange("p a n -> p (a n)").bitcast(F32), ident[:, :])
                        ins.then_inc(BANK[key].ready, 1)
                    key = ("c", t)
                    ps = free(key)
                    for p in range(4):
                        ins = pe.transpose(ps[:, p * P:(p + 1) * P], self_qk[t % 2][:, p * P:(p + 1) * P], ident[:, :])
                    ins.then_inc(BANK[key].ready, 1)

                def project_qkv(t):
                    emptied(("xT", 1, t), then=("qk", t))
                    if t == 0:
                        has("qkv")
                    project(("qk", t), t, "qkv", 0, 2 * H)
                    project(("v", t), t, "qkv", 2 * H, 3 * H)

                xT(1, 0)
                xT(1, 1)
                project_qkv(0)
                def later_values(t):
                    key = ("suf", t)
                    others = {3: None, 2: vb[:, 3, 0:VROW], 1: vsum[:, 1, :], 0: vsum[:, 0, :]}[t]
                    if t == QT - 1:
                        emptied(("v", 2), ("v", 3), then=key)
                    elif t < 2:
                        pe.wait_ge(vsum_made, b * 2 + 2 - t)
                    ps = free(key)
                    ins = pe.matmul(ps[:, 0:VROW], later[:, :], vb[:, t, 0:VROW], start=True, stop=(others is None))
                    if others is not None:
                        ins = pe.matmul(ps[:, 0:VROW], ones[:, :], others, start=False, stop=True)
                    ins.then_inc(BANK[key].ready, 1)

                def maximum(key):
                    _, g, t, h, per = key
                    n = (t + 1) * P
                    ps = free(key)
                    if g == 0 and h == 0:
                        pe.wait_ge(km0_made, b * QT + t + 1)
                    pe.matmul(ps[:, 0:per * n], qct[:, g // 2, t * P:(t + 1) * P], km[:, h:h + per, 0:n],
                              start=True, stop=False, skip_group_check=True)
                    v = ps[:, 0:per * n].rearrange("p (h n) -> p h n", h=per)[:, :, t * P:(t + 1) * P]
                    pe.matmul(v, ident_b[:, :], later_b[:, :].unsqueeze(1).broadcast_to([P, per, P]),
                              start=False, stop=True, skip_group_check=True).then_inc(BANK[key].ready, 1)

                project_qkv(1)
                xT(1, 2)
                xT(1, 3)
                for t in range(QT):
                    if t == QT - 1:
                        later_values(QT - 1)
                        later_values(QT - 2)
                    keys_T(t)
                    for key in max_jobs(0):
                        if key[2] == t - 1:
                            maximum(key)
                    if t + 2 < QT:
                        project_qkv(t + 2)

                def score(g, j, h):
                    key = ("sc", g, j, h)
                    hh = 4 * g + h
                    a = 64 * (hh % 2)
                    ps = free(key)
                    for kt, col in EXPJOBS[j]:
                        ins = pe.matmul(ps[:, col:col + S - kt * P], kat[a:a + 64, hh // 2, kt * P:(kt + 1) * P],
                                        qat[a:a + 64, hh // 2, kt * P:S], start=True, stop=True)
                    ins.then_inc(BANK[key].ready, 1)

                def weigh(g, n):
                    kt = KTORDER[n]
                    key = ("pv", g)
                    if n == 0:
                        free(key)
                    pe.wait_ge(masked, b * 4 * GROUPS + 4 * g + n + 1)
                    for h in range(4):
                        hh = 4 * g + h
                        col = h * PCOLS + KTCOL[kt]
                        ins = pe.matmul(pv.tile[32 * h:32 * h + 32, kt * P:S], vb[:, kt, hh * WIDTH:hh * WIDTH + 32],
                                        probs[:, col:col + S - kt * P], start=(n == 0), stop=(n == 3),
                                        skip_group_check=True)
                    ins.then_inc(pv_read, 1)

                later_values(1)
                for n, key in enumerate(k for k in max_jobs(0) if k[2] == QT - 1):
                    maximum(key)
                    if n == 1:
                        later_values(0)
                pe.wait_ge(q_low, b * 2 * QT + QT)
                for g in range(GROUPS):
                    pe.wait_ge(shift_put, b * GROUPS + g + 1)
                    for j in range(2):
                        key = ("qA", g, j)
                        ps = free(key)
                        for t in range(QT):
                            h = 4 * g + 2 * j
                            ins = pe.transpose(ps[:, t * P:(t + 1) * P],
                                               qa[:, t, h:h + 2, :].rearrange("p a n -> p (a n)").bitcast(F32), ident[:, :])
                        ins.then_inc(BANK[key].ready, 1)
                    if g > 0:
                        weigh(g - 1, 2)
                        weigh(g - 1, 3)
                    keys = [("kA", QT - 1, half) for half in range(2)] if g == 0 else []
                    emptied(*keys, ("qA", g, 0), ("qA", g, 1), then=("sc", g, 0, 0))
                    ahead = max_jobs(g + 1) if g + 1 < GROUPS else []
                    if ahead:
                        pe.wait_ge(km_made, b * 2 * (GROUPS - 1) + 2 * (g + 1))
                    for n in range(12):
                        score(g, n // 4, n % 4)
                        if n < len(ahead):
                            maximum(ahead[n])
                        if n == 8:
                            weigh(g, 0)
                    weigh(g, 1)
                weigh(GROUPS - 1, 2)
                weigh(GROUPS - 1, 3)

                def attention_out(s, name):
                    name_ = "pv" if s == 1 else "pv2"
                    for groups in (range(GROUPS - 1), (GROUPS - 1,)):
                        emptied(*((name_, g) for g in groups), then=("oT", s, 0) if 0 in groups else None)
                        for t in range(QT):
                            key = ("oT", s, t)
                            ps = free(key) if 0 in groups else BANK[key].tile
                            for g in groups:
                                ins = pe.transpose(ps[:, g * P:(g + 1) * P], ots[:, g, t * P:(t + 1) * P], ident[:, :])
                            if 0 not in groups:
                                ins.then_inc(BANK[key].ready, 1)
                    for k, t in output_steps():
                        key = (k, s, t)
                        if k == "o2":
                            if s == 1:
                                pe.wait_ge(o_made, b * QT + t + 1)
                            else:
                                emptied(("oT", s, t), then=key)
                            ps = free(key)
                            for c in range(HC):
                                ins = pe.transpose(ps[:, c * P:(c + 1) * P], o_all[:, t, c * P:(c + 1) * P], ident[:, :])
                            ins.then_inc(BANK[key].ready, 1)
                        else:
                            emptied(("o2", s, t), then=key)
                            if t == 0:
                                has(name)
                            ps = free(key)
                            product(ps[:, 0:H], lambda a, c: ohl[:, t % 2, a, c, :], lambda a, c: w[name][:, a, c, :], HC)\
                                .then_inc(BANK[key].ready, 1)

                key = ("ctxT",)
                ps = free(key)
                pe.wait_ge(in_ctx, 16 * b + 16)
                pe.sem_inc(passed, 1)
                for c in range(HC):
                    ins = pe.transpose(ps[:, c * SC:(c + 1) * SC], ctxr[:, c * P:(c + 1) * P], ident[0:SC, 0:SC])
                ins.then_inc(BANK[key].ready, 1)
                attention_out(1, "o")
                emptied(("ctxT",), then=("ctxkv",))
                has("xkv")
                key = ("ctxkv",)
                ps = free(key)
                product(ps[:, :], lambda a, c: ctxt[:, a, c, :, :].rearrange("p a n -> p (a n)"),
                        lambda a, c: w["xkv"][:, a, c, :], HC).then_inc(BANK[key].ready, 1)

                def transpose_q(t):
                    emptied(("q2", t), then=("c2", t))
                    key = ("c2", t)
                    ps = free(key)
                    for p in range(2):
                        ins = pe.transpose(ps[:, p * P:(p + 1) * P], cross_q[t][:, p * P:(p + 1) * P], ident[:, :])
                    ins.then_inc(BANK[key].ready, 1)

                def maximum2(t):
                    emptied(("c2", t), then=("mx2", t, 0))
                    if t == 0:
                        pe.wait_ge(kxc_made, b * 2 + 2)
                    for k in range(2):
                        key = ("mx2", t, k)
                        ps = free(key)
                        pe.matmul(ps[:, :], qct[:, k, t * P:(t + 1) * P], kxc[:, k, :, :].rearrange("p h n -> p (h n)"),
                                  start=True, stop=True).then_inc(BANK[key].ready, 1)

                def transpose_qa(t):
                    pe.wait_ge(q_low, b * 2 * QT + QT + t + 1)
                    for half in range(2):
                        emptied(("mx2", t, half), then=("qA2", t, half))
                        key = ("qA2", t, half)
                        ps = free(key)
                        for p in range(4):
                            h = 8 * half + 2 * p
                            ins = pe.transpose(ps[:, p * P:(p + 1) * P],
                                               qa[:, t, h:h + 2, :].rearrange("p a n -> p (a n)").bitcast(F32), ident[:, :])
                        ins.then_inc(BANK[key].ready, 1)

                for k, t in CROSS:
                    if k == "x":
                        xT(2, t)
                    elif k == "p":
                        emptied(("xT", 2, t), then=("q2", t))
                        if t == 0:
                            has("xq")
                        project(("q2", t), t, "xq", 0, H)
                    elif k == "c":
                        transpose_q(t)
                    elif k == "m":
                        maximum2(t)
                    elif k == "a":
                        transpose_qa(t)
                    elif k == "j":
                        emptied(("ctxkv",), then=("ctxkc",))
                        key = ("ctxkc",)
                        ps = free(key)
                        pe.sem_inc(passed, 1)
                        for c in range(2):
                            ins = pe.transpose(ps[:, c * SC:(c + 1) * SC], ckv[0:SC, c * P:(c + 1) * P], ident[0:SC, 0:SC])
                        ins.then_inc(BANK[key].ready, 1)
                    elif k == "k":
                        key = ("ctxkA",)
                        ps = free(key)
                        pe.wait_ge(cka_low, b + 1)
                        pe.sem_inc(passed, 1)
                        for p in range(PAIRS):
                            ins = pe.transpose(ps[:, p * SC:(p + 1) * SC],
                                               cka[:, 2 * p:2 * p + 2, :].rearrange("p a n -> p (a n)").bitcast(F32), ident[0:SC, 0:SC])
                        ins.then_inc(BANK[key].ready, 1)
                emptied(("ctxkA",), *(("qA2", t, half) for t in range(QT) for half in range(2)), then=("sc2", 0))

                def weigh2(p):
                    key = ("pv2", p // 2)
                    if p % 2 == 0:
                        free(key)
                    if p == 0:
                        pe.wait_ge(ctxv_put, b * 2 + 2)
                    emptied(("sc2", p))
                    a = 64 * (p % 2)
                    ins = pe.matmul(BANK[key].tile[a:a + 64, :], vx[:, p, :, :].rearrange("p a n -> p (a n)"),
                                    probs[:, p * S:(p + 1) * S], start=True, stop=True)
                    if p % 2 == 1:
                        ins.then_inc(BANK[key].ready, 1)

                for p in range(PAIRS + 2):
                    if p < PAIRS:
                        key = ("sc2", p)
                        ps = free(key)
                        pe.matmul(ps[:, :], kxt[:, p, :], qat[:, p, :], start=True, stop=True)\
                            .then_inc(BANK[key].ready, 1)
                    if p >= 2:
                        weigh2(p - 2)
                attention_out(2, "xo")

                for t in range(QT):
                    xT(3, t)
                emptied(*(("xT", 3, t) for t in range(QT)), then=("lg",))
                for name in ("gate", "dn"):
                    has(name)
                key = ("lg",)
                ps = free(key)
                product(ps[:, :], lambda a, c: w["gate"][:, a, c, :], lambda a, c: xt[:, a, c, :], HC)\
                    .then_inc(BANK[key].ready, 1)

                def up(c):
                    for key, lo in ((("gate", c), c * P), (("up", c), INNER + c * P)):
                        ps = free(key)
                        product(ps[:, :], lambda a, k: w["gu"][:, a, k, lo:lo + P], lambda a, k: xt[:, a, k, :], HC)\
                            .then_inc(BANK[key].ready, 1)

                up(0)
                emptied(("lg",))
                key = ("lgT",)
                ps = free(key)
                for t in range(QT):
                    ins = pe.transpose(ps[:, t * P:(t + 1) * P], lgs[:, t * P:(t + 1) * P], ident[:, :])
                ins.then_inc(BANK[key].ready, 1)
                up(1)
                up(2)
                key = ("rank",)
                ps = free(key)
                pe.wait_ge(oh_made, b + 1)
                v = ps[:, 0:QT * EXPERTS].rearrange("p (t e) -> p t e", t=QT)
                pe.matmul(v, below_b[:, :], onehot[:, :, :], start=True, stop=False, skip_group_check=True)
                for j in range(QT - 1):
                    pe.matmul(v[:, j + 1:QT, :], ones_b[:, :],
                              onehot[:, j, :].unsqueeze(1).broadcast_to([P, QT - 1 - j, EXPERTS]),
                              start=False, stop=(j == QT - 2), skip_group_check=True)
                for j in range(QT):
                    ins = pe.matmul(ps[:, QT * EXPERTS:(QT + 1) * EXPERTS], ones_b[:, :], onehot[:, j, :], start=(j == 0),
                                    stop=(j == QT - 1), skip_group_check=True)
                ins.then_inc(BANK[key].ready, 1)
                up(3)
                for c in range(IC):
                    pe.wait_ge(hid_low, b * IC + c + 1)
                    for t in range(QT):
                        key = ("dn", t)
                        ps = free(key) if c == 0 else BANK[key].tile
                        for n, (a, k) in enumerate(((0, 0), (0, 1), (1, 0))):
                            ins = pe.matmul(ps[:, 0:H], hhl[:, a, c, t * P:(t + 1) * P], w["dn"][:, k, c, :],
                                            start=(c == 0 and n == 0), stop=(c == IC - 1 and n == 2))
                        if c == IC - 1:
                            ins.then_inc(BANK[key].ready, 1)

            def turn(u, gathers):
                pe.wait_ge(gathered[u], gathers)
                for c in range(HC):
                    ins = pe.transpose(misc[u % 2].tile[:, c * P:(c + 1) * P], gath[:, u, c * P:(c + 1) * P], ident[:, :])
                ins.then_inc(e_t, 1)

            def widen(u, n):
                pe.wait_ge(e_x, n)
                for bank_, base_, s_ in ((gate_bank[u % 2], 0, e_g), (up_bank[u % 2], HC * INNER, e_u)):
                    for c in range(IC):
                        for k in range(HC):
                            at_ = base_ + k * INNER + c * P
                            ins = pe.matmul(bank_.tile[:, c * P:(c + 1) * P], ring[:, u % RING, at_:at_ + P],
                                            xe[:, u % 2, k * P:(k + 1) * P], start=(k == 0), stop=(k == HC - 1))
                    ins.then_inc(s_, 1)

            def narrow(u, n):
                pe.wait_ge(e_h, n + 2)
                for c in range(IC):
                    at_ = 2 * HC * INNER + c * H
                    ins = pe.matmul(sexp[u % 2].tile[:, 0:H], he[:, u % 2, c * P:(c + 1) * P], ring[:, u % RING, at_:at_ + H],
                                    start=(c == 0), stop=(c == IC - 1))
                ins.then_inc(e_y, 1)

            def expert_tiles(i, first=False, last=False):
                for u in range(DEPTH):
                    n = i * DEPTH + (u + 1)
                    pe.wait_ge(e_h, n)
                    pe.wait_ge(in_e[u % RING], i * (16 * DEPTH // RING) + 16 * (u // RING + 1))
                    widen(u, n)
                    if u + 2 < DEPTH or not last:
                        turn((u + 2) % DEPTH, i * 16 + 16 * (1 + (u + 2) // DEPTH))
                    if u > 0 or not first:
                        narrow((u - 1) % DEPTH, n - 1)

            for key in (("dn", t) for t in range(QT)):
                pe.wait_ge(BANK[key].done, BANK[key].emptied(key, B - 1))
            turn(0, 16)
            turn(1, 16)
            expert_tiles(0, first=True)
            with pe.Fori(1, EXPERTS // DEPTH - 1) as i:
                expert_tiles(i)
            expert_tiles(EXPERTS // DEPTH - 1, last=True)
            narrow(DEPTH - 1, EXPERTS)
            pe.wait_ge(ctl_made, 1)
            n_over = pe.value_load(ctl_i[0:1, 0:1], min_val=0, max_val=OVER)
            with pe.Fori(0, -(-OVER // 2)) as i:
                with pe.If(i * 2 < n_over):
                    for k in range(2):
                        with pe.If(i * 2 + 1 < n_over) if k else nullcontext():
                            turn(k, i * 16 + (16 * EXPERTS // DEPTH + 16))
                    for k in range(2):
                        with pe.If(i * 2 + 1 < n_over) if k else nullcontext():
                            pe.wait_ge(in_e[k], i * 16 + (16 * EXPERTS // RING + 16))
                            widen(k, i * 2 + (EXPERTS + 1 + k))
                    for k in range(2):
                        with pe.If(i * 2 + 1 < n_over) if k else nullcontext():
                            narrow(k, i * 2 + (EXPERTS + 1 + k))


def kernel(**inputs):
    import numpy as np
    import concourse.bacc as bacc
    from concourse import mybir as _mybir
    from concourse.bass_utils import run_bass_kernel_spmd

    a = {k: np.asarray(v) for k, v in inputs.items()}
    join = lambda *parts: np.concatenate(parts, axis=-1)
    arrays = {
        "x": a["x"].reshape(B * S, H),
        "ctx": a["ctx_1024"].reshape(B * SC, H),
        "w_qkv": join(a["L0_attn_Wq"].T, a["L0_attn_Wk"].T, a["L0_attn_Wv"].T),
        "w_o": a["L0_attn_Wo"].T,
        "w_xq": a["L0_xattn_Wq"].T,
        "w_xkv": join(a["L0_xattn_Wk"].T, a["L0_xattn_Wv"].T),
        "w_xo": a["L0_xattn_Wo"].T,
        "w_gu": join(a["L0_ffn_shared_gate_w"], a["L0_ffn_shared_up_w"]),
        "w_dn": a["L0_ffn_shared_down_w"],
        "w_gate": join(a["L0_ffn_gate_w"], np.zeros((H, P - EXPERTS), np.float32)),
        "b_qkv": join(a["L0_attn_bq"], a["L0_attn_bk"], a["L0_attn_bv"]),
        "b_o": a["L0_attn_bo"],
        "b_xq": a["L0_xattn_bq"],
        "b_xkv": join(a["L0_xattn_bk"], a["L0_xattn_bv"]),
        "b_xo": a["L0_xattn_bo"],
        "w_experts": join(*(w.reshape(EXPERTS, -1, P, w.shape[-1]).transpose(0, 2, 1, 3).reshape(EXPERTS, P, -1)
                            for w in (a["L0_ffn_routed_gate_w"], a["L0_ffn_routed_up_w"], a["L0_ffn_routed_down_w"]))),
    }
    arrays = {k: np.ascontiguousarray(v) for k, v in arrays.items()}
    nc = bacc.Bacc("TRN2", target_bir_lowering=False, num_devices=1)
    aps = {k: nc.dram_tensor(f"in_{k}", v.shape, _mybir.dt.from_np(v.dtype), kind="ExternalInput").ap()
           for k, v in arrays.items()}
    rows = nc.dram_tensor("rows", (B * S, 2 * H), F32, kind="Internal").ap()
    table = nc.dram_tensor("table", (P, COLUMNS), I32, kind="Internal").ap()
    out = nc.dram_tensor("out", (B * S, H), F32, kind="ExternalOutput").ap()
    build_decoder(nc, aps["x"], aps["ctx"], {k: aps["w_" + k] for k in WCOLS}, {k: aps["b_" + k] for k in BCOLS},
                  aps["w_experts"], rows, table, out)
    r = run_bass_kernel_spmd(nc, [{f"in_{k}": v for k, v in arrays.items()}], core_ids=[0])
    return r.results[0]["out"].reshape(B, S, H)
```
